# Optimizing a Trainium2 kernel written in Bass

```python
import numpy as np
import jax
import jax.numpy as jnp

def _softmax(x, axis=-1):
    return jax.nn.softmax(x, axis=axis)

def _gelu(x):
    return jax.nn.gelu(x, approximate=True)

def _silu(x):
    return jax.nn.silu(x)

def _sigmoid(x):
    return jax.nn.sigmoid(x)

def _layernorm(x, axis=-1, eps=1e-05):
    m = jnp.mean(x, axis=axis, keepdims=True)
    v = jnp.var(x, axis=axis, keepdims=True)
    return (x - m) / jnp.sqrt(v + eps)

def _scatter_add(tgt, idx, src, axis=0):
    return tgt.at[idx].add(src)

def _segment_sum(src, seg, n):
    return jax.ops.segment_sum(src, seg, n)
kernel_name = 'mk_adaln_d2_jaxref_r8_b4b77e'

def setup_inputs(seed: int=0):
    np.random.seed(seed)
    _w = jnp.asarray

    def _L0_attn_setup():
        import jax, jax.numpy as jnp
        import numpy as np
        B, L, E, H = (2, 128, 128, 16)
        D = E // H
        EPS = 1e-06

        def rmsnorm(x, w, eps=1e-06):
            var = jnp.mean(jnp.square(x), axis=-1, keepdims=True)
            return x * jax.lax.rsqrt(var + eps) * w

        def cosformer_attn(x, qkv_w, qkv_b, out_w, out_b):
            b, l, e = x.shape
            qkv = x @ qkv_w + qkv_b
            q, k, v = jnp.split(qkv, 3, axis=-1)
            q = q.reshape(b, l, H, D).transpose(0, 2, 1, 3)
            k = k.reshape(b, l, H, D).transpose(0, 2, 1, 3)
            v = v.reshape(b, l, H, D).transpose(0, 2, 1, 3)
            positions = jnp.arange(l, dtype=jnp.float32).reshape(1, 1, l, 1)
            cos_w = jnp.cos(jnp.pi / 2 * positions / l)
            sin_w = jnp.sin(jnp.pi / 2 * positions / l)
            q_prime = jax.nn.relu(q)
            k_prime = jax.nn.relu(k)
            q_cos, q_sin = (q_prime * cos_w, q_prime * sin_w)
            k_cos, k_sin = (k_prime * cos_w, k_prime * sin_w)
            kv_cos_cumsum = jnp.cumsum(jnp.einsum('bhld,bhle->bhlde', k_cos, v), axis=2)
            context_cos = jnp.einsum('bhld,bhlde->bhle', q_cos, kv_cos_cumsum)
            kv_sin_cumsum = jnp.cumsum(jnp.einsum('bhld,bhle->bhlde', k_sin, v), axis=2)
            context_sin = jnp.einsum('bhld,bhlde->bhle', q_sin, kv_sin_cumsum)
            context = context_cos + context_sin
            k_cos_cumsum = jnp.cumsum(k_cos, axis=2)
            k_sin_cumsum = jnp.cumsum(k_sin, axis=2)
            norm = jnp.einsum('bhld,bhld->bhl', q_cos, k_cos_cumsum) + jnp.einsum('bhld,bhld->bhl', q_sin, k_sin_cumsum)
            output = context / (norm[..., None] + EPS)
            output = output.transpose(0, 2, 1, 3).reshape(b, l, e)
            return output @ out_w + out_b
        key = jax.random.key(seed)
        ks = jax.random.split(key, 6)
        x = jax.random.normal(ks[0], (B, L, E), dtype=jnp.float32)
        qkv_w = jax.random.normal(ks[1], (E, 3 * E), dtype=jnp.float32) / np.sqrt(E)
        qkv_b = jnp.zeros((3 * E,), dtype=jnp.float32)
        out_w = jax.random.normal(ks[2], (E, E), dtype=jnp.float32) / np.sqrt(E)
        out_b = jnp.zeros((E,), dtype=jnp.float32)
        norm1_w = jnp.ones((E,), dtype=jnp.float32)
        norm2_w = jnp.ones((E,), dtype=jnp.float32)
        mlp_w1 = jax.random.normal(ks[3], (E, 4 * E), dtype=jnp.float32) / np.sqrt(E)
        mlp_b1 = jnp.zeros((4 * E,), dtype=jnp.float32)
        mlp_w2 = jax.random.normal(ks[4], (4 * E, E), dtype=jnp.float32) / np.sqrt(4 * E)
        mlp_b2 = jnp.zeros((E,), dtype=jnp.float32)
        return dict(x=x, qkv_w=qkv_w, qkv_b=qkv_b, out_w=out_w, out_b=out_b, norm1_w=norm1_w, norm2_w=norm2_w, mlp_w1=mlp_w1, mlp_b1=mlp_b1, mlp_w2=mlp_w2, mlp_b2=mlp_b2)
    _L0_attn_in = _L0_attn_setup()

    def _L0_ffn_setup():
        import jax, jax.numpy as jnp
        import numpy as np
        D_MODEL = 128
        H_SHARED = 256
        H_ROUTED = 128
        N_EXPERTS = 8
        TOP_K = 2
        key = jax.random.key(seed)
        ks = jax.random.split(key, 8)
        B, T = (2, 256)
        sc_d = 1.0 / np.sqrt(D_MODEL)
        sc_hs = 1.0 / np.sqrt(H_SHARED)
        sc_hr = 1.0 / np.sqrt(H_ROUTED)
        return {'x': jax.random.normal(ks[0], (B, T, D_MODEL), dtype=jnp.float32), 'router_w': jax.random.normal(ks[1], (N_EXPERTS, D_MODEL), dtype=jnp.float32) * sc_d, 'router_bias': jnp.zeros((N_EXPERTS,), dtype=jnp.float32), 'sw1': jax.random.normal(ks[2], (D_MODEL, H_SHARED), dtype=jnp.float32) * sc_d, 'sw3': jax.random.normal(ks[3], (D_MODEL, H_SHARED), dtype=jnp.float32) * sc_d, 'sw2': jax.random.normal(ks[4], (H_SHARED, D_MODEL), dtype=jnp.float32) * sc_hs, 'ew1': jax.random.normal(ks[5], (N_EXPERTS, D_MODEL, H_ROUTED), dtype=jnp.float32) * sc_d, 'ew2': jax.random.normal(ks[6], (N_EXPERTS, H_ROUTED, D_MODEL), dtype=jnp.float32) * sc_hr}
    _L0_ffn_in = _L0_ffn_setup()
    _L0_c = _w((lambda *s: np.random.randn(*s).astype(np.float32) * 0.05)(4, 128))
    _L0_wmod = _w((lambda *s: np.random.randn(*s).astype(np.float32) * 0.05)(128, 6 * 128) * 128 ** (-0.5))

    def _L1_attn_setup():
        import jax, jax.numpy as jnp
        import numpy as np
        N_HEADS = 16

        def _heads(x, h):
            B, T, D = x.shape
            return x.reshape(B, T, h, D // h).transpose(0, 2, 1, 3)

        def _reference_tuple_inner(x, Wq, Wk, Wv, Wo, Wg, bg):
            h = N_HEADS
            q = _heads(x @ Wq.T, h)
            k = _heads(x @ Wk.T, h)
            v = _heads(x @ Wv.T, h)
            g = _heads(jax.nn.sigmoid(x @ Wg.T + bg), h)
            qf = jax.nn.softplus(q) * (g + 1e-06)
            kf = jax.nn.softplus(k)
            kv = kf[..., :, None] * v[..., None, :]
            kv_cum = jnp.cumsum(kv, axis=2)
            z_cum = jnp.cumsum(kf, axis=2)
            num = jnp.einsum('bhtd,bhtde->bhte', qf, kv_cum)
            den = jnp.einsum('bhtd,bhtd->bht', qf, z_cum) + 1e-06
            out = num / den[..., None]
            B, _, T, dh = out.shape
            out = out.transpose(0, 2, 1, 3).reshape(B, T, h * dh)
            out = out @ Wo.T
            return (out, kv_cum[:, :, -1], z_cum[:, :, -1])
        key = jax.random.key(seed)
        B, T, D = (1, 256, 128)
        ks = jax.random.split(key, 7)
        s = 0.02
        return {'x': jax.random.normal(ks[0], (B, T, D), jnp.float32), 'Wq': jax.random.normal(ks[1], (D, D), jnp.float32) * s, 'Wk': jax.random.normal(ks[2], (D, D), jnp.float32) * s, 'Wv': jax.random.normal(ks[3], (D, D), jnp.float32) * s, 'Wo': jax.random.normal(ks[4], (D, D), jnp.float32) * s, 'Wg': jax.random.normal(ks[5], (D, D), jnp.float32) * s, 'bg': jax.random.normal(ks[6], (D,), jnp.float32) * s}
    _L1_attn_in = _L1_attn_setup()

    def _L1_ffn_setup():
        import jax, jax.numpy as jnp
        import numpy as np
        DIM = 128
        DEPTH = 6
        HEADS = 16
        DIM_HEAD = 64
        WINDOW = 32
        INNER = HEADS * DIM_HEAD
        DIM_INNER = int(DIM * 4 * 2 / 3)
        QK_SCALE = 8.0

        def shift_tokens(t):
            a, s = jnp.split(t, 2, -1)
            s = jnp.pad(s, ((0, 0), (1, 0), (0, 0)))[:, :-1]
            return jnp.concatenate([a, s], -1)

        def l2norm(t):
            return t / jnp.maximum(jnp.linalg.norm(t, axis=-1, keepdims=True), 1e-12)

        def rotate_half(x):
            x1, x2 = jnp.split(x, 2, -1)
            return jnp.concatenate([-x2, x1], -1)

        def rotary_tables(n):
            half = jnp.arange(0, DIM_HEAD, 2, dtype=jnp.float32)
            inv_freq = 1.0 / 10000.0 ** (half / DIM_HEAD)
            t = jnp.arange(n, dtype=jnp.float32)
            freqs = t[:, None] * inv_freq[None, :]
            freqs = jnp.concatenate([freqs, freqs], -1)
            base_scale = (half + 0.4 * DIM_HEAD) / (1.4 * DIM_HEAD)
            power = (t - n // 2) / (WINDOW // 2)
            scale = base_scale[None, :] ** power[:, None]
            scale = jnp.concatenate([scale, scale], -1)
            return (freqs, scale)

        def local_attention(q, k, v):
            b, h, n, d = q.shape
            w = WINDOW
            nw = n // w
            bq = q.reshape(b, h, nw, w, d)
            bk = k.reshape(b, h, nw, w, d)
            bv = v.reshape(b, h, nw, w, d)

            def look(t):
                p = jnp.pad(t, ((0, 0), (0, 0), (1, 0), (0, 0), (0, 0)))
                return jnp.concatenate([p[:, :, :nw], p[:, :, 1:]], axis=3)
            bk2, bv2 = (look(bk), look(bv))
            seq = jnp.arange(n).reshape(nw, w)
            seq_p = jnp.pad(seq, ((1, 0), (0, 0)), constant_values=-1)
            jt = jnp.concatenate([seq_p[:nw], seq_p[1:]], axis=1)
            it = seq[:, :, None]
            jb = jt[:, None, :]
            mask = (it < jb) | (it > jb + w) | (jb == -1)
            sim = jnp.einsum('bhwie,bhwje->bhwij', bq, bk2) * QK_SCALE
            sim = jnp.where(mask, -jnp.finfo(sim.dtype).max, sim)
            attn = jax.nn.softmax(sim, -1)
            out = jnp.einsum('bhwij,bhwje->bhwie', attn, bv2)
            return out.reshape(b, h, n, d)

        def attn_layer(x, Wqkv, qs, ksc, Wo):
            b, n, _ = x.shape
            qkv = x @ Wqkv
            q, k, v = jnp.split(qkv, 3, -1)
            sh = lambda t: t.reshape(b, n, HEADS, DIM_HEAD).transpose(0, 2, 1, 3)
            q, k, v = (sh(q), sh(k), sh(v))
            q = l2norm(q) * qs
            k = l2norm(k) * ksc
            freqs, scale = rotary_tables(n)
            cos, sin = (jnp.cos(freqs), jnp.sin(freqs))
            q = q * cos * scale + rotate_half(q) * sin * scale
            inv = 1.0 / scale
            k = k * cos * inv + rotate_half(k) * sin * inv
            out = local_attention(q, k, v)
            out = out.transpose(0, 2, 1, 3).reshape(b, n, INNER)
            return out @ Wo

        def ffn_layer(x, g, bln, W1, b1, W2, b2):
            mu = x.mean(-1, keepdims=True)
            var = ((x - mu) ** 2).mean(-1, keepdims=True)
            xn = (x - mu) / jnp.sqrt(var + 1e-05) * g + bln
            hg = xn @ W1 + b1
            a, gate = jnp.split(hg, 2, -1)
            return a * jax.nn.gelu(gate, approximate=False) @ W2 + b2
        key = jax.random.key(seed)
        ks = jax.random.split(key, 8)
        B, N = (2, 256)
        init = lambda k, shape: jax.random.normal(k, shape, jnp.float32) * 0.02
        return {'x': jax.random.normal(ks[0], (B, N, DIM), jnp.float32), 'Wqkv': init(ks[1], (DEPTH, DIM, 3 * INNER)), 'q_scale': jnp.ones((DEPTH, DIM_HEAD), jnp.float32), 'k_scale': jnp.ones((DEPTH, DIM_HEAD), jnp.float32), 'Wo': init(ks[2], (DEPTH, INNER, DIM)), 'ln_g': jnp.ones((DEPTH, DIM), jnp.float32), 'ln_b': jnp.zeros((DEPTH, DIM), jnp.float32), 'W1': init(ks[3], (DEPTH, DIM, 2 * DIM_INNER)), 'b1': jnp.zeros((DEPTH, 2 * DIM_INNER), jnp.float32), 'W2': init(ks[4], (DEPTH, DIM_INNER, DIM)), 'b2': jnp.zeros((DEPTH, DIM), jnp.float32)}
    _L1_ffn_in = _L1_ffn_setup()
    _L1_c = _w((lambda *s: np.random.randn(*s).astype(np.float32) * 0.05)(4, 128))
    _L1_wmod = _w((lambda *s: np.random.randn(*s).astype(np.float32) * 0.05)(128, 6 * 128) * 128 ** (-0.5))
    _d = {'L0_attn_x': _L0_attn_in['x'], 'L0_attn_qkv_w': _L0_attn_in['qkv_w'], 'L0_attn_qkv_b': _L0_attn_in['qkv_b'], 'L0_attn_out_w': _L0_attn_in['out_w'], 'L0_attn_out_b': _L0_attn_in['out_b'], 'L0_attn_norm1_w': _L0_attn_in['norm1_w'], 'L0_attn_norm2_w': _L0_attn_in['norm2_w'], 'L0_attn_mlp_w1': _L0_attn_in['mlp_w1'], 'L0_attn_mlp_b1': _L0_attn_in['mlp_b1'], 'L0_attn_mlp_w2': _L0_attn_in['mlp_w2'], 'L0_attn_mlp_b2': _L0_attn_in['mlp_b2'], 'L0_ffn_router_w': _L0_ffn_in['router_w'], 'L0_ffn_router_bias': _L0_ffn_in['router_bias'], 'L0_ffn_sw1': _L0_ffn_in['sw1'], 'L0_ffn_sw3': _L0_ffn_in['sw3'], 'L0_ffn_sw2': _L0_ffn_in['sw2'], 'L0_ffn_ew1': _L0_ffn_in['ew1'], 'L0_ffn_ew2': _L0_ffn_in['ew2'], 'L0_c': _L0_c, 'L0_wmod': _L0_wmod, 'L1_attn_Wq': _L1_attn_in['Wq'], 'L1_attn_Wk': _L1_attn_in['Wk'], 'L1_attn_Wv': _L1_attn_in['Wv'], 'L1_attn_Wo': _L1_attn_in['Wo'], 'L1_attn_Wg': _L1_attn_in['Wg'], 'L1_attn_bg': _L1_attn_in['bg'], 'L1_ffn_Wqkv': _L1_ffn_in['Wqkv'], 'L1_ffn_q_scale': _L1_ffn_in['q_scale'], 'L1_ffn_k_scale': _L1_ffn_in['k_scale'], 'L1_ffn_Wo': _L1_ffn_in['Wo'], 'L1_ffn_ln_g': _L1_ffn_in['ln_g'], 'L1_ffn_ln_b': _L1_ffn_in['ln_b'], 'L1_ffn_W1': _L1_ffn_in['W1'], 'L1_ffn_b1': _L1_ffn_in['b1'], 'L1_ffn_W2': _L1_ffn_in['W2'], 'L1_ffn_b2': _L1_ffn_in['b2'], 'L1_c': _L1_c, 'L1_wmod': _L1_wmod}
    _x0 = _d['L0_attn_x']
    _d['L0_attn_x'] = jax.random.normal(jax.random.fold_in(jax.random.key(seed), 1), (4, 1024, 128), dtype=_x0.dtype)
    del _x0
    return _d

def reference(L0_attn_x, L0_attn_qkv_w, L0_attn_qkv_b, L0_attn_out_w, L0_attn_out_b, L0_attn_norm1_w, L0_attn_norm2_w, L0_attn_mlp_w1, L0_attn_mlp_b1, L0_attn_mlp_w2, L0_attn_mlp_b2, L0_ffn_router_w, L0_ffn_router_bias, L0_ffn_sw1, L0_ffn_sw3, L0_ffn_sw2, L0_ffn_ew1, L0_ffn_ew2, L0_c, L0_wmod, L1_attn_Wq, L1_attn_Wk, L1_attn_Wv, L1_attn_Wo, L1_attn_Wg, L1_attn_bg, L1_ffn_Wqkv, L1_ffn_q_scale, L1_ffn_k_scale, L1_ffn_Wo, L1_ffn_ln_g, L1_ffn_ln_b, L1_ffn_W1, L1_ffn_b1, L1_ffn_W2, L1_ffn_b2, L1_c, L1_wmod):

    def _L0_attn_ref(x, qkv_w, qkv_b, out_w, out_b, norm1_w, norm2_w, mlp_w1, mlp_b1, mlp_w2, mlp_b2):
        import jax, jax.numpy as jnp
        import numpy as np
        B, L, E, H = (2, 128, 128, 16)
        D = E // H
        EPS = 1e-06

        def rmsnorm(x, w, eps=1e-06):
            var = jnp.mean(jnp.square(x), axis=-1, keepdims=True)
            return x * jax.lax.rsqrt(var + eps) * w

        def cosformer_attn(x, qkv_w, qkv_b, out_w, out_b):
            b, l, e = x.shape
            qkv = x @ qkv_w + qkv_b
            q, k, v = jnp.split(qkv, 3, axis=-1)
            q = q.reshape(b, l, H, D).transpose(0, 2, 1, 3)
            k = k.reshape(b, l, H, D).transpose(0, 2, 1, 3)
            v = v.reshape(b, l, H, D).transpose(0, 2, 1, 3)
            positions = jnp.arange(l, dtype=jnp.float32).reshape(1, 1, l, 1)
            cos_w = jnp.cos(jnp.pi / 2 * positions / l)
            sin_w = jnp.sin(jnp.pi / 2 * positions / l)
            q_prime = jax.nn.relu(q)
            k_prime = jax.nn.relu(k)
            q_cos, q_sin = (q_prime * cos_w, q_prime * sin_w)
            k_cos, k_sin = (k_prime * cos_w, k_prime * sin_w)
            kv_cos_cumsum = jnp.cumsum(jnp.einsum('bhld,bhle->bhlde', k_cos, v), axis=2)
            context_cos = jnp.einsum('bhld,bhlde->bhle', q_cos, kv_cos_cumsum)
            kv_sin_cumsum = jnp.cumsum(jnp.einsum('bhld,bhle->bhlde', k_sin, v), axis=2)
            context_sin = jnp.einsum('bhld,bhlde->bhle', q_sin, kv_sin_cumsum)
            context = context_cos + context_sin
            k_cos_cumsum = jnp.cumsum(k_cos, axis=2)
            k_sin_cumsum = jnp.cumsum(k_sin, axis=2)
            norm = jnp.einsum('bhld,bhld->bhl', q_cos, k_cos_cumsum) + jnp.einsum('bhld,bhld->bhl', q_sin, k_sin_cumsum)
            output = context / (norm[..., None] + EPS)
            output = output.transpose(0, 2, 1, 3).reshape(b, l, e)
            return output @ out_w + out_b
        h = x + cosformer_attn(rmsnorm(x, norm1_w), qkv_w, qkv_b, out_w, out_b)
        m = rmsnorm(h, norm2_w)
        m = jax.nn.gelu(m @ mlp_w1 + mlp_b1) @ mlp_w2 + mlp_b2
        return h + m

    def _L0_ffn_ref(x, router_w, router_bias, sw1, sw3, sw2, ew1, ew2):
        import jax, jax.numpy as jnp
        import numpy as np
        D_MODEL = 128
        H_SHARED = 256
        H_ROUTED = 128
        N_EXPERTS = 8
        TOP_K = 2
        B, T, C = x.shape
        xf = x.reshape(-1, C)
        shared_out = jax.nn.silu(xf @ sw1) * (xf @ sw3) @ sw2
        s = jax.nn.sigmoid((xf @ router_w.T).astype(jnp.float32))
        sel_scores = s + router_bias.astype(jnp.float32)
        _, topk_idx = jax.lax.top_k(sel_scores, TOP_K)
        s_sel = jnp.take_along_axis(s, topk_idx, axis=1)
        denom = s_sel.sum(axis=1, keepdims=True)
        gates = jnp.where(denom > 1e-09, s_sel / (denom + 1e-09), 1.0 / TOP_K).astype(x.dtype)
        one_hot = jax.nn.one_hot(topk_idx, N_EXPERTS, dtype=x.dtype)
        comb = jnp.einsum('nke,nk->ne', one_hot, gates)
        h = jax.nn.gelu(jnp.einsum('nd,edh->neh', xf, ew1), approximate=False)
        y = jnp.einsum('neh,ehd->ned', h, ew2)
        routed_out = jnp.einsum('ned,ne->nd', y, comb)
        return (shared_out + routed_out).reshape(B, T, C)

    def _L1_attn_ref(x, Wq, Wk, Wv, Wo, Wg, bg):
        import jax, jax.numpy as jnp
        import numpy as np
        N_HEADS = 16

        def _heads(x, h):
            B, T, D = x.shape
            return x.reshape(B, T, h, D // h).transpose(0, 2, 1, 3)

        def _reference_tuple_inner(x, Wq, Wk, Wv, Wo, Wg, bg):
            h = N_HEADS
            q = _heads(x @ Wq.T, h)
            k = _heads(x @ Wk.T, h)
            v = _heads(x @ Wv.T, h)
            g = _heads(jax.nn.sigmoid(x @ Wg.T + bg), h)
            qf = jax.nn.softplus(q) * (g + 1e-06)
            kf = jax.nn.softplus(k)
            kv = kf[..., :, None] * v[..., None, :]
            kv_cum = jnp.cumsum(kv, axis=2)
            z_cum = jnp.cumsum(kf, axis=2)
            num = jnp.einsum('bhtd,bhtde->bhte', qf, kv_cum)
            den = jnp.einsum('bhtd,bhtd->bht', qf, z_cum) + 1e-06
            out = num / den[..., None]
            B, _, T, dh = out.shape
            out = out.transpose(0, 2, 1, 3).reshape(B, T, h * dh)
            out = out @ Wo.T
            return (out, kv_cum[:, :, -1], z_cum[:, :, -1])
        return _reference_tuple_inner(x, Wq, Wk, Wv, Wo, Wg, bg)[0]

    def _L1_ffn_ref(x, Wqkv, q_scale, k_scale, Wo, ln_g, ln_b, W1, b1, W2, b2):
        import jax, jax.numpy as jnp
        import numpy as np
        DIM = 128
        DEPTH = 6
        HEADS = 16
        DIM_HEAD = 64
        WINDOW = 32
        INNER = HEADS * DIM_HEAD
        DIM_INNER = int(DIM * 4 * 2 / 3)
        QK_SCALE = 8.0

        def shift_tokens(t):
            a, s = jnp.split(t, 2, -1)
            s = jnp.pad(s, ((0, 0), (1, 0), (0, 0)))[:, :-1]
            return jnp.concatenate([a, s], -1)

        def l2norm(t):
            return t / jnp.maximum(jnp.linalg.norm(t, axis=-1, keepdims=True), 1e-12)

        def rotate_half(x):
            x1, x2 = jnp.split(x, 2, -1)
            return jnp.concatenate([-x2, x1], -1)

        def rotary_tables(n):
            half = jnp.arange(0, DIM_HEAD, 2, dtype=jnp.float32)
            inv_freq = 1.0 / 10000.0 ** (half / DIM_HEAD)
            t = jnp.arange(n, dtype=jnp.float32)
            freqs = t[:, None] * inv_freq[None, :]
            freqs = jnp.concatenate([freqs, freqs], -1)
            base_scale = (half + 0.4 * DIM_HEAD) / (1.4 * DIM_HEAD)
            power = (t - n // 2) / (WINDOW // 2)
            scale = base_scale[None, :] ** power[:, None]
            scale = jnp.concatenate([scale, scale], -1)
            return (freqs, scale)

        def local_attention(q, k, v):
            b, h, n, d = q.shape
            w = WINDOW
            nw = n // w
            bq = q.reshape(b, h, nw, w, d)
            bk = k.reshape(b, h, nw, w, d)
            bv = v.reshape(b, h, nw, w, d)

            def look(t):
                p = jnp.pad(t, ((0, 0), (0, 0), (1, 0), (0, 0), (0, 0)))
                return jnp.concatenate([p[:, :, :nw], p[:, :, 1:]], axis=3)
            bk2, bv2 = (look(bk), look(bv))
            seq = jnp.arange(n).reshape(nw, w)
            seq_p = jnp.pad(seq, ((1, 0), (0, 0)), constant_values=-1)
            jt = jnp.concatenate([seq_p[:nw], seq_p[1:]], axis=1)
            it = seq[:, :, None]
            jb = jt[:, None, :]
            mask = (it < jb) | (it > jb + w) | (jb == -1)
            sim = jnp.einsum('bhwie,bhwje->bhwij', bq, bk2) * QK_SCALE
            sim = jnp.where(mask, -jnp.finfo(sim.dtype).max, sim)
            attn = jax.nn.softmax(sim, -1)
            out = jnp.einsum('bhwij,bhwje->bhwie', attn, bv2)
            return out.reshape(b, h, n, d)

        def attn_layer(x, Wqkv, qs, ksc, Wo):
            b, n, _ = x.shape
            qkv = x @ Wqkv
            q, k, v = jnp.split(qkv, 3, -1)
            sh = lambda t: t.reshape(b, n, HEADS, DIM_HEAD).transpose(0, 2, 1, 3)
            q, k, v = (sh(q), sh(k), sh(v))
            q = l2norm(q) * qs
            k = l2norm(k) * ksc
            freqs, scale = rotary_tables(n)
            cos, sin = (jnp.cos(freqs), jnp.sin(freqs))
            q = q * cos * scale + rotate_half(q) * sin * scale
            inv = 1.0 / scale
            k = k * cos * inv + rotate_half(k) * sin * inv
            out = local_attention(q, k, v)
            out = out.transpose(0, 2, 1, 3).reshape(b, n, INNER)
            return out @ Wo

        def ffn_layer(x, g, bln, W1, b1, W2, b2):
            mu = x.mean(-1, keepdims=True)
            var = ((x - mu) ** 2).mean(-1, keepdims=True)
            xn = (x - mu) / jnp.sqrt(var + 1e-05) * g + bln
            hg = xn @ W1 + b1
            a, gate = jnp.split(hg, 2, -1)
            return a * jax.nn.gelu(gate, approximate=False) @ W2 + b2
        for i in range(DEPTH):
            x = attn_layer(shift_tokens(x), Wqkv[i], q_scale[i], k_scale[i], Wo[i]) + x
            x = ffn_layer(shift_tokens(x), ln_g[i], ln_b[i], W1[i], b1[i], W2[i], b2[i]) + x
        return x
    x = L0_attn_x
    mod = (_silu(L0_c) @ L0_wmod).reshape(L0_c.shape[0], 6, 1, -1)
    sa, ca, ga, sb, cb, gb = (mod[:, 0], mod[:, 1], mod[:, 2], mod[:, 3], mod[:, 4], mod[:, 5])
    ga = (2 * (ga >= 0) - 1) * jnp.maximum(jnp.abs(ga), 0.25)
    gb = (2 * (gb >= 0) - 1) * jnp.maximum(jnp.abs(gb), 0.25)
    h = _layernorm(x, axis=-1) * (1 + ca) + sa
    x = x + ga * _L0_attn_ref(h, L0_attn_qkv_w, L0_attn_qkv_b, L0_attn_out_w, L0_attn_out_b, L0_attn_norm1_w, L0_attn_norm2_w, L0_attn_mlp_w1, L0_attn_mlp_b1, L0_attn_mlp_w2, L0_attn_mlp_b2)
    h = _layernorm(x, axis=-1) * (1 + cb) + sb
    x = x + gb * _L0_ffn_ref(h, L0_ffn_router_w, L0_ffn_router_bias, L0_ffn_sw1, L0_ffn_sw3, L0_ffn_sw2, L0_ffn_ew1, L0_ffn_ew2)
    mod = (_silu(L1_c) @ L1_wmod).reshape(L1_c.shape[0], 6, 1, -1)
    sa, ca, ga, sb, cb, gb = (mod[:, 0], mod[:, 1], mod[:, 2], mod[:, 3], mod[:, 4], mod[:, 5])
    ga = (2 * (ga >= 0) - 1) * jnp.maximum(jnp.abs(ga), 0.25)
    gb = (2 * (gb >= 0) - 1) * jnp.maximum(jnp.abs(gb), 0.25)
    h = _layernorm(x, axis=-1) * (1 + ca) + sa
    x = x + ga * _L1_attn_ref(h, L1_attn_Wq, L1_attn_Wk, L1_attn_Wv, L1_attn_Wo, L1_attn_Wg, L1_attn_bg)
    h = _layernorm(x, axis=-1) * (1 + cb) + sb
    x = x + gb * _L1_ffn_ref(h, L1_ffn_Wqkv, L1_ffn_q_scale, L1_ffn_k_scale, L1_ffn_Wo, L1_ffn_ln_g, L1_ffn_ln_b, L1_ffn_W1, L1_ffn_b1, L1_ffn_W2, L1_ffn_b2)
    return x

_drawn_inputs = setup_inputs


def setup_inputs(seed=0):
    import zlib

    import numpy as np

    out = dict(_drawn_inputs(seed))
    spreads = {'L0_attn_qkv_b': (0.0, 0.1),
     'L0_attn_out_b': (0.0, 0.1),
     'L0_attn_norm1_w': (1.0, 0.6),
     'L0_attn_norm2_w': (1.0, 0.2),
     'L0_attn_mlp_b1': (0.0, 0.361),
     'L0_attn_mlp_b2': (0.0, 0.1),
     'L0_ffn_router_bias': (0.0, 0.1),
     'L1_ffn_q_scale': (1.0, 0.6),
     'L1_ffn_k_scale': (1.0, 0.6),
     'L1_ffn_ln_g': (1.0, 0.6),
     'L1_ffn_ln_b': (0.0, 0.8),
     'L1_ffn_b1': (0.0, 0.8),
     'L1_ffn_b2': (0.0, 0.651)}
    factors = {'L1_attn_Wq': 8.0,
     'L1_attn_Wk': 8.0,
     'L1_attn_Wv': 8.0,
     'L1_attn_Wo': 8.0,
     'L1_attn_Wg': 8.0,
     'L1_attn_bg': 64.0,
     'L1_ffn_W1': 7.832,
     'L1_ffn_W2': 7.682}
    for name, (base, spread) in spreads.items():
        noise = np.random.default_rng([zlib.crc32(name.encode()), seed]).standard_normal(out[name].shape)
        drawn = base * np.exp(spread * noise) if base else spread * noise
        out[name] = jnp.asarray(drawn.astype(out[name].dtype))
    for name, factor in factors.items():
        out[name] = (out[name] * factor).astype(out[name].dtype)
    return out
```

```python
from contextlib import ExitStack

import concourse.bass as bass
from concourse import mybir

F32 = mybir.dt.float32
BF16 = mybir.dt.bfloat16
ALU = mybir.AluOpType
ACT = mybir.ActivationFunctionType
AX = mybir.AxisListType
ds = bass.ds

P = 128
B, L, C = 4, 1024, 128
N = B * L
TPB = L // P
NT = N // P
GW = 512
NG = N // GW
GPB = L // GW
HEADS = 16
HD = C // HEADS
VW = 32
F_MLP = 4 * C // P
EXPERTS = 8
SHARED = 256 // P
DEPTH = 6
DH = 64
INNER = HEADS * DH
PAIRS = HEADS // 2
WIN = 32
NWIN = P // WIN
KEYS = 2 * WIN
HALO = WIN
DIN = int(C * 4 * 2 / 3)
CH = [(0, 128), (128, 128), (256, DIN - 256)]
XSW = HALO + L + 4
QK_SCALE = 8.0
NEG = -3.0e38
LOG_EXP = "natural_log_exp_and_others"
VB_W = 2 * DH + 2


def build(nc, a, out):
    ctx = ExitStack()
    with ctx:
        def sb(name, shape, dt=F32, scope=ctx):
            return scope.enter_context(nc.sbuf_tensor(name, shape, dt))

        primed = []

        def sem(name):
            return ctx.enter_context(nc.semaphore(name))

        def step(name):
            primed.append(sem(name))
            return primed[-1]

        X = sb("X", [P, N])
        H = sb("H", [P, N])
        XSA = sb("XSA", [P, B * XSW])
        XSF = sb("XSF", [P, B * XSW])
        Wqkv = sb("Wqkv", [P, 3 * INNER])
        Wo6 = sb("Wo6", [P, PAIRS, C])
        W1 = sb("W1", [P, 2 * DIN])
        W2 = sb("W2", [P, 3, C])
        lncol = sb("lncol", [P, 2])
        b1col = sb("b1col", [P, 6])
        qks = sb("qks", [P, 2, DH])
        b2col = sb("b2col", [P, 1])
        ident = sb("ident", [P, P])
        onesm = sb("onesm", [P, P])
        mod = sb("mod", [P, 2, 6, B])
        xc = sb("xc", [P, GW])
        sq = sb("sq", [P, GW])
        ve = sb("ve", [P, GW])
        rs = sb("rs", [P, GW])
        xn = sb("xn", [P, GW])

        early = ExitStack()
        wq0 = sb("wq0", [P, 3 * C], scope=early)
        bqk0 = sb("bqk0", [P, 2], scope=early)
        bkv0 = sb("bkv0", [P, 2 * C], scope=early)
        wo0 = sb("wo0", [P, C], scope=early)
        cols0 = sb("cols0", [P, 4 + F_MLP], scope=early)
        mw1 = sb("mw1", [P, 4 * C], scope=early)
        mw2 = sb("mw2", [P, F_MLP, C], scope=early)
        wr = sb("wr", [P, EXPERTS], scope=early)
        rbias = sb("rbias", [P, EXPERTS], scope=early)
        sw1 = sb("sw1", [P, SHARED * P], scope=early)
        sw3 = sb("sw3", [P, SHARED * P], scope=early)
        sw2 = sb("sw2", [P, SHARED, C], scope=early)
        ew1 = sb("ew1", [P, EXPERTS, P], scope=early)
        ew2 = sb("ew2", [P, EXPERTS, P], scope=early)
        wl1 = sb("wl1", [P, 5, C], scope=early)
        bg1 = sb("bg1", [P, 1], scope=early)
        cT = sb("cT", [P, 2, B], scope=early)
        scT = sb("scT", [P, 2, B], scope=early)
        wmod = sb("wmod", [P, 2, 6 * C], scope=early)
        gtmp = sb("gtmp", [P, 4, B], scope=early)
        gsign = sb("gsign", [P, 4, B], scope=early)
        gabs = sb("gabs", [P, 4, B], scope=early)
        hmask = sb("hmask", [P, HEADS], scope=early)
        cmask = sb("cmask", [P, 2, P], scope=early)
        crow = sb("crow", [P, 2, L], scope=early)
        ccol = sb("ccol", [P, 2, TPB], scope=early)
        hold = sb("hold", [P, TPB], scope=early)
        hm9 = sb("hm9", [P, 2 * HEADS, HD + 1], scope=early)
        esel = sb("esel", [P, EXPERTS, P], scope=early)
        low = sb("low", [P, EXPERTS, EXPERTS], scope=early)
        attn = ExitStack()
        ht = sb("ht", [P, P], scope=attn)
        qf = sb("qf", [P, P], scope=attn)
        kf = sb("kf", [P, P], scope=attn)
        qcs = sb("qcs", [P, 2, P], scope=attn)
        Qbd = sb("Qbd", [P, HEADS, P], scope=attn)
        Pm = sb("Pm", [P, HEADS, P], scope=attn)
        ktok = sb("ktok", [P, 2, P], scope=attn)
        vaug = sb("vaug", [P, HEADS, VW], scope=attn)
        state = sb("state", [P, 2, HEADS, VW], scope=attn)
        stnew = sb("stnew", [P, 2, HEADS, HD + 1], scope=attn)
        oT = sb("oT", [P, 4, P], scope=attn)
        nrm = sb("nrm", [P, HEADS], scope=attn)
        rec = sb("rec", [P, HEADS], scope=attn)
        ctxt = sb("ctxt", [P, P], scope=attn)
        spa = sb("spa", [P, 3, P], scope=attn)
        spe = sb("spe", [P, 3, P], scope=attn)
        spl = sb("spl", [P, 3, P], scope=attn)
        qsp = sb("qsp", [P, P], scope=attn)
        attn.close()
        dense = ExitStack()
        hin = sb("hin", [P, 2, GW], scope=dense)
        hidm = sb("hidm", [P, F_MLP, GW], scope=dense)
        hid = sb("hid", [P, 2, GW], scope=dense)
        hid2 = sb("hid2", [P, 2, GW], scope=dense)
        sg = sb("sg", [P, 4, EXPERTS], scope=dense)
        sel = sb("sel", [P, 4, EXPERTS], scope=dense)
        above = sb("above", [P, 4, EXPERTS, EXPERTS], scope=dense)
        level = sb("level", [P, 4, EXPERTS, EXPERTS], scope=dense)
        rank = sb("rank", [P, 4, EXPERTS], scope=dense)
        ssel = sb("ssel", [P, 4, EXPERTS], scope=dense)
        den = sb("den", [P, 5, 4], scope=dense)
        comb = sb("comb", [P, 4, EXPERTS], scope=dense)
        selm = sb("selm", [P, 4, EXPERTS], scope=dense)
        gsel = sb("gsel", [P, 4, EXPERTS], scope=dense)
        gelse = sb("gelse", [P, 4, EXPERTS], scope=dense)
        sgT = sb("sgT", [EXPERTS, GW], scope=dense)
        combT = sb("combT", [P, GW], scope=dense)
        dense.close()
        early.close()

        late = ExitStack()
        rope = sb("rope", [P, 2, TPB, 2 * DH], scope=late)
        ropel = sb("ropel", [P, 2, TPB, 2 * DH], scope=late)
        wmask = sb("wmask", [P, 2, GW], BF16, scope=late)
        identh = sb("identh", [P, P], BF16, scope=late)
        kbd = sb("kbd", [P, PAIRS, 2, HALO + P], scope=late)
        Vbd = sb("Vbd", [P, NWIN, PAIRS, VB_W], scope=late)
        work = ExitStack()
        xt = sb("xt", [P, P], scope=work)
        xv = sb("xv", [P, HALO + P], scope=work)
        sqk = sb("sqk", [P, 2, INNER], scope=work)
        ss = sb("ss", [P, 2, HEADS], scope=work)
        ssm = sb("ssm", [P, 2, HEADS], scope=work)
        rqk = sb("rqk", [P, 2, HEADS], scope=work)
        qkn = sb("qkn", [P, 2, INNER], scope=work)
        m1 = sb("m1", [P, 2, INNER], scope=work)
        m2 = sb("m2", [P, 2, INNER], scope=work)
        qT = sb("qT", [P, PAIRS, P], scope=work)
        smax = sb("smax", [P, HEADS], scope=work)
        ssub = sb("ssub", [P, INNER], scope=work)
        pE = sb("pE", [P, INNER], scope=work)
        pT = sb("pT", [P, PAIRS, P], scope=work)
        orec = sb("orec", [P, HEADS], scope=work)
        On = sb("On", [P, INNER], scope=work)
        OTs = sb("OTs", [P, PAIRS, P], scope=work)
        rot = m1
        work.close()
        ffn = ExitStack()
        fx = sb("fx", [P, 2, GW], scope=ffn)
        gl = sb("gl", [P, 3, GW], scope=ffn)
        hg = sb("hg", [P, 3, GW], scope=ffn)
        ffn.close()
        late.close()

        PS = ctx.enter_context(nc.psum_tensor("PS", [P, 8, GW], F32))

        s_load = sem("s_load")
        s_load2 = sem("s_load2")
        s_wa = sem("s_wa")
        s_wf = sem("s_wf")
        s_out = sem("s_out")
        s_const = sem("s_const")
        s_phase = sem("s_phase")
        s_apart = sem("s_apart")
        s_cast = sem("s_cast")
        s_silu = sem("s_silu")
        s_modps = sem("s_modps")
        s_mod = sem("s_mod")
        n_mean, n_xc, n_sq, n_var = step("n_mean"), step("n_xc"), step("n_sq"), step("n_var")
        n_ve, n_ln, n_r, n_used, n_out = step("n_ve"), step("n_ln"), step("n_r"), step("n_used"), step("n_out")
        a_ht, a_qk, a_qf, a_kf = step("a_ht"), step("a_qk"), step("a_qf"), step("a_kf")
        a_abs, a_exp, a_ln, a_qsp = sem("a_abs"), step("a_exp"), step("a_ln"), step("a_qsp")
        a_kv, a_ktok, a_v, a_qcs = step("a_kv"), step("a_ktok"), step("a_v"), step("a_qcs")
        a_bd, a_bdp, a_s, a_pm = step("a_bd"), step("a_bdp"), step("a_s"), step("a_pm")
        a_in, a_o = step("a_in"), step("a_o")
        a_oc, a_ot, a_nrm, a_rec = step("a_oc"), step("a_ot"), step("a_nrm"), step("a_rec")
        a_ctx, a_ct, a_st, a_stm = step("a_ctx"), step("a_ct"), step("a_st"), step("a_stm")
        a_state, a_done = step("a_state"), step("a_done")
        d_wo, d_h, d_up, d_act = step("d_wo"), step("d_h"), step("d_up"), step("d_act")
        d_y, d_h2, d_x = step("d_y"), step("d_h2"), step("d_x")
        e_lg, e_sg, e_sgt, e_s, e_dve = step("e_lg"), step("e_sg"), step("e_sgt"), step("e_s"), step("e_dve")
        e_comb, e_cT, e_cTs = step("e_comb"), step("e_cT"), step("e_cTs")
        e_u, e_act, e_mul, e_down, e_y, e_x = (step("e_u"), step("e_act"), step("e_mul"), step("e_down"),
                                               step("e_y"), step("e_x"))
        g_ps, g_out = step("g_ps"), step("g_out")
        f_wo, f_x, f_xs = step("f_wo"), step("f_x"), step("f_xs")
        t_rope, t_xt, t_xv, t_q, t_k = step("t_rope"), step("t_xt"), step("t_xv"), step("t_q"), step("t_k")
        t_sqq, t_sqk, t_red, t_sm = step("t_sqq"), step("t_sqk"), step("t_red"), step("t_sm")
        t_ln, t_root, t_nq, t_nk = step("t_ln"), step("t_root"), step("t_nq"), step("t_nk")
        t_mq, t_mk, t_rotq, t_rotk = step("t_mq"), step("t_mk"), step("t_rotq"), step("t_rotk")
        t_va, t_vb, t_vac, t_vbc = step("t_va"), step("t_vb"), step("t_vac"), step("t_vbc")
        t_qT, t_kT, t_qTc, t_kTc, t_halo = (step("t_qT"), step("t_kT"), step("t_qTc"), step("t_kTc"),
                                            step("t_halo"))
        t_s, t_max, t_sub, t_exp = step("t_s"), step("t_max"), step("t_sub"), step("t_exp")
        t_pT, t_pTc, t_o, t_orec, t_on = (step("t_pT"), step("t_pTc"), step("t_o"), step("t_orec"),
                                          step("t_on"))
        t_oT, t_oTc, t_y, t_h, t_xs = step("t_oT"), step("t_oTc"), step("t_y"), step("t_h"), step("t_xs")
        h_u, h_act, h_hg, h_y, h_h, h_xs = (step("h_u"), step("h_act"), step("h_hg"), step("h_y"),
                                            step("h_h"), step("h_xs"))

        loads = [
            (X[:, :], a["xT"]), (cT[:, :, :], a["cT"]), (wmod[:, :, :], a["wmod"]),
            (ident[:, :], a["ident"]), (onesm[:, :], a["onesm"]),
            (wq0[:, :], a["qkv_w"]), (bqk0[:, :], a["bqk0"]), (bkv0[:, :], a["bkv0"].broadcast_to([P, 2 * C])),
            (wo0[:, :], a["out_w"]), (cols0[:, :], a["cols0"]), (hmask[:, :], a["hmask"]), (hold[:, :], a["hold"]),
            (hm9[:, :, :], a["hm9"]),
            (cmask[:, :, :], a["cmask"]), (ccol[:, :, :], a["ccol"]),
            (crow[:, :, :], a["crow"].unsqueeze(0).broadcast_to([P, 2, L])),
            (mw1[:, :], a["mlp_w1"]), (mw2[:, :, :], a["mlp_w2"]),
            (wr[:, :], a["router_wT"]), (rbias[:, :], a["router_bias"].broadcast_to([P, EXPERTS])),
            (sw1[:, :], a["sw1"]), (sw3[:, :], a["sw3"]), (sw2[:, :, :], a["sw2"]),
            (ew1[:, :, :], a["ew1"]), (ew2[:, :, :], a["ew2"]), (wl1[:, :, :], a["wl1"]),
            (bg1[:, :], a["bg1"]), (esel[:, :, :], a["esel"]), (low[:, :, :], a["low"]),
        ]
        wmask32 = m1
        late_loads = [(rope[:, :, :, :], a["rope"]), (wmask32[:, :, 0:GW], a["wmask"])]
        loads_a = 3
        loads_f = 5

        def load_attention(sp, l):
            sp.dma_start(Wqkv[:, :], a["Wqkv"][ds(l, 1), :, :].rearrange("o p n -> (o p) n")).then_inc(s_wa, 16)
            sp.dma_start(Wo6[:, :, :], a["Wo"][ds(l, 1), :, :, :].rearrange("o p c n -> (o p) c n")).then_inc(s_wa, 16)
            sp.dma_start(qks[:, :, :], a["qks"][ds(l, 1), :, :].broadcast_to([P, 2, DH])).then_inc(s_wa, 16)

        def load_ffn(sp, l):
            sp.dma_start(W1[:, :], a["W1"][ds(l, 1), :, :].rearrange("o p n -> (o p) n")).then_inc(s_wf, 16)
            sp.dma_start(W2[:, :, :], a["W2"][ds(l, 1), :, :, :].rearrange("o p c n -> (o p) c n")).then_inc(s_wf, 16)
            sp.dma_start(lncol[:, :], a["lncol"][ds(l, 1), :, :].rearrange("o p n -> (o p) n")).then_inc(s_wf, 16)
            sp.dma_start(b1col[:, :], a["b1col"][ds(l, 1), :, :].rearrange("o p n -> (o p) n")).then_inc(s_wf, 16)
            sp.dma_start(b2col[:, :], a["b2col"][ds(l, 1), :, :].rearrange("o p n -> (o p) n")).then_inc(s_wf, 16)

        def wait_apart(eng, semaphore, value):
            eng.wait_ge(semaphore, value)
            eng.sem_inc(s_apart, 1)

        def end_phase(eng, n):
            eng.drain().then_inc(s_phase, 1)
            wait_apart(eng, s_phase, 4 * n + 4)

        PH_MOD, PH_PREP0, PH_ATT0, PH_MLP, PH_MOE, PH_PREP1, PH_ATT1, PH_WO1, PH_ZERO = range(9)
        PH_LAYERS = 9
        PH_FIN = PH_LAYERS + 2 * DEPTH

        LN_PREP0, ST_PREP0 = 0, 0
        LN_MLP, ST_MLP = NG, 2 * NG
        LN_MOE, ST_MOE = NG, 3 * NG
        LN_PREP1, ST_PREP1 = 2 * NG, 4 * NG
        LN_WO1, ST_WO1 = 3 * NG, 5 * NG
        LN_FFN, ST_FFN = 4 * NG, 6 * NG

        def mean_pe(pe, src, u, bank):
            pe.wait_ge(n_xc, u + 1)
            pe.matmul(PS[:, bank, :], onesm[:, :], src, start=True, stop=True).then_inc(n_mean, 1)

        def centre_dve(dve, src, u, su, bank):
            dve.wait_ge(n_mean, u + 2)
            dve.wait_ge(n_used, su + 1)
            dve.tensor_tensor(xc[:, :], src, PS[:, bank, :], ALU.subtract).then_inc(n_xc, 1)

        def square_act(act, src, su):
            act.wait_ge(n_var, su + 1)
            act.activation(sq[:, :], src, ACT.Square).then_inc(n_sq, 1)

        def var_pe(pe, su, bank):
            pe.wait_ge(n_sq, su + 2)
            pe.wait_ge(n_ve, su + 1)
            pe.matmul(PS[:, bank, :], onesm[:, :], sq[:, :], start=True, stop=True).then_inc(n_var, 1)

        def eps_dve(dve, su, bank, eps):
            dve.wait_ge(n_var, su + 2)
            dve.wait_ge(n_r, su + 1)
            dve.tensor_scalar(ve[:, :], PS[:, bank, :], eps, None, ALU.add).then_inc(n_ve, 1)

        def rsqrt_act(act, su, switch=False):
            if switch:
                act.preload_act_table_set(LOG_EXP)
            act.wait_ge(n_ve, su + 2)
            act.wait_ge(n_used, su + 1)
            act.activation(rs[:, :], ve[:, :], ACT.Ln).then_inc(n_ln, 1)
            act.wait_ge(n_ln, su + 2)
            act.activation(rs[:, :], rs[:, :], ACT.Exp, scale=-0.5).then_inc(n_r, 1)

        def affine_dve(dve, dst, u, su, scale, shift):
            dve.wait_ge(n_r, su + 2)
            dve.wait_ge(n_out, u + 1)
            dve.tensor_tensor(xn[:, :], xc[:, :], rs[:, :], ALU.mult).then_inc(n_used, 1)
            dve.wait_ge(n_used, su + 2)
            dve.tensor_scalar(dst, xn[:, :], scale, shift, ALU.mult, ALU.add).then_inc(n_out, 1)

        def group(t, g):
            return t[:, ds(g * GW, GW)]

        def xs_group(t, g, shift=0):
            return (g // GPB) * XSW + (g % GPB) * GW + (HALO + shift)

        def modcol(block, which, g):
            return mod[:, block, which, ds(g // GPB, 1)]

        SHIFT_A, SCALE_A, GATE_A, SHIFT_B, SCALE_B, GATE_B = range(6)

        def la_project_pe(pe, i, n, cosine):
            pe.wait_ge(a_ht, n + 2)
            wq, wk = (wq0[:, 0:C], wq0[:, C:2 * C]) if cosine else (wl1[:, 0, :], wl1[:, 1, :])
            pe.matmul(PS[:, 0, 0:P], wq, ht[:, :], start=True, stop=True)
            pe.matmul(PS[:, 0, P:2 * P], wk, ht[:, :], start=True, stop=True).then_inc(a_qk, 1)
            pe.wait_ge(a_v, n + 1)
            pe.wait_ge(a_ktok, n + 1)
            if cosine:
                pe.matmul(PS[:, 1, 0:2 * C], onesm[:, :], bkv0[:, :], start=True, stop=False)
                pe.matmul(PS[:, 1, 0:2 * C], ht[:, :], wq0[:, C:3 * C], start=False, stop=True).then_inc(a_kv, 1)
            else:
                pe.matmul(PS[:, 1, 0:2 * C], ht[:, :], wl1[:, 1:3, :].rearrange("p a c -> p (a c)"),
                          start=True, stop=True).then_inc(a_kv, 1)

        def la_scores_pe(pe, i, n, older):
            pe.wait_ge(a_kf, n + 2)
            pe.wait_ge(a_qf, n + 2)
            pe.wait_ge(a_bd, n + 2)
            pe.wait_ge(a_stm, n + 1)
            for q in range(4):
                if q == 1 and older:
                    pe.wait_ge(a_done, n - 2 + 2)
                if q == 2:
                    pe.wait_ge(a_bdp, n + 2)
                pe.matmul(PS[:, 2 + q, :], kf[:, :], Qbd[:, 4 * q:4 * q + 4, :].rearrange("p h t -> p (h t)"),
                          start=True, stop=True).then_inc(a_s, 1)

        def la_earlier_pe(pe, i, n, kinds):
            pe.wait_ge(a_oc, n + 1)
            pe.wait_ge(a_state, n + 1)
            pe.wait_ge(a_qcs, n + 2)
            for q in range(4):
                for c in range(kinds):
                    mm = pe.matmul(PS[:, 6, q * P:(q + 1) * P],
                                   state[:, c, 4 * q:4 * q + 4, :].rearrange("p h v -> p (h v)"),
                                   qcs[:, c, :], start=(q == 0 and c == 0), stop=False, skip_group_check=True)
            mm.then_inc(a_in, 1)

        def la_own_pe(pe, i, n, kinds):
            w = HEADS * (HD + 1)
            pe.wait_ge(a_v, n + 2)
            pe.wait_ge(a_pm, 4 * n + 5)
            for h in range(HEADS):
                r = VW * (h % 4)
                mm = pe.matmul(PS[r:r + VW, 6, (h // 4) * P:(h // 4 + 1) * P], vaug[:, h, :], Pm[:, h, :],
                               start=False, stop=(h == HEADS - 1), skip_group_check=True)
            mm.then_inc(a_o, 1)
            pe.wait_ge(a_ktok, n + 2)
            for c in range(kinds):
                mm = pe.matmul(PS[:, 2, c * w:(c + 1) * w], ktok[:, c, :], vaug[:, :, 0:HD + 1], start=True, stop=True)
            mm.then_inc(a_st, 1)

        def la_otok_pe(pe, i, n):
            pe.wait_ge(a_oc, n + 2)
            pe.wait_ge(a_ctx, n + 1)
            for q in range(4):
                mm = pe.transpose(PS[:, 7, q * P:(q + 1) * P], oT[:, q, :], ident[:, :])
            mm.then_inc(a_ot, 1)

        def la_ctx_pe(pe, i, n, newer):
            pe.wait_ge(a_ctx, n + 2)
            if newer:
                pe.wait_ge(a_pm, 4 * (n + 1) + 3)
            pe.transpose(PS[:, 3, 0:P], ctxt[:, :], ident[:, :]).then_inc(a_ct, 1)

        def la_pe(pe, i, n, A, B_, C_, cosine):
            kinds = 2 if cosine else 1
            if B_:
                la_scores_pe(pe, i - 1, n - 1, C_)
            if C_:
                la_otok_pe(pe, i - 2, n - 2)
            if A:
                la_project_pe(pe, i, n, cosine)
            if B_:
                la_earlier_pe(pe, i - 1, n - 1, kinds)
            if C_:
                la_ctx_pe(pe, i - 2, n - 2, B_)
            if B_:
                la_own_pe(pe, i - 1, n - 1, kinds)

        def la_act(act, i, n, A, B_, C_, cosine):
            if A:
                act.wait_ge(a_kv, n + 1)
                act.activation(ht[:, :], XSF[:, ds(i * P, P)], ACT.Copy).then_inc(a_ht, 1)
                act.wait_ge(a_qk, n + 2)
            if A and cosine:
                act.wait_ge(a_bd, n + 1)
                act.wait_ge(a_bdp, n + 1)
                act.wait_ge(a_qcs, n + 1)
                act.activation(qf[:, :], PS[:, 0, 0:P], ACT.Relu, bias=bqk0[:, 0:1]).then_inc(a_qf, 1)
                act.wait_ge(a_s, 4 * n + 1)
                act.activation(kf[:, :], PS[:, 0, P:2 * P], ACT.Relu, bias=bqk0[:, 1:2]).then_inc(a_kf, 1)
            elif A:
                act.wait_ge(a_exp, n - NT + 1)
                act.activation(spa[:, 0:2, :].rearrange("p a t -> p (a t)"), PS[:, 0, 0:2 * P], ACT.Abs).then_inc(a_abs, 1)
                act.wait_ge(a_kv, n + 2)
                act.activation(spa[:, 2, :], PS[:, 1, 0:P], ACT.Abs).then_inc(a_abs, 1)
                act.wait_ge(a_abs, 2 * i + 2)
                act.wait_ge(a_ln, n - NT + 1)
                act.activation(spe[:, :, :], spa[:, :, :], ACT.Exp, scale=-1.0).then_inc(a_exp, 1)
                act.wait_ge(a_exp, i + 2)
                act.wait_ge(a_ktok, n + 1)
                act.activation(spl[:, :, :], spe[:, :, :], ACT.Ln, bias=1.0).then_inc(a_ln, 1)
            if C_:
                act.wait_ge(a_ct, n - 2 + 2)
                dst = XSA if cosine else H
                act.activation(dst[:, ds((i - 2) * P, P)], PS[:, 3, 0:P], ACT.Copy).then_inc(a_done, 1)
            if B_:
                act.wait_ge(a_o, n - 1 + 2)
                act.wait_ge(a_ot, n - 1 + 1)
                act.activation(oT[:, :, :].rearrange("p a t -> p (a t)"), PS[:, 6, :], ACT.Copy).then_inc(a_oc, 1)

        HALF = HEADS // 2

        def la_pool(pool, i, n, A, B_, C_, cosine):
            if A:
                pool.wait_ge(a_qf, n + 2)
                wait_apart(pool, a_s, 4 * n + 1)
                for h in range(HALF, HEADS):
                    ins = pool.tensor_scalar(Qbd[:, h, :], qf[:, :], hmask[:, h:h + 1], 1.0, ALU.mult, ALU.mult)
                ins.then_inc(a_bdp, 1)

        def la_mask_dve(dve, i, n, cosine):
            dve.wait_ge(a_o, n + 1)
            for q in range(4):
                dve.wait_ge(a_s, 4 * n + q + 2)
                dve.tensor_tensor(Pm[:, 4 * q:4 * q + 4, :], PS[:, 2 + q, :].rearrange("p (h t) -> p h t", t=P),
                                  cmask[:, 0 if cosine else 1, :].unsqueeze(1).broadcast_to([P, 4, P]),
                                  ALU.mult).then_inc(a_pm, 1)

        def la_norm_dve(dve, i, n):
            dve.wait_ge(a_ot, n + 2)
            o = PS[:, 7, :].rearrange("p (h v) -> p h v", v=VW)
            dve.tensor_scalar(nrm[:, :], o[:, :, HD], 1e-6, None, ALU.add).then_inc(a_nrm, 1)
            dve.wait_ge(a_nrm, n + 2)
            dve.reciprocal(rec[:, :], nrm[:, :]).then_inc(a_rec, 1)
            dve.wait_ge(a_rec, n + 2)
            dve.wait_ge(a_ct, n + 1)
            dve.tensor_tensor(ctxt[:, :].rearrange("p (h d) -> p h d", d=HD), o[:, :, 0:HD],
                              rec[:, :].unsqueeze(2).broadcast_to([P, HEADS, HD]), ALU.mult).then_inc(a_ctx, 1)

        def la_queries_dve(dve, i, n, cosine):
            if not cosine:
                dve.wait_ge(a_ln, i + 2)
                dve.wait_ge(a_s, 4 * n + 1)
                dve.scalar_tensor_tensor(qsp[:, :], PS[:, 0, 0:P], 0.0, spl[:, 0, :], ALU.max, ALU.add).then_inc(a_qsp, 1)
                dve.scalar_tensor_tensor(kf[:, :], PS[:, 0, P:2 * P], 0.0, spl[:, 1, :], ALU.max, ALU.add).then_inc(a_kf, 1)
                dve.wait_ge(a_qsp, i + 2)
                dve.wait_ge(a_bd, n + 1)
                dve.wait_ge(a_bdp, n + 1)
                dve.wait_ge(a_qcs, n + 1)
                dve.scalar_tensor_tensor(qf[:, :], H[:, ds(i * P, P)], 1e-6, qsp[:, :], ALU.add, ALU.mult).then_inc(a_qf, 1)
            dve.wait_ge(a_qf, n + 2)
            dve.wait_ge(a_s, 4 * n + 1)
            dve.tensor_tensor(Qbd[:, 0:HALF, :], qf[:, :].unsqueeze(1).broadcast_to([P, HALF, P]),
                              hmask[:, 0:HALF].unsqueeze(2).broadcast_to([P, HALF, P]), ALU.mult).then_inc(a_bd, 1)
            dve.wait_ge(a_in, n + 1)
            if cosine:
                for c in range(2):
                    ins = dve.tensor_tensor(qcs[:, c, :], qf[:, :], crow[:, c, ds((i % TPB) * P, P)], ALU.mult)
            else:
                ins = dve.tensor_copy(qcs[:, 0, :], qf[:, :])
            ins.then_inc(a_qcs, 1)

        def la_state_dve(dve, i, n, kinds):
            w = HEADS * (HD + 1)
            keep = hold[:, ds(i % TPB, 1)]
            dve.wait_ge(a_st, n + 2)
            dve.wait_ge(a_state, n + 1)
            new = stnew[:, 0:kinds, :, :].rearrange("p c h v -> p (c h) v")
            dve.scalar_tensor_tensor(new, PS[:, 2, 0:kinds * w].rearrange("p (h v) -> p h v", v=HD + 1), keep,
                                     hm9[:, 0:kinds * HEADS, :], ALU.mult, ALU.mult).then_inc(a_stm, 1)
            dve.wait_ge(a_stm, n + 2)
            sums = state[:, 0:kinds, :, 0:HD + 1].rearrange("p c h v -> p (c h) v")
            dve.scalar_tensor_tensor(sums, sums, keep, new, ALU.mult, ALU.add).then_inc(a_state, 1)

        def la_tokens_dve(dve, i, n, cosine):
            dve.wait_ge(a_st, n + 1)
            dve.wait_ge(a_kv, n + 2)
            dve.tensor_copy(vaug[:, :, 0:HD], PS[:, 1, C:2 * C].rearrange("p (h d) -> p h d", d=HD)).then_inc(a_v, 1)
            if cosine:
                for c in range(2):
                    ins = dve.tensor_scalar(ktok[:, c, :], PS[:, 1, 0:C], 0.0, ccol[:, c, ds(i % TPB, 1)],
                                            ALU.max, ALU.mult)
                ins.then_inc(a_ktok, 1)
            else:
                dve.scalar_tensor_tensor(ktok[:, 0, :], PS[:, 1, 0:C], 0.0, spl[:, 2, :], ALU.max, ALU.add).then_inc(a_ktok, 1)

        def la_dve(dve, i, n, A, B_, C_, cosine):
            if B_:
                la_mask_dve(dve, i - 1, n - 1, cosine)
            if C_:
                la_norm_dve(dve, i - 2, n - 2)
            if A:
                la_queries_dve(dve, i, n, cosine)
            if B_:
                la_state_dve(dve, i - 1, n - 1, 2 if cosine else 1)
            if A:
                la_tokens_dve(dve, i, n, cosine)

        def la_tiles(eng, body, cosine):
            n0 = 0 if cosine else NT

            def peeled(i):
                body(eng, i, n0 + i, *(s <= i < NT + s for s in range(3)), cosine)

            peeled(0)
            peeled(1)
            with eng.Fori(2, NT) as i:
                body(eng, i, i + n0, True, True, True, cosine)
            peeled(NT)
            peeled(NT + 1)

        def mlp_a_pe(pe, g):
            pe.wait_ge(d_h, g + 1)
            pe.matmul(PS[:, 2, :], wo0[:, :], group(XSA, g), start=True, stop=True).then_inc(d_wo, 1)
            var_pe(pe, ST_MLP + g, 1)

        def mlp_b_pe(pe, g):
            pe.wait_ge(n_used, ST_MLP + g + 2)
            for f in range(F_MLP):
                pe.wait_ge(d_act, F_MLP * g + f + 1)
                pe.matmul(PS[:, 3 + f, :], mw1[:, f * P:(f + 1) * P], hin[:, ds(g % 2, 1), :],
                          start=True, stop=True).then_inc(d_up, 1)
            pe.wait_ge(d_h2, g + 1)
            for f in range(F_MLP):
                pe.wait_ge(d_act, F_MLP * g + f + 2)
                mm = pe.matmul(PS[:, 7, :], mw2[:, f, :], hidm[:, f, :], start=(f == 0), stop=(f == F_MLP - 1))
            mm.then_inc(d_y, 1)

        def mlp_a_act(act, g):
            act.wait_ge(d_h, g + 2)
            square_act(act, group(H, g), ST_MLP + g)
            rsqrt_act(act, ST_MLP + g, switch=True)

        def mlp_b_act(act, g):
            for f in range(F_MLP):
                act.wait_ge(d_up, F_MLP * g + f + 2)
                act.wait_ge(d_y, g + 1)
                act.activation(hidm[:, f, :], PS[:, 3 + f, :], ACT.Gelu_apprx_tanh,
                               bias=cols0[:, 4 + f:5 + f]).then_inc(d_act, 1)

        def mlp_a_dve(dve, g):
            su = ST_MLP + g
            dve.wait_ge(d_wo, g + 2)
            dve.scalar_tensor_tensor(group(H, g), PS[:, 2, :], cols0[:, 0:1], group(H, g), ALU.add, ALU.add).then_inc(d_h, 1)
            eps_dve(dve, su, 1, 1e-6)
            dve.wait_ge(n_r, su + 2)
            dve.wait_ge(d_up, F_MLP * g + 1)
            dve.scalar_tensor_tensor(hin[:, ds(g % 2, 1), :], group(H, g).unsqueeze(1), cols0[:, 2:3],
                                     rs[:, :].unsqueeze(1), ALU.mult, ALU.mult).then_inc(n_used, 1)

        def mlp_b_dve(dve, g):
            dve.wait_ge(d_y, g + 2)
            dve.scalar_tensor_tensor(group(H, g), PS[:, 7, :], cols0[:, 3:4], group(H, g), ALU.add, ALU.add).then_inc(d_h2, 1)
            dve.wait_ge(d_h2, g + 2)
            dve.scalar_tensor_tensor(group(X, g), group(H, g), modcol(0, GATE_A, g), group(X, g),
                                     ALU.mult, ALU.add).then_inc(d_x, 1)

        ITEMS = SHARED + EXPERTS

        def moe_router_pe(pe, g):
            pe.wait_ge(n_out, LN_MOE + g + 2)
            pe.wait_ge(e_cTs, g + 1)
            pe.matmul(PS[0:EXPERTS, 2, :], wr[:, :], hin[:, ds(g % 2, 1), :], start=True, stop=True).then_inc(e_lg, 1)
            wait_apart(pe, e_sg, g + 2)
            for t in range(4):
                mm = pe.transpose(PS[:, 2, t * EXPERTS:(t + 1) * EXPERTS], sgT[:, t * P:(t + 1) * P],
                                  ident[0:EXPERTS, 0:EXPERTS])
            mm.then_inc(e_sgt, 1)

        def moe_weights_pe(pe, g):
            pe.wait_ge(e_comb, g + 2)
            for t in range(4):
                mm = pe.transpose(PS[0:EXPERTS, 2, t * P:(t + 1) * P], comb[:, t, :], ident[:, :])
            mm.then_inc(e_cT, 1)

        def moe_up_pe(pe, g, k):
            c = ITEMS * g + k
            pe.wait_ge(e_mul, c)
            if k < SHARED:
                first, second, rhs2 = sw1[:, k * P:(k + 1) * P], sw3[:, k * P:(k + 1) * P], hin[:, ds(g % 2, 1), :]
            else:
                first, second, rhs2 = ew1[:, k - SHARED, :], esel[:, k - SHARED, :], combT[:, :]
            if k == SHARED:
                pe.wait_ge(e_cTs, g + 2)
            pe.matmul(PS[:, 3 + k % 2, :], first, hin[:, ds(g % 2, 1), :], start=True, stop=True)
            pe.matmul(PS[:, 5 + k % 2, :], second, rhs2, start=True, stop=True).then_inc(e_u, 1)

        def moe_down_pe(pe, g, k):
            pe.wait_ge(e_mul, ITEMS * g + k + 2)
            if k == 0:
                pe.wait_ge(e_x, g + 1)
            w = sw2[:, k, :] if k < SHARED else ew2[:, k - SHARED, :]
            pe.matmul(PS[:, 7, :], w, hid2[:, k % 2, :], start=(k == 0), stop=(k == ITEMS - 1)).then_inc(e_down, 1)

        def moe_act(act, g, k):
            c = ITEMS * g + k
            act.wait_ge(e_u, c + 2)
            act.wait_ge(e_mul, c)
            act.activation(hid[:, k % 2, :], PS[:, 3 + k % 2, :], ACT.Silu if k < SHARED else ACT.Gelu).then_inc(e_act, 1)

        def moe_mul_dve(dve, g, k):
            c = ITEMS * g + k
            dve.wait_ge(e_act, c + 2)
            dve.wait_ge(e_down, c)
            dve.tensor_tensor(hid2[:, k % 2, :], hid[:, k % 2, :], PS[:, 5 + k % 2, :], ALU.mult).then_inc(e_mul, 1)

        ROUTE = 12

        def moe_route_dve(dve, g):
            k = [0]

            def link(ins):
                k[0] += 1
                ins.then_inc(e_dve, 1)
                dve.wait_ge(e_dve, ROUTE * g + k[0] + 1)

            b4 = [P, 4, EXPERTS, EXPERTS]
            dve.wait_ge(e_sgt, g + 2)
            dve.wait_ge(e_cT, g + 1)
            dve.tensor_copy(sg[:, :, :], PS[:, 2, 0:4 * EXPERTS].rearrange("p (t e) -> p t e", e=EXPERTS)).then_inc(e_s, 1)
            dve.wait_ge(e_s, g + 2)
            link(dve.tensor_tensor(sel[:, :, :], sg[:, :, :], rbias[:, :].unsqueeze(1).broadcast_to([P, 4, EXPERTS]), ALU.add))
            other, own = sel[:, :, :].unsqueeze(2).broadcast_to(b4), sel[:, :, :].unsqueeze(3).broadcast_to(b4)
            dve.tensor_tensor(above[:, :, :, :], other, own, ALU.is_gt)
            link(dve.tensor_tensor(level[:, :, :, :], other, own, ALU.is_ge))
            link(dve.tensor_tensor(level[:, :, :, :], level[:, :, :, :], low[:, :, :].unsqueeze(1).broadcast_to(b4), ALU.mult))
            link(dve.tensor_tensor(above[:, :, :, :], above[:, :, :, :], level[:, :, :, :], ALU.max))
            link(dve.tensor_reduce(rank[:, :, :], above[:, :, :, :], AX.X, ALU.add))
            link(dve.tensor_scalar(selm[:, :, :], rank[:, :, :], 2.0, None, ALU.is_lt))
            link(dve.tensor_tensor(ssel[:, :, :], selm[:, :, :], sg[:, :, :], ALU.mult))
            link(dve.tensor_reduce(den[:, 0, :], ssel[:, :, :], AX.X, ALU.add))
            dve.tensor_scalar(den[:, 1, :], den[:, 0, :], 1e-9, None, ALU.add)
            link(dve.tensor_scalar(den[:, 2, :], den[:, 0, :], 1e-9, None, ALU.is_gt))
            dve.tensor_scalar(den[:, 4, :], den[:, 2, :], -0.5, 0.5, ALU.mult, ALU.add)
            link(dve.reciprocal(den[:, 1, :], den[:, 1, :]))
            link(dve.tensor_tensor(den[:, 3, :], den[:, 1, :], den[:, 2, :], ALU.mult))
            dve.tensor_tensor(gsel[:, :, :], ssel[:, :, :], den[:, 3, :].unsqueeze(2).broadcast_to([P, 4, EXPERTS]), ALU.mult)
            link(dve.tensor_tensor(gelse[:, :, :], selm[:, :, :], den[:, 4, :].unsqueeze(2).broadcast_to([P, 4, EXPERTS]), ALU.mult))
            assert k[0] == ROUTE
            dve.tensor_tensor(comb[:, :, :], gsel[:, :, :], gelse[:, :, :], ALU.add).then_inc(e_comb, 1)
            dve.wait_ge(e_cT, g + 2)
            dve.tensor_copy(combT[0:EXPERTS, :], PS[0:EXPERTS, 2, :]).then_inc(e_cTs, 1)

        def two_banks(first):
            return PS[:, first:first + 2, :].rearrange("p b n -> p (b n)")

        def column(eng, i, at):
            off = (i // TPB) * XSW + (i % TPB) * P + at
            return off if isinstance(i, int) else eng.snap(off)

        def project(pe, bank, x, kind):
            for j in range(2):
                c0 = kind * INNER + j * GW
                mm = pe.matmul(PS[:, bank + j, :], x, Wqkv[:, c0:c0 + GW], start=True, stop=True)
            return mm

        def qk_pe(pe, i, n, older):
            pe.wait_ge(t_xt, n + 2)
            pe.wait_ge(t_nq, n + 1)
            project(pe, 0, xt[:, :], 0).then_inc(t_q, 1)
            if older:
                pe.wait_ge(t_on, n - 3 + 2)
            pe.wait_ge(t_nk, n + 1)
            project(pe, 2, xt[:, :], 1).then_inc(t_k, 1)

        def v_pe(pe, i, n, newer):
            pe.wait_ge(t_xv, n + 2)
            if newer:
                pe.wait_ge(t_nq, n + 2 + 2)
            project(pe, 0, xv[:, HALO:HALO + P], 2).then_inc(t_va, 1)
            if newer:
                pe.wait_ge(t_nk, n + 2 + 2)
            project(pe, 2, xv[:, 0:P], 2).then_inc(t_vb, 1)

        def eight_transposes(pe, bank, src):
            for j in range(8):
                mm = pe.transpose(PS[:, bank + j // 4, (j % 4) * P:(j % 4 + 1) * P], src(j), ident[:, :])
            return mm

        def pT_pe(pe, i, n):
            pe.wait_ge(t_exp, n + 2)
            eight_transposes(pe, 6, lambda j: pE[:, j * P:(j + 1) * P]).then_inc(t_pT, 1)

        OB = [(3, 0), (3, 1), (4, 0), (4, 1), (4, 2), (5, 0), (5, 1), (5, 2)]

        def pv_pe(pe, i, n):
            pe.wait_ge(t_pTc, n + 2)
            pe.wait_ge(t_vac, n + 2)
            pe.wait_ge(t_vbc, n + 2)
            pe.wait_ge(t_h, n + 1)
            for p in range(PAIRS):
                bank, at = OB[p]
                for w in range(NWIN):
                    mm = pe.matmul(PS[WIN * w:WIN * (w + 1), bank, at * VB_W:(at + 1) * VB_W],
                                   pT[:, p, WIN * w:WIN * (w + 1)], Vbd[:, w, p, :], start=True, stop=True)
            mm.then_inc(t_o, 1)

        def oT_pe(pe, i, n):
            pe.wait_ge(t_on, n + 2)
            eight_transposes(pe, 4, lambda j: On[:, j * P:(j + 1) * P]).then_inc(t_oT, 1)

        def wo_pe(pe, i, n):
            pe.wait_ge(t_oTc, n + 2)
            for c in range(PAIRS):
                mm = pe.matmul(PS[:, 4, 0:P], Wo6[:, c, :], OTs[:, c, :], start=(c == 0), stop=(c == PAIRS - 1))
            mm.then_inc(t_y, 1)

        def qkT_pe(pe, i, n, older):
            pe.wait_ge(t_rotq, n + 2)
            pe.wait_ge(t_pTc, n + 1)
            eight_transposes(pe, 6, lambda j: rot[:, 0, j * P:(j + 1) * P]).then_inc(t_qT, 1)
            pe.wait_ge(t_rotk, n + 2)
            if older:
                pe.wait_ge(t_h, n - 2 + 2)
            eight_transposes(pe, 4, lambda j: rot[:, 1, j * P:(j + 1) * P]).then_inc(t_kT, 1)

        def s_pe(pe, i, n):
            first = (i % TPB + TPB - 1) // TPB
            first = first if isinstance(i, int) else pe.snap(first)
            pe.wait_ge(t_qTc, n + 2)
            for j in range(2):
                pe.matmul(PS[:, 6 + j, :], identh[:, :], wmask[:, ds(first, 1), :], start=True, stop=False,
                          skip_group_check=True)
            pe.wait_ge(t_kTc, n + 2)
            for p in range(PAIRS):
                for w in range(NWIN):
                    mm = pe.matmul(PS[WIN * w:WIN * (w + 1), 6 + p // 4, (p % 4) * P:(p % 4 + 1) * P],
                                   qT[:, p, WIN * w:WIN * (w + 1)], kbd[:, p, :, WIN * w:WIN * w + KEYS],
                                   start=False, stop=(p % 4 == 3), skip_group_check=True)
            mm.then_inc(t_s, 1)

        def exp_act(act, i, n):
            act.wait_ge(t_sub, n + 2)
            act.wait_ge(t_pT, n + 1)
            act.activation(pE[:, :], ssub[:, :], ACT.Exp).then_inc(t_exp, 1)

        def sq_act(act, i, n):
            act.wait_ge(t_q, n + 2)
            act.wait_ge(t_red, n + 1)
            act.activation(sqk[:, 0, :], two_banks(0), ACT.Square).then_inc(t_sqq, 1)
            act.wait_ge(t_k, n + 2)
            act.activation(sqk[:, 1, :], two_banks(2), ACT.Square).then_inc(t_sqk, 1)

        def root_act(act, i, n):
            act.wait_ge(t_sm, n + 2)
            act.wait_ge(t_nk, n + 1)
            act.activation(rqk[:, :, :], ssm[:, :, :], ACT.Ln).then_inc(t_ln, 1)
            act.wait_ge(t_ln, n + 2)
            act.activation(rqk[:, :, :], rqk[:, :, :], ACT.Exp, scale=-0.5).then_inc(t_root, 1)

        def pTc_act(act, i, n):
            act.wait_ge(t_pT, n + 2)
            act.wait_ge(t_o, n + 1)
            act.activation(pT[:, :, :].rearrange("p c t -> p (c t)"), two_banks(6), ACT.Copy).then_inc(t_pTc, 1)

        def v_windows(act, bank, windows):
            for half, w in enumerate(windows):
                v = PS[64 * half:64 * half + KEYS, bank:bank + 2, :].rearrange("p b (c d) -> p (b c) d", d=2 * DH)
                for hd in range(2):
                    ins = act.activation(Vbd[64 * hd:64 * hd + KEYS, w, :, hd * DH:(hd + 1) * DH],
                                         v[:, :, hd * DH:(hd + 1) * DH], ACT.Copy)
            return ins

        def vc_act(act, i, n):
            act.wait_ge(t_o, n + 1)
            act.wait_ge(t_va, n + 2)
            v_windows(act, 0, (1, 3)).then_inc(t_vac, 1)
            act.wait_ge(t_vb, n + 2)
            v_windows(act, 2, (0, 2)).then_inc(t_vbc, 1)

        def oTc_act(act, i, n):
            act.wait_ge(t_oT, n + 2)
            act.wait_ge(t_y, n + 1)
            act.activation(OTs[:, :, :].rearrange("p c t -> p (c t)"), two_banks(4), ACT.Copy).then_inc(t_oTc, 1)

        def qkTc_act(act, i, n):
            act.wait_ge(t_qT, n + 2)
            act.wait_ge(t_s, n + 1)
            act.activation(qT[:, :, :].rearrange("p c t -> p (c t)"), two_banks(6), ACT.Copy).then_inc(t_qTc, 1)
            act.wait_ge(t_kT, n + 2)
            act.wait_ge(t_halo, n + 2)
            act.activation(kbd[0:DH, :, 0, HALO:HALO + P],
                           PS[0:DH, 4:6, :].rearrange("p b (c t) -> p (b c) t", t=P), ACT.Copy)
            act.activation(kbd[DH:2 * DH, :, 1, HALO:HALO + P],
                           PS[DH:2 * DH, 4:6, :].rearrange("p b (c t) -> p (b c) t", t=P), ACT.Copy).then_inc(t_kTc, 1)

        def heads(ap, width):
            return ap.rearrange("p (h d) -> p h d", d=width)

        def rope_dve(dve, l):
            dve.wait_ge(s_wa, 16 * loads_a * (l + 1))
            dve.tensor_tensor(ropel[:, 0, :, :], rope[:, 0, :, :],
                              qks[:, :, :].rearrange("p k d -> p (k d)").unsqueeze(1).broadcast_to([P, TPB, 2 * DH]), ALU.mult)
            for half in range(2):
                a0, b0 = half * (DH // 2), (1 - half) * (DH // 2)
                for k in range(2):
                    ins = dve.tensor_tensor(ropel[:, 1, :, k * DH + a0:k * DH + a0 + DH // 2],
                                            rope[:, 1, :, k * DH + a0:k * DH + a0 + DH // 2],
                                            qks[:, k, b0:b0 + DH // 2].unsqueeze(1).broadcast_to([P, TPB, DH // 2]), ALU.mult)
            ins.then_inc(t_rope, 1)
            dve.wait_ge(t_rope, l + 2)

        def softmax_dve(dve, i, n):
            dve.wait_ge(t_s, n + 2)
            dve.tensor_reduce(smax[:, :], heads(two_banks(6), KEYS), AX.X, ALU.max).then_inc(t_max, 1)
            dve.wait_ge(t_max, n + 2)
            dve.wait_ge(t_exp, n + 1)
            dve.tensor_tensor(heads(ssub[:, :], KEYS), heads(two_banks(6), KEYS),
                              smax[:, :].unsqueeze(2).broadcast_to([P, HEADS, KEYS]), ALU.subtract).then_inc(t_sub, 1)

        def red_dve(dve, i, n):
            dve.wait_ge(t_sqq, n + 2)
            dve.wait_ge(t_sqk, n + 2)
            dve.wait_ge(t_sm, n + 1)
            dve.tensor_reduce(ss[:, :, :], sqk[:, :, :].rearrange("p k (h d) -> p k h d", d=DH), AX.X, ALU.add).then_inc(t_red, 1)
            dve.wait_ge(t_red, n + 2)
            dve.wait_ge(t_ln, n + 1)
            dve.tensor_scalar(ssm[:, :, :], ss[:, :, :], 1e-24, None, ALU.max).then_inc(t_sm, 1)

        def scale_dve(dve, i, n):
            dve.wait_ge(t_root, n + 2)
            for k, (read, done) in enumerate(((t_mq, t_nq), (t_mk, t_nk))):
                dve.wait_ge(read, n + 1)
                dve.tensor_tensor(heads(qkn[:, k, :], DH), heads(two_banks(2 * k), DH),
                                  rqk[:, k, :].unsqueeze(2).broadcast_to([P, HEADS, DH]), ALU.mult).then_inc(done, 1)

        def rotate_dve(dve, i, n):
            T = i % TPB if isinstance(i, int) else dve.snap(i % TPB)
            half = DH // 2
            for k, (given, used, done) in enumerate(((t_nq, t_qT, t_mq), (t_nk, t_kT, t_mk))):

                def table(c, d0, d1):
                    return ropel[:, c, ds(T, 1), k * DH + d0:k * DH + d1].broadcast_to([P, HEADS, d1 - d0])

                dve.wait_ge(given, n + 2)
                dve.wait_ge(used, n + 1)
                v, w1, w2 = heads(qkn[:, k, :], DH), heads(m1[:, k, :], DH), heads(m2[:, k, :], DH)
                dve.tensor_tensor(w1, v, table(0, 0, DH), ALU.mult)
                dve.tensor_tensor(w2[:, :, 0:half], v[:, :, half:DH], table(1, 0, half), ALU.mult)
                dve.tensor_tensor(w2[:, :, half:DH], v[:, :, 0:half], table(1, half, DH), ALU.mult).then_inc(done, 1)

        def onorm_dve(dve, i, n):
            dve.wait_ge(t_o, n + 2)
            p0 = 0
            spans = []
            for bank, cnt in ((3, 2), (4, 3), (5, 3)):
                spans.append((p0, cnt, PS[:, bank, 0:cnt * VB_W].rearrange("p (c v) -> p c v", v=VB_W)))
                p0 += cnt
            for p0, cnt, o in spans:
                ins = dve.reciprocal(orec[:, 2 * p0:2 * (p0 + cnt)].rearrange("p (c s) -> p c s", s=2), o[:, :, 2 * DH:VB_W])
            ins.then_inc(t_orec, 1)
            dve.wait_ge(t_orec, n + 2)
            dve.wait_ge(t_oT, n + 1)
            for p0, cnt, o in spans:
                for s in range(2):
                    ins = dve.tensor_tensor(
                        On[:, :].rearrange("p (c d) -> p c d", d=2 * DH)[:, p0:p0 + cnt, s * DH:(s + 1) * DH],
                        o[:, :, s * DH:(s + 1) * DH],
                        orec[:, :].rearrange("p (c s) -> p c s", s=2)[:, p0:p0 + cnt, s:s + 1].broadcast_to([P, cnt, DH]), ALU.mult)
            ins.then_inc(t_on, 1)

        def resid_dve(dve, i, n):
            dve.wait_ge(t_y, n + 2)
            h = H[:, ds(i * P, P)]
            dve.tensor_tensor(h, h, PS[:, 4, 0:P], ALU.add).then_inc(t_h, 1)

        def xt_pool(pool, i, n):
            off = column(pool, i, HALO)
            wait_apart(pool, t_k, n + 1)
            pool.tensor_copy(xt[:, :], XSA[:, ds(off, P)]).then_inc(t_xt, 1)

        def xv_pool(pool, i, n):
            off = column(pool, i, 0)
            wait_apart(pool, t_vb, n + 1)
            pool.tensor_copy(xv[:, :], XSA[:, ds(off, HALO + P)]).then_inc(t_xv, 1)
            wait_apart(pool, t_xv, n + 2)

        def halo_pool(pool, i, n):
            wait_apart(pool, t_s, n + 1)
            pool.tensor_copy(kbd[:, :, :, 0:HALO], kbd[:, :, :, P:P + HALO]).then_inc(t_halo, 1)

        def rotate_pool(pool, i, n):
            for k, (given, done) in enumerate(((t_mq, t_rotq), (t_mk, t_rotk))):
                pool.wait_ge(given, n + 2)
                pool.tensor_tensor(rot[:, k, :], m1[:, k, :], m2[:, k, :], ALU.add).then_inc(done, 1)
            wait_apart(pool, t_rotk, n + 2)

        def shift_copies(pool, dst, off, src, done, n):
            w = src.shape[-1]
            pool.tensor_copy(dst[0:64, ds(off, w)], src[0:64, :])
            pool.tensor_copy(dst[64:128, ds(off + 1, w)], src[64:128, :]).then_inc(done, 1)
            wait_apart(pool, done, n + 2)

        def xs_pool(pool, i, n):
            off = column(pool, i, HALO)
            wait_apart(pool, t_h, n + 2)
            shift_copies(pool, XSF, off, H[:, ds(i * P, P)], t_xs, n)

        def att_pe(pe, i, n, A, B_, C_, D):
            if D:
                pv_pe(pe, i - 3, n - 3)
            if A:
                qk_pe(pe, i, n, D)
            if C_:
                pT_pe(pe, i - 2, n - 2)
            if D:
                oT_pe(pe, i - 3, n - 3)
                wo_pe(pe, i - 3, n - 3)
            if B_:
                qkT_pe(pe, i - 1, n - 1, D)
            if C_:
                v_pe(pe, i - 2, n - 2, A)
            if B_:
                s_pe(pe, i - 1, n - 1)

        def att_act(act, i, n, A, B_, C_, D):
            if C_:
                exp_act(act, i - 2, n - 2)
            if A:
                sq_act(act, i, n)
            if C_:
                pTc_act(act, i - 2, n - 2)
            if D:
                oTc_act(act, i - 3, n - 3)
            if A:
                root_act(act, i, n)
            if B_:
                qkTc_act(act, i - 1, n - 1)
            if C_:
                vc_act(act, i - 2, n - 2)

        def att_dve(dve, i, n, A, B_, C_, D):
            if C_:
                softmax_dve(dve, i - 2, n - 2)
            if D:
                onorm_dve(dve, i - 3, n - 3)
            if B_:
                rotate_dve(dve, i - 1, n - 1)
            if A:
                red_dve(dve, i, n)
            if D:
                resid_dve(dve, i - 3, n - 3)
            if A:
                scale_dve(dve, i, n)

        def att_pool(pool, i, n, A, B_, C_, D):
            if isinstance(i, int) and i == 0:
                xt_pool(pool, 0, n)
            if C_:
                xv_pool(pool, i - 2, n - 2)
            if B_:
                halo_pool(pool, i - 1, n - 1)
                rotate_pool(pool, i - 1, n - 1)
            if D:
                xs_pool(pool, i - 3, n - 3)
            if not isinstance(i, int) or i + 1 < NT:
                xt_pool(pool, i + 1, n + 1)

        def tiles(eng, l, body):
            def peeled(i):
                body(eng, i, l * NT + i, *(s <= i < NT + s for s in range(4)))

            for i in range(3):
                peeled(i)
            with eng.Fori(3, NT - 1) as i:
                body(eng, i, l * NT + i, True, True, True, True)
            for i in range(NT - 1, NT + 3):
                peeled(i)

        def ff_mean_pe(pe, g, n):
            mean_pe(pe, XSF[:, ds(xs_group(XSF, g), GW)], LN_FFN + n, 0)

        def ff_up_pe(pe, g, n):
            pe.wait_ge(n_out, LN_FFN + n + 2)
            for c in range(3):
                c0, m = CH[c]
                pe.wait_ge(h_h if c == 0 else h_act, n + 1 if c == 0 else 3 * n + 1)
                pe.matmul(PS[0:m, 2 + c, :], W1[:, DIN + c0:DIN + c0 + m], fx[:, ds(n % 2, 1), :],
                          start=True, stop=True)
                pe.wait_ge(h_hg, 3 * n + 1)
                pe.matmul(PS[0:m, 5 + c, :], W1[:, c0:c0 + m], fx[:, ds(n % 2, 1), :],
                          start=True, stop=True).then_inc(h_u, 1)

        def ff_down_pe(pe, g, n):
            for c in range(3):
                c0, m = CH[c]
                pe.wait_ge(h_hg, 3 * n + c + 2)
                mm = pe.matmul(PS[:, 2, :], W2[0:m, c, :], hg[0:m, c, :], start=(c == 0), stop=(c == 2))
            mm.then_inc(h_y, 1)

        def ff_act(act, g, n):
            for c in range(3):
                c0, m = CH[c]
                act.wait_ge(h_u, 3 * n + c + 2)
                act.wait_ge(h_hg, 3 * n + 1)
                act.activation(gl[0:m, c, :], PS[0:m, 2 + c, :], ACT.Gelu, bias=b1col[0:m, 3 + c:4 + c]).then_inc(h_act, 1)

        def ff_mul_dve(dve, g, n):
            for c in range(3):
                c0, m = CH[c]
                dve.wait_ge(h_act, 3 * n + c + 2)
                dve.wait_ge(h_y, n + 1)
                dve.scalar_tensor_tensor(hg[0:m, c, :], PS[0:m, 5 + c, :], b1col[0:m, c:c + 1], gl[0:m, c, :],
                                         ALU.add, ALU.mult).then_inc(h_hg, 1)

        def ff_h_dve(dve, g, n):
            dve.wait_ge(h_y, n + 2)
            dve.scalar_tensor_tensor(group(H, g), PS[:, 2, :], b2col[:, 0:1], group(H, g), ALU.add, ALU.add).then_inc(h_h, 1)

        def ff_norm_dve(dve, g, n, part):
            u, su = LN_FFN + n, ST_FFN + n
            if part == 0:
                centre_dve(dve, XSF[:, ds(xs_group(XSF, g), GW)], u, su, 0)
            else:
                eps_dve(dve, su, 1, 1e-5)
                dve.wait_ge(h_u, 3 * n + 1)
                affine_dve(dve, fx[:, ds(n % 2, 1), :], u, su, lncol[:, 0:1], lncol[:, 1:2])

        def xs_off(eng, g):
            return xs_group(XSF, g) if isinstance(g, int) else eng.snap(xs_group(XSF, g))

        def ff_pool(pool, g, n):
            off = xs_off(pool, g)
            wait_apart(pool, h_h, n + 2)
            shift_copies(pool, XSA, off, group(H, g), h_xs, n)

        def groups(eng, l, first, body):
            first(eng, 0, l * NG)
            with eng.Fori(0, NG - 1) as g:
                body(eng, g, l * NG + g, True)
            body(eng, NG - 1, l * NG + NG - 1, False)

        def ff_body_pe(pe, g, n, more):
            if more:
                ff_mean_pe(pe, g + 1, n + 1)
            ff_up_pe(pe, g, n)
            if more:
                var_pe(pe, ST_FFN + n + 1, 1)
            ff_down_pe(pe, g, n)

        def ff_first_pe(pe, g, n):
            ff_mean_pe(pe, g, n)
            var_pe(pe, ST_FFN + n, 1)

        def ff_sq_act(act, g, n):
            act.wait_ge(n_xc, LN_FFN + n + 2)
            square_act(act, xc[:, :], ST_FFN + n)

        def ff_first_act(act, g, n):
            ff_sq_act(act, g, n)
            rsqrt_act(act, ST_FFN + n, switch=True)

        def ff_body_act(act, g, n, more):
            if more:
                ff_sq_act(act, g + 1, n + 1)
            ff_act(act, g, n)
            if more:
                rsqrt_act(act, ST_FFN + n + 1, switch=True)

        def ff_first_dve(dve, g, n):
            ff_norm_dve(dve, g, n, 0)
            ff_norm_dve(dve, g, n, 1)

        def ff_body_dve(dve, g, n, more):
            if more:
                ff_norm_dve(dve, g + 1, n + 1, 0)
            ff_mul_dve(dve, g, n)
            if more:
                ff_norm_dve(dve, g + 1, n + 1, 1)
            ff_h_dve(dve, g, n)

        block = ctx.enter_context(nc.Block())

        @block.sync
        def _(sp):
            for s in primed:
                sp.sem_inc(s, 1)
            for dst, src in loads:
                sp.dma_start(dst, src).then_inc(s_load, 16)
            load_attention(sp, 0)
            load_ffn(sp, 0)
            sp.wait_ge(s_phase, 4 * (PH_WO1 + 1))
            for dst, src in late_loads:
                sp.dma_start(dst, src).then_inc(s_load2, 16)
            with sp.Fori(1, DEPTH) as l:
                sp.wait_ge(s_phase, 4 * (PH_LAYERS + 2 * l - 1))
                load_attention(sp, l)
                sp.wait_ge(s_phase, 4 * (PH_LAYERS + 2 * l))
                load_ffn(sp, l)
            with sp.Fori(0, NG) as g:
                sp.wait_ge(f_x, g + NG + 2)
                sp.dma_start(out[:, ds(g * GW, GW)], group(X, g)).then_inc(s_out, 16)
            sp.wait_ge(s_out, 16 * NG)

        @block.tensor
        def _(pe):
            pe.wait_ge(s_load, 16 * len(loads))
            pe.wait_ge(s_silu, 1)
            for k in range(2):
                for j in range(6):
                    o = (6 * k + j) * B
                    mm = pe.matmul(PS[:, 0, o:o + B], wmod[:, k, j * C:(j + 1) * C], scT[:, k, :], start=True, stop=True)
            mm.then_inc(s_modps, 1)
            end_phase(pe, PH_MOD)
            with pe.Fori(0, NG) as g:
                mean_pe(pe, group(X, g), LN_PREP0 + g, 0)
                var_pe(pe, ST_PREP0 + 2 * g, 1)
                var_pe(pe, ST_PREP0 + 2 * g + 1, 1)
            end_phase(pe, PH_PREP0)
            la_tiles(pe, la_pe, True)
            end_phase(pe, PH_ATT0)
            mlp_a_pe(pe, 0)
            with pe.Fori(0, NG - 1) as g:
                mlp_a_pe(pe, g + 1)
                mlp_b_pe(pe, g)
            mlp_b_pe(pe, NG - 1)
            end_phase(pe, PH_MLP)
            with pe.Fori(0, NG) as g:
                mean_pe(pe, group(X, g), LN_MOE + g, 0)
                var_pe(pe, ST_MOE + g, 1)
                moe_router_pe(pe, g)
                moe_up_pe(pe, g, 0)
                moe_up_pe(pe, g, 1)
                moe_weights_pe(pe, g)
                for k in range(ITEMS):
                    moe_down_pe(pe, g, k)
                    if k + 2 < ITEMS:
                        moe_up_pe(pe, g, k + 2)
            end_phase(pe, PH_MOE)
            with pe.Fori(0, NG) as g:
                mean_pe(pe, group(X, g), LN_PREP1 + g, 0)
                var_pe(pe, ST_PREP1 + g, 1)
                pe.wait_ge(n_out, LN_PREP1 + g + 2)
                pe.wait_ge(g_out, g + 1)
                pe.matmul(PS[:, 2, :], wl1[:, 4, :], group(XSF, g), start=True, stop=True).then_inc(g_ps, 1)
            end_phase(pe, PH_PREP1)
            la_tiles(pe, la_pe, False)
            end_phase(pe, PH_ATT1)
            with pe.Fori(0, NG) as g:
                pe.wait_ge(f_x, g + 1)
                pe.matmul(PS[:, 2, :], wl1[:, 3, :], group(H, g), start=True, stop=True).then_inc(f_wo, 1)
                pe.wait_ge(f_x, g + 2)
                mean_pe(pe, group(X, g), LN_WO1 + g, 0)
                var_pe(pe, ST_WO1 + g, 1)
            end_phase(pe, PH_WO1)
            end_phase(pe, PH_ZERO)
            with pe.Fori(0, DEPTH) as l:
                pe.wait_ge(s_wa, 16 * loads_a * (l + 1))
                pe.wait_ge(s_cast, 1)
                tiles(pe, l, att_pe)
                end_phase(pe, PH_LAYERS + 2 * l)
                pe.wait_ge(s_wf, 16 * loads_f * (l + 1))
                groups(pe, l, ff_first_pe, ff_body_pe)
                end_phase(pe, PH_LAYERS + 2 * l + 1)

        @block.scalar
        def _(act):
            act.wait_ge(s_load, 16 * len(loads))
            act.activation(scT[:, :, :], cT[:, :, :], ACT.Silu).then_inc(s_silu, 1)
            act.preload_act_table_set(LOG_EXP)
            end_phase(act, PH_MOD)
            with act.Fori(0, NG) as g:
                act.wait_ge(n_xc, LN_PREP0 + g + 2)
                square_act(act, xc[:, :], ST_PREP0 + 2 * g)
                rsqrt_act(act, ST_PREP0 + 2 * g)
                act.wait_ge(n_out, LN_PREP0 + g + 2)
                square_act(act, group(H, g), ST_PREP0 + 2 * g + 1)
                rsqrt_act(act, ST_PREP0 + 2 * g + 1)
            end_phase(act, PH_PREP0)
            la_tiles(act, la_act, True)
            end_phase(act, PH_ATT0)
            mlp_a_act(act, 0)
            with act.Fori(0, NG - 1) as g:
                mlp_a_act(act, g + 1)
                mlp_b_act(act, g)
            mlp_b_act(act, NG - 1)
            end_phase(act, PH_MLP)
            with act.Fori(0, NG) as g:
                act.wait_ge(n_xc, LN_MOE + g + 2)
                square_act(act, xc[:, :], ST_MOE + g)
                rsqrt_act(act, ST_MOE + g, switch=True)
                act.wait_ge(e_lg, g + 2)
                act.wait_ge(e_sgt, g + 1)
                act.activation(sgT[:, :], PS[0:EXPERTS, 2, :], ACT.Sigmoid).then_inc(e_sg, 1)
                for k in range(ITEMS):
                    moe_act(act, g, k)
            end_phase(act, PH_MOE)
            with act.Fori(0, NG) as g:
                act.wait_ge(n_xc, LN_PREP1 + g + 2)
                square_act(act, xc[:, :], ST_PREP1 + g)
                rsqrt_act(act, ST_PREP1 + g, switch=True)
                act.wait_ge(g_ps, g + 2)
                act.activation(group(H, g), PS[:, 2, :], ACT.Sigmoid, bias=bg1[:, 0:1]).then_inc(g_out, 1)
            act.preload_act_table_set(LOG_EXP)
            end_phase(act, PH_PREP1)
            la_tiles(act, la_act, False)
            end_phase(act, PH_ATT1)
            with act.Fori(0, NG) as g:
                act.wait_ge(n_xc, LN_WO1 + g + 2)
                square_act(act, xc[:, :], ST_WO1 + g)
                rsqrt_act(act, ST_WO1 + g)
            end_phase(act, PH_WO1)
            end_phase(act, PH_ZERO)
            with act.Fori(0, DEPTH) as l:
                act.preload_act_table_set(LOG_EXP)
                tiles(act, l, att_act)
                end_phase(act, PH_LAYERS + 2 * l)
                act.wait_ge(s_wf, 16 * loads_f * (l + 1))
                groups(act, l, ff_first_act, ff_body_act)
                end_phase(act, PH_LAYERS + 2 * l + 1)

        @block.gpsimd
        def _(pool):
            pool.memset(vaug[:, :, :], 0.0).then_inc(s_const, 1)
            pool.wait_ge(s_const, 1)
            pool.memset(vaug[:, :, HD:HD + 1], 1.0).then_inc(s_const, 1)
            end_phase(pool, PH_MOD)
            end_phase(pool, PH_PREP0)
            la_tiles(pool, la_pool, True)
            end_phase(pool, PH_ATT0)
            pool.memset(combT[:, :], 0.0)
            end_phase(pool, PH_MLP)
            end_phase(pool, PH_MOE)
            pool.memset(vaug[:, :, :], 0.0).then_inc(s_const, 1)
            pool.wait_ge(s_const, 4)
            pool.memset(vaug[:, :, HD:HD + 1], 1.0)
            end_phase(pool, PH_PREP1)
            pool.memset(XSA[:, :], 0.0)
            la_tiles(pool, la_pool, False)
            end_phase(pool, PH_ATT1)
            pool.memset(XSF[:, :], 0.0).then_inc(s_const, 1)
            pool.wait_ge(s_const, 6)
            with pool.Fori(0, NG) as g:
                off = xs_off(pool, g)
                wait_apart(pool, n_out, LN_WO1 + g + 2)
                shift_copies(pool, XSA, off, group(H, g), f_xs, g)
            end_phase(pool, PH_WO1)
            pool.memset(kbd[:, :, :, :], 0.0)
            pool.memset(Vbd[:, :, :, :], 0.0).then_inc(s_const, 1)
            pool.wait_ge(s_const, 7)
            pool.memset(Vbd[0:64, :, :, 2 * DH:2 * DH + 1], 1.0)
            pool.memset(Vbd[64:128, :, :, 2 * DH + 1:VB_W], 1.0).then_inc(s_const, 1)
            pool.wait_ge(s_const, 8)
            end_phase(pool, PH_ZERO)
            with pool.Fori(0, DEPTH) as l:
                tiles(pool, l, att_pool)
                end_phase(pool, PH_LAYERS + 2 * l)
                with pool.Fori(0, NG) as g:
                    ff_pool(pool, g, l * NG + g)
                end_phase(pool, PH_LAYERS + 2 * l + 1)

        @block.vector
        def _(dve):
            dve.wait_ge(s_load, 16 * len(loads))
            dve.wait_ge(s_modps, 1)
            for k in range(2):
                ps = PS[:, 0, 6 * B * k:6 * B * (k + 1)].rearrange("p (j b) -> p j b", b=B)
                for j in range(6):
                    if j in (SCALE_A, SCALE_B):
                        dve.tensor_scalar(mod[:, k, j, :], ps[:, j, :], 1.0, None, ALU.add)
                    elif j in (SHIFT_A, SHIFT_B):
                        dve.tensor_copy(mod[:, k, j, :], ps[:, j, :])
                    else:
                        q = 2 * k + (j == GATE_B)
                        dve.tensor_copy(gtmp[:, q, :], ps[:, j, :])
                        dve.tensor_scalar(gsign[:, q, :], ps[:, j, :], 0.0, 2.0, ALU.is_ge, ALU.mult).then_inc(s_mod, 1)
            dve.wait_ge(s_mod, 4)
            dve.scalar_tensor_tensor(gabs[:, :, :], gtmp[:, :, :], -1.0, gtmp[:, :, :], ALU.mult, ALU.max).then_inc(s_mod, 1)
            dve.wait_ge(s_mod, 5)
            dve.tensor_scalar(gtmp[:, :, :], gabs[:, :, :], 0.25, None, ALU.max).then_inc(s_mod, 1)
            dve.wait_ge(s_mod, 6)
            for k in range(2):
                for j in (GATE_A, GATE_B):
                    q = 2 * k + (j == GATE_B)
                    dve.scalar_tensor_tensor(mod[:, k, j, :], gsign[:, q, :], -1.0, gtmp[:, q, :], ALU.add, ALU.mult)
            end_phase(dve, PH_MOD)
            with dve.Fori(0, NG) as g:
                u, su = LN_PREP0 + g, ST_PREP0 + 2 * g
                centre_dve(dve, group(X, g), u, su, 0)
                eps_dve(dve, su, 1, 1e-5)
                affine_dve(dve, group(H, g), u, su, modcol(0, SCALE_A, g), modcol(0, SHIFT_A, g))
                eps_dve(dve, su + 1, 1, 1e-6)
                dve.wait_ge(n_r, su + 3)
                dve.scalar_tensor_tensor(group(XSF, g), group(H, g), cols0[:, 1:2], rs[:, :], ALU.mult, ALU.mult).then_inc(n_used, 1)
            end_phase(dve, PH_PREP0)
            dve.memset(state[:, :, :, :], 0.0).then_inc(s_const, 1)
            dve.wait_ge(s_const, 3)
            la_tiles(dve, la_dve, True)
            end_phase(dve, PH_ATT0)
            mlp_a_dve(dve, 0)
            with dve.Fori(0, NG - 1) as g:
                mlp_a_dve(dve, g + 1)
                mlp_b_dve(dve, g)
            mlp_b_dve(dve, NG - 1)
            end_phase(dve, PH_MLP)
            with dve.Fori(0, NG) as g:
                u, su = LN_MOE + g, ST_MOE + g
                centre_dve(dve, group(X, g), u, su, 0)
                eps_dve(dve, su, 1, 1e-5)
                dve.wait_ge(e_y, 1)
                affine_dve(dve, hin[:, ds(g % 2, 1), :], u, su, modcol(0, SCALE_B, g), modcol(0, SHIFT_B, g))
                moe_route_dve(dve, g)
                for k in range(ITEMS):
                    moe_mul_dve(dve, g, k)
                dve.wait_ge(e_down, ITEMS * (g + 1) + 1)
                dve.scalar_tensor_tensor(group(X, g), PS[:, 7, :], modcol(0, GATE_B, g), group(X, g),
                                         ALU.mult, ALU.add).then_inc(e_x, 1)
            end_phase(dve, PH_MOE)
            with dve.Fori(0, NG) as g:
                u, su = LN_PREP1 + g, ST_PREP1 + g
                centre_dve(dve, group(X, g), u, su, 0)
                eps_dve(dve, su, 1, 1e-5)
                affine_dve(dve, group(XSF, g), u, su, modcol(1, SCALE_A, g), modcol(1, SHIFT_A, g))
            end_phase(dve, PH_PREP1)
            dve.memset(state[:, :, :, :], 0.0).then_inc(s_const, 1)
            dve.wait_ge(s_const, 5)
            la_tiles(dve, la_dve, False)
            end_phase(dve, PH_ATT1)
            with dve.Fori(0, NG) as g:
                u, su = LN_WO1 + g, ST_WO1 + g
                dve.wait_ge(f_wo, g + 2)
                dve.scalar_tensor_tensor(group(X, g), PS[:, 2, :], modcol(1, GATE_A, g), group(X, g),
                                         ALU.mult, ALU.add).then_inc(f_x, 1)
                dve.wait_ge(f_x, g + 2)
                centre_dve(dve, group(X, g), u, su, 0)
                eps_dve(dve, su, 1, 1e-5)
                affine_dve(dve, group(H, g), u, su, modcol(1, SCALE_B, g), modcol(1, SHIFT_B, g))
            end_phase(dve, PH_WO1)
            end_phase(dve, PH_ZERO)
            dve.wait_ge(s_load2, 16 * len(late_loads))
            dve.tensor_copy(identh[:, :], ident[:, :])
            dve.tensor_copy(wmask[:, :, :], wmask32[:, :, 0:GW]).then_inc(s_cast, 1)
            dve.wait_ge(s_cast, 1)
            with dve.Fori(0, DEPTH) as l:
                rope_dve(dve, l)
                tiles(dve, l, att_dve)
                end_phase(dve, PH_LAYERS + 2 * l)
                dve.wait_ge(s_wf, 16 * loads_f * (l + 1))
                groups(dve, l, ff_first_dve, ff_body_dve)
                end_phase(dve, PH_LAYERS + 2 * l + 1)
            with dve.Fori(0, NG) as g:
                dve.scalar_tensor_tensor(group(X, g), group(H, g), modcol(1, GATE_B, g), group(X, g),
                                         ALU.mult, ALU.add).then_inc(f_x, 1)


def constants():
    import numpy as np
    f = np.float32
    k = {"ident": np.eye(P, dtype=f)}
    k["onesm"] = np.full((P, P), 1.0 / P, f)
    rows = np.arange(P)
    k["hmask"] = (rows[:, None] // HD == np.arange(HEADS)[None]).astype(f)
    k["hold"] = np.broadcast_to((np.arange(TPB) < TPB - 1)[None], (P, TPB)).astype(f)
    k["hm9"] = np.broadcast_to(np.tile(k["hmask"], (1, 2))[:, :, None], (P, 2 * HEADS, HD + 1)).astype(f)
    causal = (rows[None, :] >= rows[:, None])
    diff = (rows[None, :] - rows[:, None]) * (np.pi / 2 / L)
    k["cmask"] = np.stack([np.where(causal, np.cos(diff), 0.0), causal], 1).astype(f)
    angle = np.arange(L) * (np.pi / 2 / L)
    cs = np.stack([np.cos(angle), np.sin(angle)])
    k["crow"] = cs.astype(f)
    k["ccol"] = np.ascontiguousarray(cs.reshape(2, TPB, P).transpose(2, 0, 1)).astype(f)
    k["esel"] = np.zeros((P, EXPERTS, P), f)
    for e in range(EXPERTS):
        k["esel"][e, e, :] = 1
    e = np.arange(EXPERTS)
    k["low"] = np.broadcast_to((e[None, :] < e[:, None])[None], (P, EXPERTS, EXPERTS)).astype(f)
    half = np.arange(0, DH, 2)
    freq = np.arange(L)[:, None] / 10000.0 ** (half / DH)[None]
    freq = np.concatenate([freq, freq], 1)
    base = (half + 0.4 * DH) / (1.4 * DH)
    scale = base[None] ** ((np.arange(L) - L // 2) / (WIN // 2))[:, None]
    scale = np.concatenate([scale, scale], 1)
    sign = np.where(np.arange(DH) < DH // 2, -1.0, 1.0)[None]
    scale_q = scale * QK_SCALE
    t = np.stack([np.concatenate([np.cos(freq) * scale_q, np.cos(freq) / scale], 1),
                  np.concatenate([np.sin(freq) * scale_q * sign, np.sin(freq) / scale * sign], 1)])
    k["rope"] = np.ascontiguousarray(t.reshape(2, TPB, P, 2 * DH).transpose(2, 0, 1, 3)).astype(f)
    q, j = rows[:, None] % WIN, np.arange(KEYS)[None]
    seen = (j >= q) & (j <= q + WIN)
    first = seen & ~((rows[:, None] < WIN) & (j < WIN))
    m = np.stack([first, seen], 1)
    k["wmask"] = np.where(np.tile(m, (1, 1, GW // KEYS)), 0.0, NEG).astype(f)
    return k


def kernel(**inputs):
    import numpy as np
    import concourse.bacc as bacc
    from concourse import mybir as mb
    from concourse.bass_utils import run_bass_kernel_spmd as run

    x = {k: np.asarray(v) for k, v in inputs.items()}

    def lay(v):
        return np.ascontiguousarray(v)

    def col(*vs):
        return lay(np.stack(vs, -1))

    L0, F0, A1, F1 = "L0_attn_", "L0_ffn_", "L1_attn_", "L1_ffn_"
    arr = {
        "xT": lay(x[L0 + "x"].reshape(N, C).T),
        "cT": lay(np.stack([x["L0_c"].T, x["L1_c"].T], 1)),
        "wmod": lay(np.stack([x["L0_wmod"], x["L1_wmod"]], 1)),
        "qkv_w": x[L0 + "qkv_w"],
        "bqk0": col(x[L0 + "qkv_b"][0:C], x[L0 + "qkv_b"][C:2 * C]),
        "bkv0": lay(x[L0 + "qkv_b"][C:3 * C].reshape(1, 2 * C)),
        "out_w": x[L0 + "out_w"],
        "cols0": col(x[L0 + "out_b"], x[L0 + "norm1_w"], x[L0 + "norm2_w"], x[L0 + "mlp_b2"],
                     *x[L0 + "mlp_b1"].reshape(F_MLP, P)),
        "mlp_w1": x[L0 + "mlp_w1"],
        "mlp_w2": lay(x[L0 + "mlp_w2"].reshape(F_MLP, P, C).transpose(1, 0, 2)),
        "router_wT": lay(x[F0 + "router_w"].T),
        "router_bias": lay(x[F0 + "router_bias"].reshape(1, EXPERTS)),
        "sw1": x[F0 + "sw1"], "sw3": x[F0 + "sw3"],
        "sw2": lay(x[F0 + "sw2"].reshape(SHARED, P, C).transpose(1, 0, 2)),
        "ew1": lay(x[F0 + "ew1"].transpose(1, 0, 2)),
        "ew2": lay(x[F0 + "ew2"].transpose(1, 0, 2)),
        "wl1": lay(np.stack([x[A1 + w].T for w in ("Wq", "Wk", "Wv", "Wo", "Wg")], 1)),
        "bg1": lay(x[A1 + "bg"].reshape(C, 1)),
        "Wqkv": x[F1 + "Wqkv"],
        "Wo": lay(x[F1 + "Wo"].reshape(DEPTH, PAIRS, P, C).transpose(0, 2, 1, 3)),
        "qks": lay(np.stack([x[F1 + "q_scale"], x[F1 + "k_scale"]], 1)),
        "W1": x[F1 + "W1"],
        "lncol": col(x[F1 + "ln_g"], x[F1 + "ln_b"]),
        "b2col": lay(x[F1 + "b2"].reshape(DEPTH, C, 1)),
    }
    w2 = np.zeros((DEPTH, 3, P, C), np.float32)
    b1 = np.zeros((DEPTH, P, 6), np.float32)
    for c, (c0, m) in enumerate(CH):
        w2[:, c, 0:m] = x[F1 + "W2"][:, c0:c0 + m]
        b1[:, 0:m, c] = x[F1 + "b1"][:, c0:c0 + m]
        b1[:, 0:m, 3 + c] = x[F1 + "b1"][:, DIN + c0:DIN + c0 + m]
    arr["W2"] = lay(w2.transpose(0, 2, 1, 3))
    arr["b1col"] = b1
    arr.update(constants())

    nc = bacc.Bacc("TRN2", target_bir_lowering=False, num_devices=1)
    aps = {k: nc.dram_tensor(f"in_{k}", v.shape, mb.dt.from_np(v.dtype), kind="ExternalInput").ap() for k, v in arr.items()}
    out = nc.dram_tensor("out_xT", (C, N), F32, kind="ExternalOutput").ap()
    build(nc, aps, out)
    r = run(nc, [{f"in_{k}": v for k, v in arr.items()}], core_ids=[0])
    return np.ascontiguousarray(r.results[0]["out_xT"].T).reshape(B, L, C)
```

```python
from contextlib import ExitStack

import concourse.bass as bass
from concourse import mybir

F32 = mybir.dt.float32
BF16 = mybir.dt.bfloat16
ALU = mybir.AluOpType
ACT = mybir.ActivationFunctionType
AX = mybir.AxisListType
ds = bass.ds

P = 128
B, L, C = 4, 1024, 128
N = B * L
TPB = L // P
NT = N // P
GW = 512
NG = N // GW
GPB = L // GW
HEADS = 16
HD = C // HEADS
VW = 32
F_MLP = 4 * C // P
EXPERTS = 8
SHARED = 256 // P
DEPTH = 6
DH = 64
INNER = HEADS * DH
PAIRS = HEADS // 2
WIN = 32
NWIN = P // WIN
KEYS = 2 * WIN
HALO = WIN
DIN = int(C * 4 * 2 / 3)
CH = [(0, 128), (128, 128), (256, DIN - 256)]
XSW = HALO + L + 4
QK_SCALE = 8.0
NEG = -3.0e38
LOG_EXP = "natural_log_exp_and_others"
GELU, GELU_TANH = "gelu_and_others", "gelu_apprx_tanh_and_others"


def build(nc, a, out):
    ctx = ExitStack()
    with ctx:
        def sb(name, shape, dt=F32, scope=ctx):
            return scope.enter_context(nc.sbuf_tensor(name, shape, dt))

        primed = []

        def sem(name):
            return ctx.enter_context(nc.semaphore(name))

        def step(name):
            primed.append(sem(name))
            return primed[-1]

        X = sb("X", [P, N])
        H = sb("H", [P, N])
        XSA = sb("XSA", [P, B * XSW])
        XSF = sb("XSF", [P, B * XSW])
        Wqkv = sb("Wqkv", [P, 3 * INNER])
        Wo6 = sb("Wo6", [P, PAIRS, C])
        W1 = sb("W1", [P, 2 * DIN])
        W2 = sb("W2", [P, 3, C])
        lncol = sb("lncol", [P, 2])
        b1col = sb("b1col", [P, 6])
        qks = sb("qks", [P, 2, DH])
        b2col = sb("b2col", [P, 1])
        ident = sb("ident", [P, P])
        onesm = sb("onesm", [P, P])
        mod = sb("mod", [P, 2, 6, B])
        xc = sb("xc", [P, GW])
        sq = sb("sq", [P, GW])
        ve = sb("ve", [P, GW])
        rs = sb("rs", [P, GW])
        xn = sb("xn", [P, GW])

        early = ExitStack()
        wq0 = sb("wq0", [P, 3 * C], scope=early)
        bqk0 = sb("bqk0", [P, 2], scope=early)
        bkv0 = sb("bkv0", [P, 2 * C], scope=early)
        wo0 = sb("wo0", [P, C], scope=early)
        cols0 = sb("cols0", [P, 4 + F_MLP], scope=early)
        mw1 = sb("mw1", [P, 4 * C], scope=early)
        mw2 = sb("mw2", [P, F_MLP, C], scope=early)
        wr = sb("wr", [P, EXPERTS], scope=early)
        rbias = sb("rbias", [P, EXPERTS], scope=early)
        sw1 = sb("sw1", [P, SHARED * P], scope=early)
        sw3 = sb("sw3", [P, SHARED * P], scope=early)
        sw2 = sb("sw2", [P, SHARED, C], scope=early)
        ew1 = sb("ew1", [P, EXPERTS, P], scope=early)
        ew2 = sb("ew2", [P, EXPERTS, P], scope=early)
        wl1 = sb("wl1", [P, 5, C], scope=early)
        bg1 = sb("bg1", [P, 1], scope=early)
        cT = sb("cT", [P, 2, B], scope=early)
        scT = sb("scT", [P, 2, B], scope=early)
        wmod = sb("wmod", [P, 2, 6 * C], scope=early)
        gtmp = sb("gtmp", [P, 4, B], scope=early)
        gsign = sb("gsign", [P, 4, B], scope=early)
        gabs = sb("gabs", [P, 4, B], scope=early)
        hmask = sb("hmask", [P, HEADS], scope=early)
        cmask = sb("cmask", [P, 2, P], scope=early)
        crow = sb("crow", [P, 2, L], scope=early)
        ccol = sb("ccol", [P, 2, TPB], scope=early)
        hold = sb("hold", [P, TPB], scope=early)
        hm9 = sb("hm9", [P, 2 * HEADS, HD + 1], scope=early)
        esel = sb("esel", [P, EXPERTS, P], scope=early)
        low = sb("low", [P, EXPERTS, EXPERTS], scope=early)
        attn = ExitStack()
        ht = sb("ht", [P, P], scope=attn)
        qf = sb("qf", [P, P], scope=attn)
        kf = sb("kf", [P, P], scope=attn)
        qcs = sb("qcs", [P, 2, P], scope=attn)
        Qbd = sb("Qbd", [P, HEADS, P], scope=attn)
        Pm = sb("Pm", [P, HEADS, P], scope=attn)
        ktok = sb("ktok", [P, 2, P], scope=attn)
        vaug = sb("vaug", [P, HEADS, VW], scope=attn)
        state = sb("state", [P, 2, HEADS, VW], scope=attn)
        stnew = sb("stnew", [P, 2, HEADS, HD + 1], scope=attn)
        oT = sb("oT", [P, 4, P], scope=attn)
        nrm = sb("nrm", [P, HEADS], scope=attn)
        rec = sb("rec", [P, HEADS], scope=attn)
        ctxt = sb("ctxt", [P, P], scope=attn)
        spa = sb("spa", [P, 3, P], scope=attn)
        spe = sb("spe", [P, 3, P], scope=attn)
        spl = sb("spl", [P, 3, P], scope=attn)
        qsp = sb("qsp", [P, P], scope=attn)
        attn.close()
        dense = ExitStack()
        hin = sb("hin", [P, 2, GW], scope=dense)
        hidm = sb("hidm", [P, F_MLP, GW], scope=dense)
        hid = sb("hid", [P, 2, GW], scope=dense)
        hid2 = sb("hid2", [P, 2, GW], scope=dense)
        sg = sb("sg", [P, 4, EXPERTS], scope=dense)
        sel = sb("sel", [P, 4, EXPERTS], scope=dense)
        above = sb("above", [P, 4, EXPERTS, EXPERTS], scope=dense)
        level = sb("level", [P, 4, EXPERTS, EXPERTS], scope=dense)
        rank = sb("rank", [P, 4, EXPERTS], scope=dense)
        ssel = sb("ssel", [P, 4, EXPERTS], scope=dense)
        den = sb("den", [P, 5, 4], scope=dense)
        comb = sb("comb", [P, 4, EXPERTS], scope=dense)
        selm = sb("selm", [P, 4, EXPERTS], scope=dense)
        gsel = sb("gsel", [P, 4, EXPERTS], scope=dense)
        gelse = sb("gelse", [P, 4, EXPERTS], scope=dense)
        sgT = sb("sgT", [EXPERTS, GW], scope=dense)
        combT = sb("combT", [P, GW], scope=dense)
        dense.close()
        early.close()

        late = ExitStack()
        rope = sb("rope", [P, 2, TPB, 2 * DH], scope=late)
        ropel = sb("ropel", [P, 2, TPB, 2 * DH], scope=late)
        wmask = sb("wmask", [P, 2, GW], BF16, scope=late)
        identh = sb("identh", [P, P], BF16, scope=late)
        kbd = sb("kbd", [P, PAIRS, 2, HALO + P], scope=late)
        Vbd = sb("Vbd", [P, NWIN, PAIRS, 2 * DH], scope=late)
        work = ExitStack()
        xt = sb("xt", [P, P], scope=work)
        xv = sb("xv", [P, P], scope=work)
        sqk = sb("sqk", [P, 2, INNER], scope=work)
        ss = sb("ss", [P, 2, HEADS], scope=work)
        ssm = sb("ssm", [P, 2, HEADS], scope=work)
        rqk = sb("rqk", [P, 2, HEADS], scope=work)
        qkn = sb("qkn", [P, 2, INNER], scope=work)
        m1 = sb("m1", [P, 2, INNER], scope=work)
        m2 = sb("m2", [P, 2, INNER], scope=work)
        qT = sb("qT", [P, PAIRS, P], scope=work)
        smax = sb("smax", [P, HEADS], scope=work)
        ssub = sb("ssub", [P, INNER], scope=work)
        pE = sb("pE", [P, INNER], scope=work)
        pT = sb("pT", [P, PAIRS, P], scope=work)
        vst = sb("vst", [P, INNER], scope=work)
        psums = sb("psums", [P, HEADS], scope=work)
        orec = sb("orec", [P, HEADS], scope=work)
        On = sb("On", [P, INNER], scope=work)
        OTs = sb("OTs", [P, PAIRS, P], scope=work)
        rot = m1
        work.close()
        ffn = ExitStack()
        fx = sb("fx", [P, 2, GW], scope=ffn)
        gl = sb("gl", [P, 3, GW], scope=ffn)
        hg = sb("hg", [P, 3, GW], scope=ffn)
        ffn.close()
        late.close()

        PS = ctx.enter_context(nc.psum_tensor("PS", [P, 8, GW], F32))

        s_first = sem("s_first")
        s_load = sem("s_load")
        s_load2 = sem("s_load2")
        s_wa = sem("s_wa")
        s_wf = sem("s_wf")
        s_out = sem("s_out")
        s_const = sem("s_const")
        s_phase = sem("s_phase")
        s_apart = sem("s_apart")
        s_cast = sem("s_cast")
        s_silu = sem("s_silu")
        s_modps = sem("s_modps")
        s_mod = sem("s_mod")
        n_mean, n_xc, n_sq, n_var = step("n_mean"), step("n_xc"), step("n_sq"), step("n_var")
        n_ve, n_ln, n_r, n_used, n_out = step("n_ve"), step("n_ln"), step("n_r"), step("n_used"), step("n_out")
        a_ht, a_qk, a_qf, a_kf = step("a_ht"), step("a_qk"), step("a_qf"), step("a_kf")
        a_abs, a_exp, a_ln, a_qsp = sem("a_abs"), step("a_exp"), step("a_ln"), step("a_qsp")
        a_kv, a_ktok, a_v, a_qcs = step("a_kv"), step("a_ktok"), step("a_v"), step("a_qcs")
        a_bd, a_bdp, a_s, a_pm = step("a_bd"), step("a_bdp"), step("a_s"), step("a_pm")
        a_in, a_o = step("a_in"), step("a_o")
        a_oc, a_ot, a_nrm, a_rec = step("a_oc"), step("a_ot"), step("a_nrm"), step("a_rec")
        a_ctx, a_ct, a_st, a_stm = step("a_ctx"), step("a_ct"), step("a_st"), step("a_stm")
        a_state, a_done = step("a_state"), step("a_done")
        d_wo, d_h, d_up, d_act = step("d_wo"), step("d_h"), step("d_up"), step("d_act")
        d_y, d_h2, d_x = step("d_y"), step("d_h2"), step("d_x")
        e_lg, e_sg, e_sgt, e_s, e_dve = step("e_lg"), step("e_sg"), step("e_sgt"), step("e_s"), step("e_dve")
        e_comb, e_cT, e_cTs = step("e_comb"), step("e_cT"), step("e_cTs")
        e_u, e_act, e_mul, e_down, e_x = (step("e_u"), step("e_act"), step("e_mul"), step("e_down"),
                                          step("e_x"))
        g_ps, g_out = step("g_ps"), step("g_out")
        f_wo, f_x, f_xs = step("f_wo"), step("f_x"), step("f_xs")
        t_rope, t_xt, t_xv, t_q, t_k = step("t_rope"), step("t_xt"), step("t_xv"), step("t_q"), step("t_k")
        t_sqq, t_sqk, t_red, t_sm = step("t_sqq"), step("t_sqk"), step("t_red"), step("t_sm")
        t_ln, t_root, t_nq, t_nk = step("t_ln"), step("t_root"), step("t_nq"), step("t_nk")
        t_mq, t_mk, t_rotq, t_rotk = step("t_mq"), step("t_mk"), step("t_rotq"), step("t_rotk")
        t_v, t_vs, t_vlast, t_sum = step("t_v"), step("t_vs"), step("t_vlast"), step("t_sum")
        t_vc, t_vcp, t_vcd = step("t_vc"), step("t_vcp"), step("t_vcd")
        t_qT, t_kT, t_qTc, t_kTc, t_halo = (step("t_qT"), step("t_kT"), step("t_qTc"), step("t_kTc"),
                                            step("t_halo"))
        t_s, t_max, t_sub, t_exp = step("t_s"), step("t_max"), step("t_sub"), step("t_exp")
        t_pT, t_pTc, t_o, t_orec, t_on = (step("t_pT"), step("t_pTc"), step("t_o"), step("t_orec"),
                                          step("t_on"))
        t_oT, t_oTc, t_y, t_h, t_xs = step("t_oT"), step("t_oTc"), step("t_y"), step("t_h"), step("t_xs")
        h_u, h_act, h_hg, h_y, h_h, h_xs = (step("h_u"), step("h_act"), step("h_hg"), step("h_y"),
                                            step("h_h"), step("h_xs"))

        first_loads = [
            (cT[:, :, :], a["cT"]), (wmod[:, :, :], a["wmod"]), (onesm[:, :], a["onesm"]),
            (X[:, :], a["xT"]),
        ]
        loads = [
            (ident[:, :], a["ident"]),
            (wq0[:, :], a["qkv_w"]), (bqk0[:, :], a["bqk0"]), (bkv0[:, :], a["bkv0"].broadcast_to([P, 2 * C])),
            (wo0[:, :], a["out_w"]), (cols0[:, :], a["cols0"]), (hmask[:, :], a["hmask"]), (hold[:, :], a["hold"]),
            (hm9[:, :, :], a["hm9"]),
            (cmask[:, :, :], a["cmask"]), (ccol[:, :, :], a["ccol"]),
            (crow[:, :, :], a["crow"].unsqueeze(0).broadcast_to([P, 2, L])),
            (mw1[:, :], a["mlp_w1"]), (mw2[:, :, :], a["mlp_w2"]),
            (wr[:, :], a["router_wT"]), (rbias[:, :], a["router_bias"].broadcast_to([P, EXPERTS])),
            (sw1[:, :], a["sw1"]), (sw3[:, :], a["sw3"]), (sw2[:, :, :], a["sw2"]),
            (ew1[:, :, :], a["ew1"]), (ew2[:, :, :], a["ew2"]), (wl1[:, :, :], a["wl1"]),
            (bg1[:, :], a["bg1"]), (esel[:, :, :], a["esel"]), (low[:, :, :], a["low"]),
        ]
        wmask32 = m1
        late_loads = [(rope[:, :, :, :], a["rope"]), (wmask32[:, :, 0:GW], a["wmask"])]
        loads_a = 3
        loads_f = 5

        def load_attention(sp, l):
            sp.dma_start(Wqkv[:, :], a["Wqkv"][ds(l, 1), :, :].rearrange("o p n -> (o p) n")).then_inc(s_wa, 16)
            sp.dma_start(Wo6[:, :, :], a["Wo"][ds(l, 1), :, :, :].rearrange("o p c n -> (o p) c n")).then_inc(s_wa, 16)
            sp.dma_start(qks[:, :, :], a["qks"][ds(l, 1), :, :].broadcast_to([P, 2, DH])).then_inc(s_wa, 16)

        def load_ffn(sp, l):
            sp.dma_start(W1[:, :], a["W1"][ds(l, 1), :, :].rearrange("o p n -> (o p) n")).then_inc(s_wf, 16)
            sp.dma_start(W2[:, :, :], a["W2"][ds(l, 1), :, :, :].rearrange("o p c n -> (o p) c n")).then_inc(s_wf, 16)
            sp.dma_start(lncol[:, :], a["lncol"][ds(l, 1), :, :].rearrange("o p n -> (o p) n")).then_inc(s_wf, 16)
            sp.dma_start(b1col[:, :], a["b1col"][ds(l, 1), :, :].rearrange("o p n -> (o p) n")).then_inc(s_wf, 16)
            sp.dma_start(b2col[:, :], a["b2col"][ds(l, 1), :, :].rearrange("o p n -> (o p) n")).then_inc(s_wf, 16)

        def wait_apart(eng, semaphore, value):
            eng.wait_ge(semaphore, value)
            eng.sem_inc(s_apart, 1)

        def end_phase(eng, n):
            eng.drain().then_inc(s_phase, 1)
            wait_apart(eng, s_phase, 4 * n + 4)

        PH_MOD, PH_PREP0, PH_ATT0, PH_MLP, PH_MOE, PH_PREP1, PH_ATT1, PH_WO1, PH_ZERO = range(9)
        PH_LAYERS = 9
        PH_FIN = PH_LAYERS + 2 * DEPTH

        LN_PREP0, ST_PREP0 = 0, 0
        LN_MLP, ST_MLP = NG, 2 * NG
        LN_MOE, ST_MOE = NG, 3 * NG
        LN_PREP1, ST_PREP1 = 2 * NG, 4 * NG
        LN_WO1, ST_WO1 = 3 * NG, 5 * NG
        LN_FFN, ST_FFN = 4 * NG, 6 * NG

        def mean_pe(pe, src, u, bank):
            pe.wait_ge(n_xc, u + 1)
            pe.matmul(PS[:, bank, :], onesm[:, :], src, start=True, stop=True).then_inc(n_mean, 1)

        def centre_dve(dve, src, u, su, bank):
            dve.wait_ge(n_mean, u + 2)
            dve.wait_ge(n_used, su + 1)
            dve.tensor_tensor(xc[:, :], src, PS[:, bank, :], ALU.subtract).then_inc(n_xc, 1)

        def square_act(act, src, su):
            act.wait_ge(n_var, su + 1)
            act.activation(sq[:, :], src, ACT.Square).then_inc(n_sq, 1)

        def var_pe(pe, su, bank):
            pe.wait_ge(n_sq, su + 2)
            pe.wait_ge(n_ve, su + 1)
            pe.matmul(PS[:, bank, :], onesm[:, :], sq[:, :], start=True, stop=True).then_inc(n_var, 1)

        def eps_dve(dve, su, bank, eps):
            dve.wait_ge(n_var, su + 2)
            dve.wait_ge(n_r, su + 1)
            dve.tensor_scalar(ve[:, :], PS[:, bank, :], eps, None, ALU.add).then_inc(n_ve, 1)

        def rsqrt_act(act, su, switch=False):
            if switch:
                act.preload_act_table_set(LOG_EXP)
            act.wait_ge(n_ve, su + 2)
            act.wait_ge(n_used, su + 1)
            act.activation(rs[:, :], ve[:, :], ACT.Ln).then_inc(n_ln, 1)
            act.wait_ge(n_ln, su + 2)
            act.activation(rs[:, :], rs[:, :], ACT.Exp, scale=-0.5).then_inc(n_r, 1)

        def affine_dve(dve, dst, u, su, scale, shift):
            dve.wait_ge(n_r, su + 2)
            dve.wait_ge(n_out, u + 1)
            dve.tensor_tensor(xn[:, :], xc[:, :], rs[:, :], ALU.mult).then_inc(n_used, 1)
            dve.wait_ge(n_used, su + 2)
            dve.tensor_scalar(dst, xn[:, :], scale, shift, ALU.mult, ALU.add).then_inc(n_out, 1)

        def group(t, g):
            return t[:, ds(g * GW, GW)]

        def xs_group(t, g, shift=0):
            return (g // GPB) * XSW + (g % GPB) * GW + (HALO + shift)

        def modcol(block, which, g):
            return mod[:, block, which, ds(g // GPB, 1)]

        SHIFT_A, SCALE_A, GATE_A, SHIFT_B, SCALE_B, GATE_B = range(6)

        def la_project_pe(pe, i, n, cosine):
            pe.wait_ge(a_ht, n + 2)
            wq, wk = (wq0[:, 0:C], wq0[:, C:2 * C]) if cosine else (wl1[:, 0, :], wl1[:, 1, :])
            pe.matmul(PS[:, 0, 0:P], wq, ht[:, :], start=True, stop=True)
            pe.matmul(PS[:, 0, P:2 * P], wk, ht[:, :], start=True, stop=True).then_inc(a_qk, 1)
            pe.wait_ge(a_v, n + 1)
            pe.wait_ge(a_ktok, n + 1)
            if cosine:
                pe.matmul(PS[:, 1, 0:2 * C], onesm[:, :], bkv0[:, :], start=True, stop=False)
                pe.matmul(PS[:, 1, 0:2 * C], ht[:, :], wq0[:, C:3 * C], start=False, stop=True).then_inc(a_kv, 1)
            else:
                pe.matmul(PS[:, 1, 0:2 * C], ht[:, :], wl1[:, 1:3, :].rearrange("p a c -> p (a c)"),
                          start=True, stop=True).then_inc(a_kv, 1)

        def la_scores_pe(pe, i, n, older):
            pe.wait_ge(a_kf, n + 2)
            pe.wait_ge(a_qf, n + 2)
            pe.wait_ge(a_bd, n + 2)
            pe.wait_ge(a_stm, n + 1)
            for q in range(4):
                if q == 1 and older:
                    pe.wait_ge(a_done, n - 2 + 2)
                if q == 2:
                    pe.wait_ge(a_bdp, n + 2)
                pe.matmul(PS[:, 2 + q, :], kf[:, :], Qbd[:, 4 * q:4 * q + 4, :].rearrange("p h t -> p (h t)"),
                          start=True, stop=True).then_inc(a_s, 1)

        def la_earlier_pe(pe, i, n, kinds):
            pe.wait_ge(a_oc, n + 1)
            pe.wait_ge(a_state, n + 1)
            pe.wait_ge(a_qcs, n + 2)
            for q in range(4):
                for c in range(kinds):
                    mm = pe.matmul(PS[:, 6, q * P:(q + 1) * P],
                                   state[:, c, 4 * q:4 * q + 4, :].rearrange("p h v -> p (h v)"),
                                   qcs[:, c, :], start=(q == 0 and c == 0), stop=False, skip_group_check=True)
            mm.then_inc(a_in, 1)

        def la_own_pe(pe, i, n, kinds):
            w = HEADS * (HD + 1)
            pe.wait_ge(a_v, n + 2)
            pe.wait_ge(a_pm, 4 * n + 5)
            for h in range(HEADS):
                r = VW * (h % 4)
                mm = pe.matmul(PS[r:r + VW, 6, (h // 4) * P:(h // 4 + 1) * P], vaug[:, h, :], Pm[:, h, :],
                               start=False, stop=(h == HEADS - 1), skip_group_check=True)
            mm.then_inc(a_o, 1)
            pe.wait_ge(a_ktok, n + 2)
            for c in range(kinds):
                mm = pe.matmul(PS[:, 2, c * w:(c + 1) * w], ktok[:, c, :], vaug[:, :, 0:HD + 1], start=True, stop=True)
            mm.then_inc(a_st, 1)

        def la_otok_pe(pe, i, n):
            pe.wait_ge(a_oc, n + 2)
            pe.wait_ge(a_ctx, n + 1)
            for q in range(4):
                mm = pe.transpose(PS[:, 7, q * P:(q + 1) * P], oT[:, q, :], ident[:, :])
            mm.then_inc(a_ot, 1)

        def la_ctx_pe(pe, i, n, newer):
            pe.wait_ge(a_ctx, n + 2)
            if newer:
                pe.wait_ge(a_pm, 4 * (n + 1) + 3)
            pe.transpose(PS[:, 3, 0:P], ctxt[:, :], ident[:, :]).then_inc(a_ct, 1)

        def la_pe(pe, i, n, A, B_, C_, cosine):
            kinds = 2 if cosine else 1
            if B_:
                la_scores_pe(pe, i - 1, n - 1, C_)
            if C_:
                la_otok_pe(pe, i - 2, n - 2)
            if A:
                la_project_pe(pe, i, n, cosine)
            if B_:
                la_earlier_pe(pe, i - 1, n - 1, kinds)
            if C_:
                la_ctx_pe(pe, i - 2, n - 2, B_)
            if B_:
                la_own_pe(pe, i - 1, n - 1, kinds)

        def la_act(act, i, n, A, B_, C_, cosine):
            if A:
                act.wait_ge(a_kv, n + 1)
                act.activation(ht[:, :], XSF[:, ds(i * P, P)], ACT.Copy).then_inc(a_ht, 1)
                act.wait_ge(a_qk, n + 2)
            if A and cosine:
                act.wait_ge(a_bd, n + 1)
                act.wait_ge(a_bdp, n + 1)
                act.wait_ge(a_qcs, n + 1)
                act.activation(qf[:, :], PS[:, 0, 0:P], ACT.Relu, bias=bqk0[:, 0:1]).then_inc(a_qf, 1)
                act.wait_ge(a_s, 4 * n + 1)
                act.activation(kf[:, :], PS[:, 0, P:2 * P], ACT.Relu, bias=bqk0[:, 1:2]).then_inc(a_kf, 1)
            elif A:
                act.wait_ge(a_exp, n - NT + 1)
                act.activation(spa[:, 0:2, :].rearrange("p a t -> p (a t)"), PS[:, 0, 0:2 * P], ACT.Abs).then_inc(a_abs, 1)
                act.wait_ge(a_kv, n + 2)
                act.activation(spa[:, 2, :], PS[:, 1, 0:P], ACT.Abs).then_inc(a_abs, 1)
                act.wait_ge(a_abs, 2 * i + 2)
                act.wait_ge(a_ln, n - NT + 1)
                act.activation(spe[:, :, :], spa[:, :, :], ACT.Exp, scale=-1.0).then_inc(a_exp, 1)
                act.wait_ge(a_exp, i + 2)
                act.wait_ge(a_ktok, n + 1)
                act.activation(spl[:, :, :], spe[:, :, :], ACT.Ln, bias=1.0).then_inc(a_ln, 1)
            if C_:
                act.wait_ge(a_ct, n - 2 + 2)
                dst = XSA if cosine else H
                act.activation(dst[:, ds((i - 2) * P, P)], PS[:, 3, 0:P], ACT.Copy).then_inc(a_done, 1)
            if B_:
                act.wait_ge(a_o, n - 1 + 2)
                act.wait_ge(a_ot, n - 1 + 1)
                act.activation(oT[:, :, :].rearrange("p a t -> p (a t)"), PS[:, 6, :], ACT.Copy).then_inc(a_oc, 1)

        HALF = HEADS // 2

        def la_pool(pool, i, n, A, B_, C_, cosine):
            if A:
                pool.wait_ge(a_qf, n + 2)
                wait_apart(pool, a_s, 4 * n + 1)
                for h in range(HALF, HEADS):
                    ins = pool.tensor_scalar(Qbd[:, h, :], qf[:, :], hmask[:, h:h + 1], 1.0, ALU.mult, ALU.mult)
                ins.then_inc(a_bdp, 1)

        def la_mask_dve(dve, i, n, cosine):
            dve.wait_ge(a_o, n + 1)
            for q in range(4):
                dve.wait_ge(a_s, 4 * n + q + 2)
                dve.tensor_tensor(Pm[:, 4 * q:4 * q + 4, :], PS[:, 2 + q, :].rearrange("p (h t) -> p h t", t=P),
                                  cmask[:, 0 if cosine else 1, :].unsqueeze(1).broadcast_to([P, 4, P]),
                                  ALU.mult).then_inc(a_pm, 1)

        def la_norm_dve(dve, i, n):
            dve.wait_ge(a_ot, n + 2)
            o = PS[:, 7, :].rearrange("p (h v) -> p h v", v=VW)
            dve.tensor_scalar(nrm[:, :], o[:, :, HD], 1e-6, None, ALU.add).then_inc(a_nrm, 1)
            dve.wait_ge(a_nrm, n + 2)
            dve.reciprocal(rec[:, :], nrm[:, :]).then_inc(a_rec, 1)
            dve.wait_ge(a_rec, n + 2)
            dve.wait_ge(a_ct, n + 1)
            dve.tensor_tensor(ctxt[:, :].rearrange("p (h d) -> p h d", d=HD), o[:, :, 0:HD],
                              rec[:, :].unsqueeze(2).broadcast_to([P, HEADS, HD]), ALU.mult).then_inc(a_ctx, 1)

        def la_queries_dve(dve, i, n, cosine):
            if not cosine:
                dve.wait_ge(a_ln, i + 2)
                dve.wait_ge(a_s, 4 * n + 1)
                dve.scalar_tensor_tensor(qsp[:, :], PS[:, 0, 0:P], 0.0, spl[:, 0, :], ALU.max, ALU.add).then_inc(a_qsp, 1)
                dve.scalar_tensor_tensor(kf[:, :], PS[:, 0, P:2 * P], 0.0, spl[:, 1, :], ALU.max, ALU.add).then_inc(a_kf, 1)
                dve.wait_ge(a_qsp, i + 2)
                dve.wait_ge(a_bd, n + 1)
                dve.wait_ge(a_bdp, n + 1)
                dve.wait_ge(a_qcs, n + 1)
                dve.scalar_tensor_tensor(qf[:, :], H[:, ds(i * P, P)], 1e-6, qsp[:, :], ALU.add, ALU.mult).then_inc(a_qf, 1)
            dve.wait_ge(a_qf, n + 2)
            dve.wait_ge(a_s, 4 * n + 1)
            dve.tensor_tensor(Qbd[:, 0:HALF, :], qf[:, :].unsqueeze(1).broadcast_to([P, HALF, P]),
                              hmask[:, 0:HALF].unsqueeze(2).broadcast_to([P, HALF, P]), ALU.mult).then_inc(a_bd, 1)
            dve.wait_ge(a_in, n + 1)
            if cosine:
                for c in range(2):
                    ins = dve.tensor_tensor(qcs[:, c, :], qf[:, :], crow[:, c, ds((i % TPB) * P, P)], ALU.mult)
            else:
                ins = dve.tensor_copy(qcs[:, 0, :], qf[:, :])
            ins.then_inc(a_qcs, 1)

        def la_state_dve(dve, i, n, kinds):
            w = HEADS * (HD + 1)
            keep = hold[:, ds(i % TPB, 1)]
            dve.wait_ge(a_st, n + 2)
            dve.wait_ge(a_state, n + 1)
            new = stnew[:, 0:kinds, :, :].rearrange("p c h v -> p (c h) v")
            dve.scalar_tensor_tensor(new, PS[:, 2, 0:kinds * w].rearrange("p (h v) -> p h v", v=HD + 1), keep,
                                     hm9[:, 0:kinds * HEADS, :], ALU.mult, ALU.mult).then_inc(a_stm, 1)
            dve.wait_ge(a_stm, n + 2)
            sums = state[:, 0:kinds, :, 0:HD + 1].rearrange("p c h v -> p (c h) v")
            dve.scalar_tensor_tensor(sums, sums, keep, new, ALU.mult, ALU.add).then_inc(a_state, 1)

        def la_tokens_dve(dve, i, n, cosine):
            dve.wait_ge(a_st, n + 1)
            dve.wait_ge(a_kv, n + 2)
            dve.tensor_copy(vaug[:, :, 0:HD], PS[:, 1, C:2 * C].rearrange("p (h d) -> p h d", d=HD)).then_inc(a_v, 1)
            if cosine:
                for c in range(2):
                    ins = dve.tensor_scalar(ktok[:, c, :], PS[:, 1, 0:C], 0.0, ccol[:, c, ds(i % TPB, 1)],
                                            ALU.max, ALU.mult)
                ins.then_inc(a_ktok, 1)
            else:
                dve.scalar_tensor_tensor(ktok[:, 0, :], PS[:, 1, 0:C], 0.0, spl[:, 2, :], ALU.max, ALU.add).then_inc(a_ktok, 1)

        def la_dve(dve, i, n, A, B_, C_, cosine):
            if B_:
                la_mask_dve(dve, i - 1, n - 1, cosine)
            if C_:
                la_norm_dve(dve, i - 2, n - 2)
            if A:
                la_queries_dve(dve, i, n, cosine)
            if B_:
                la_state_dve(dve, i - 1, n - 1, 2 if cosine else 1)
            if A:
                la_tokens_dve(dve, i, n, cosine)

        def la_tiles(eng, body, cosine):
            n0 = 0 if cosine else NT

            def peeled(i):
                body(eng, i, n0 + i, *(s <= i < NT + s for s in range(3)), cosine)

            peeled(0)
            peeled(1)
            with eng.Fori(2, NT) as i:
                body(eng, i, i + n0, True, True, True, cosine)
            peeled(NT)
            peeled(NT + 1)

        def mlp_wo_pe(pe, g):
            pe.wait_ge(d_h, g + 1)
            pe.matmul(PS[:, 2, :], wo0[:, :], group(XSA, g), start=True, stop=True).then_inc(d_wo, 1)

        def mlp_up_pe(pe, g, blocks):
            pe.wait_ge(n_used, ST_MLP + g + 2)
            for f in blocks:
                pe.wait_ge(d_act, F_MLP * g + f + 1)
                pe.matmul(PS[:, 3 + f, :], mw1[:, f * P:(f + 1) * P], hin[:, ds(g % 2, 1), :],
                          start=True, stop=True).then_inc(d_up, 1)

        def mlp_down_pe(pe, g):
            pe.wait_ge(d_h2, g + 1)
            for f in range(F_MLP):
                pe.wait_ge(d_act, F_MLP * g + f + 2)
                mm = pe.matmul(PS[:, 7, :], mw2[:, f, :], hidm[:, f, :], start=(f == 0), stop=(f == F_MLP - 1))
            mm.then_inc(d_y, 1)

        def mlp_sq_act(act, g):
            act.wait_ge(d_h, g + 2)
            square_act(act, group(H, g), ST_MLP + g)

        def mlp_act(act, g, blocks):
            for f in blocks:
                act.wait_ge(d_up, F_MLP * g + f + 2)
                act.wait_ge(d_y, g + 1)
                act.activation(hidm[:, f, :], PS[:, 3 + f, :], ACT.Gelu_apprx_tanh,
                               bias=cols0[:, 4 + f:5 + f]).then_inc(d_act, 1)

        def mlp_h_dve(dve, g):
            dve.wait_ge(d_wo, g + 2)
            dve.scalar_tensor_tensor(group(H, g), PS[:, 2, :], cols0[:, 0:1], group(H, g), ALU.add, ALU.add).then_inc(d_h, 1)

        def mlp_in_dve(dve, g):
            su = ST_MLP + g
            dve.wait_ge(n_r, su + 2)
            dve.scalar_tensor_tensor(hin[:, ds(g % 2, 1), :], group(H, g).unsqueeze(1), cols0[:, 2:3],
                                     rs[:, :].unsqueeze(1), ALU.mult, ALU.mult).then_inc(n_used, 1)

        def mlp_out_dve(dve, g):
            dve.wait_ge(d_y, g + 2)
            dve.scalar_tensor_tensor(group(H, g), PS[:, 7, :], cols0[:, 3:4], group(H, g), ALU.add, ALU.add).then_inc(d_h2, 1)
            dve.wait_ge(d_h2, g + 2)
            dve.scalar_tensor_tensor(group(X, g), group(H, g), modcol(0, GATE_A, g), group(X, g),
                                     ALU.mult, ALU.add).then_inc(d_x, 1)

        def mlp_pe(pe, g, this, more):
            if more:
                mlp_wo_pe(pe, g + 1)
            if this:
                mlp_up_pe(pe, g, (0, 1))
            if more:
                var_pe(pe, ST_MLP + g + 1, 1)
            if this:
                mlp_up_pe(pe, g, (2, 3))
                mlp_down_pe(pe, g)

        def mlp_all_act(act, g, this, more):
            if more:
                mlp_sq_act(act, g + 1)
            if this:
                mlp_act(act, g, (0, 1))
            if more:
                rsqrt_act(act, ST_MLP + g + 1, switch=True)
            if this:
                mlp_act(act, g, (2, 3))
            else:
                act.preload_act_table_set(GELU_TANH)

        def mlp_dve(dve, g, this, more):
            if more:
                mlp_h_dve(dve, g + 1)
                eps_dve(dve, ST_MLP + g + 1, 1, 1e-6)
                mlp_in_dve(dve, g + 1)
            if this:
                mlp_out_dve(dve, g)

        def skewed(eng, body):
            body(eng, -1, False, True)
            with eng.Fori(0, NG - 1) as g:
                body(eng, g, True, True)
            body(eng, NG - 1, True, False)

        ITEMS = SHARED + EXPERTS

        def moe_router_pe(pe, g):
            pe.wait_ge(n_out, LN_MOE + g + 2)
            pe.wait_ge(e_cTs, g + 1)
            pe.matmul(PS[0:EXPERTS, 2, :], wr[:, :], hin[:, ds(g % 2, 1), :], start=True, stop=True).then_inc(e_lg, 1)

        def moe_tokens_pe(pe, g):
            wait_apart(pe, e_sg, g + 2)
            for t in range(4):
                mm = pe.transpose(PS[:, 2, t * EXPERTS:(t + 1) * EXPERTS], sgT[:, t * P:(t + 1) * P],
                                  ident[0:EXPERTS, 0:EXPERTS])
            mm.then_inc(e_sgt, 1)

        def moe_weights_pe(pe, g):
            pe.wait_ge(e_comb, g + 2)
            for t in range(4):
                mm = pe.transpose(PS[0:EXPERTS, 2, t * P:(t + 1) * P], comb[:, t, :], ident[:, :])
            mm.then_inc(e_cT, 1)

        def moe_up_pe(pe, g, k):
            c = ITEMS * g + k
            pe.wait_ge(e_mul, c)
            if k < SHARED:
                first, second, rhs2 = sw1[:, k * P:(k + 1) * P], sw3[:, k * P:(k + 1) * P], hin[:, ds(g % 2, 1), :]
            else:
                first, second, rhs2 = ew1[:, k - SHARED, :], esel[:, k - SHARED, :], combT[:, :]
            if k == SHARED:
                pe.wait_ge(e_cTs, g + 2)
            pe.matmul(PS[:, 3 + k % 2, :], first, hin[:, ds(g % 2, 1), :], start=True, stop=True)
            pe.matmul(PS[:, 5 + k % 2, :], second, rhs2, start=True, stop=True).then_inc(e_u, 1)

        def moe_down_pe(pe, g, k):
            pe.wait_ge(e_mul, ITEMS * g + k + 2)
            if k == 0:
                pe.wait_ge(e_x, g + 1)
            w = sw2[:, k, :] if k < SHARED else ew2[:, k - SHARED, :]
            pe.matmul(PS[:, 7, :], w, hid2[:, k % 2, :], start=(k == 0), stop=(k == ITEMS - 1)).then_inc(e_down, 1)

        def moe_act(act, g, k):
            c = ITEMS * g + k
            act.wait_ge(e_u, c + 2)
            act.wait_ge(e_mul, c)
            act.activation(hid[:, k % 2, :], PS[:, 3 + k % 2, :], ACT.Silu if k < SHARED else ACT.Gelu).then_inc(e_act, 1)

        def moe_mul_dve(dve, g, k):
            c = ITEMS * g + k
            dve.wait_ge(e_act, c + 2)
            dve.wait_ge(e_down, c)
            dve.tensor_tensor(hid2[:, k % 2, :], hid[:, k % 2, :], PS[:, 5 + k % 2, :], ALU.mult).then_inc(e_mul, 1)

        ROUTE = 12

        def moe_route_dve(dve, g):
            k = [0]

            def link(ins):
                k[0] += 1
                ins.then_inc(e_dve, 1)
                dve.wait_ge(e_dve, ROUTE * g + k[0] + 1)

            b4 = [P, 4, EXPERTS, EXPERTS]
            dve.wait_ge(e_sgt, g + 2)
            dve.wait_ge(e_cT, g + 1)
            dve.tensor_copy(sg[:, :, :], PS[:, 2, 0:4 * EXPERTS].rearrange("p (t e) -> p t e", e=EXPERTS)).then_inc(e_s, 1)
            dve.wait_ge(e_s, g + 2)
            link(dve.tensor_tensor(sel[:, :, :], sg[:, :, :], rbias[:, :].unsqueeze(1).broadcast_to([P, 4, EXPERTS]), ALU.add))
            other, own = sel[:, :, :].unsqueeze(2).broadcast_to(b4), sel[:, :, :].unsqueeze(3).broadcast_to(b4)
            dve.tensor_tensor(above[:, :, :, :], other, own, ALU.is_gt)
            link(dve.tensor_tensor(level[:, :, :, :], other, own, ALU.is_ge))
            link(dve.tensor_tensor(level[:, :, :, :], level[:, :, :, :], low[:, :, :].unsqueeze(1).broadcast_to(b4), ALU.mult))
            link(dve.tensor_tensor(above[:, :, :, :], above[:, :, :, :], level[:, :, :, :], ALU.max))
            link(dve.tensor_reduce(rank[:, :, :], above[:, :, :, :], AX.X, ALU.add))
            link(dve.tensor_scalar(selm[:, :, :], rank[:, :, :], 2.0, None, ALU.is_lt))
            link(dve.tensor_tensor(ssel[:, :, :], selm[:, :, :], sg[:, :, :], ALU.mult))
            link(dve.tensor_reduce(den[:, 0, :], ssel[:, :, :], AX.X, ALU.add))
            dve.tensor_scalar(den[:, 1, :], den[:, 0, :], 1e-9, None, ALU.add)
            link(dve.tensor_scalar(den[:, 2, :], den[:, 0, :], 1e-9, None, ALU.is_gt))
            dve.tensor_scalar(den[:, 4, :], den[:, 2, :], -0.5, 0.5, ALU.mult, ALU.add)
            link(dve.reciprocal(den[:, 1, :], den[:, 1, :]))
            link(dve.tensor_tensor(den[:, 3, :], den[:, 1, :], den[:, 2, :], ALU.mult))
            dve.tensor_tensor(gsel[:, :, :], ssel[:, :, :], den[:, 3, :].unsqueeze(2).broadcast_to([P, 4, EXPERTS]), ALU.mult)
            link(dve.tensor_tensor(gelse[:, :, :], selm[:, :, :], den[:, 4, :].unsqueeze(2).broadcast_to([P, 4, EXPERTS]), ALU.mult))
            assert k[0] == ROUTE
            dve.tensor_tensor(comb[:, :, :], gsel[:, :, :], gelse[:, :, :], ALU.add).then_inc(e_comb, 1)

        def moe_norm_dve(dve, g, part):
            u, su = LN_MOE + g, ST_MOE + g
            if part == 0:
                centre_dve(dve, group(X, g), u, su, 0)
            elif part == 1:
                eps_dve(dve, su, 1, 1e-5)
            else:
                affine_dve(dve, hin[:, ds(g % 2, 1), :], u, su, modcol(0, SCALE_B, g), modcol(0, SHIFT_B, g))

        def moe_weights_dve(dve, g):
            dve.wait_ge(e_cT, g + 2)
            dve.wait_ge(e_u, ITEMS * g + 1)
            dve.tensor_copy(combT[0:EXPERTS, :], PS[0:EXPERTS, 2, :]).then_inc(e_cTs, 1)

        def moe_x_dve(dve, g):
            dve.wait_ge(e_down, ITEMS * (g + 1) + 1)
            dve.scalar_tensor_tensor(group(X, g), PS[:, 7, :], modcol(0, GATE_B, g), group(X, g),
                                     ALU.mult, ALU.add).then_inc(e_x, 1)

        def moe_sq_act(act, g):
            act.wait_ge(n_xc, LN_MOE + g + 2)
            square_act(act, xc[:, :], ST_MOE + g)

        def moe_sigmoid_act(act, g):
            act.wait_ge(e_lg, g + 2)
            act.wait_ge(e_sgt, g + 1)
            act.activation(sgT[:, :], PS[0:EXPERTS, 2, :], ACT.Sigmoid).then_inc(e_sg, 1)

        def moe_pe(pe, g, this, more):
            steps = {0: lambda: mean_pe(pe, group(X, g + 1), LN_MOE + g + 1, 0),
                     2: lambda: var_pe(pe, ST_MOE + g + 1, 1),
                     4: lambda: moe_router_pe(pe, g + 1),
                     6: lambda: moe_tokens_pe(pe, g + 1),
                     ITEMS - 1: lambda: moe_weights_pe(pe, g + 1)}
            if this:
                moe_up_pe(pe, g, 0)
                moe_up_pe(pe, g, 1)
            for k in range(ITEMS):
                if this:
                    moe_down_pe(pe, g, k)
                    if k + 2 < ITEMS:
                        moe_up_pe(pe, g, k + 2)
                if more and k in steps:
                    steps[k]()

        def moe_all_act(act, g, this, more):
            steps = {1: lambda: moe_sq_act(act, g + 1),
                     3: lambda: rsqrt_act(act, ST_MOE + g + 1, switch=True),
                     6: lambda: moe_sigmoid_act(act, g + 1)}
            for k in range(ITEMS):
                if this:
                    moe_act(act, g, k)
                if more and k in steps:
                    steps[k]()

        def moe_dve(dve, g, this, more):
            steps = {1: lambda: moe_norm_dve(dve, g + 1, 0),
                     3: lambda: moe_norm_dve(dve, g + 1, 1),
                     4: lambda: moe_norm_dve(dve, g + 1, 2),
                     8: lambda: moe_route_dve(dve, g + 1)}
            for k in range(ITEMS):
                if this:
                    moe_mul_dve(dve, g, k)
                if more and k in steps:
                    steps[k]()
            if more:
                moe_weights_dve(dve, g + 1)
            if this:
                moe_x_dve(dve, g)

        def two_banks(first):
            return PS[:, first:first + 2, :].rearrange("p b n -> p (b n)")

        def column(eng, i, at):
            off = (i // TPB) * XSW + (i % TPB) * P + at
            return off if isinstance(i, int) else eng.snap(off)

        def project(pe, bank, x, kind):
            for j in range(2):
                c0 = kind * INNER + j * GW
                mm = pe.matmul(PS[:, bank + j, :], x, Wqkv[:, c0:c0 + GW], start=True, stop=True)
            return mm

        def q_pe(pe, i, n, older):
            pe.wait_ge(t_xt, n + 2)
            pe.wait_ge(t_nq, n + 1)
            if older:
                pe.wait_ge(t_vs, n - 3 + 2)
            project(pe, 0, xt[:, :], 0).then_inc(t_q, 1)

        def k_pe(pe, i, n, older):
            pe.wait_ge(t_nk, n + 1)
            if older:
                pe.wait_ge(t_h, n - 4 + 2)
            project(pe, 2, xt[:, :], 1).then_inc(t_k, 1)

        def v_pe(pe, i, n, newer):
            pe.wait_ge(t_xv, n + 2)
            pe.wait_ge(t_vs, n + 1)
            if newer:
                pe.wait_ge(t_nq, n + 2 + 2)
            project(pe, 0, xv[:, :], 2).then_inc(t_v, 1)

        def eight_transposes(pe, bank, src):
            for j in range(8):
                mm = pe.transpose(PS[:, bank + j // 4, (j % 4) * P:(j % 4 + 1) * P], src(j), ident[:, :])
            return mm

        def pT_pe(pe, i, n):
            pe.wait_ge(t_exp, 2 * n + 2)
            for j in range(8):
                if j == 4:
                    pe.wait_ge(t_exp, 2 * n + 3)
                mm = pe.transpose(PS[:, 6 + j // 4, (j % 4) * P:(j % 4 + 1) * P], pE[:, j * P:(j + 1) * P], ident[:, :])
            mm.then_inc(t_pT, 1)

        def pv_pe(pe, i, n):
            pe.wait_ge(t_pTc, n + 2)
            pe.wait_ge(t_vc, n + 2)
            pe.wait_ge(t_vcp, n + 2)
            pe.wait_ge(t_vcd, n + 2)
            pe.wait_ge(t_oTc, n + 1)
            for p in range(PAIRS):
                for w in range(NWIN):
                    mm = pe.matmul(PS[WIN * w:WIN * (w + 1), 4 + p // 4, (p % 4) * P:(p % 4 + 1) * P],
                                   pT[:, p, WIN * w:WIN * (w + 1)], Vbd[:, w, p, :], start=True, stop=True)
            mm.then_inc(t_o, 1)

        def oT_pe(pe, i, n):
            pe.wait_ge(t_on, n + 2)
            eight_transposes(pe, 4, lambda j: On[:, j * P:(j + 1) * P]).then_inc(t_oT, 1)

        def wo_pe(pe, i, n, newer):
            pe.wait_ge(t_oTc, n + 2)
            pe.wait_ge(t_h, n + 1)
            if newer:
                pe.wait_ge(t_nk, n + 3 + 2)
            for c in range(PAIRS):
                mm = pe.matmul(PS[:, 2, 0:P], Wo6[:, c, :], OTs[:, c, :], start=(c == 0), stop=(c == PAIRS - 1))
            mm.then_inc(t_y, 1)

        def qT_pe(pe, i, n):
            pe.wait_ge(t_rotq, n + 2)
            pe.wait_ge(t_pTc, n + 1)
            eight_transposes(pe, 6, lambda j: rot[:, 0, j * P:(j + 1) * P]).then_inc(t_qT, 1)

        def kT_pe(pe, i, n, older):
            pe.wait_ge(t_rotk, n + 2)
            if older:
                pe.wait_ge(t_oTc, n - 2 + 2)
            eight_transposes(pe, 4, lambda j: rot[:, 1, j * P:(j + 1) * P]).then_inc(t_kT, 1)

        def s_pe(pe, i, n):
            first = (i % TPB + TPB - 1) // TPB
            first = first if isinstance(i, int) else pe.snap(first)
            pe.wait_ge(t_qTc, n + 2)
            for j in range(2):
                pe.matmul(PS[:, 6 + j, :], identh[:, :], wmask[:, ds(first, 1), :], start=True, stop=False,
                          skip_group_check=True)
            pe.wait_ge(t_kTc, n + 2)
            for p in range(PAIRS):
                for w in range(NWIN):
                    mm = pe.matmul(PS[WIN * w:WIN * (w + 1), 6 + p // 4, (p % 4) * P:(p % 4 + 1) * P],
                                   qT[:, p, WIN * w:WIN * (w + 1)], kbd[:, p, :, WIN * w:WIN * w + KEYS],
                                   start=False, stop=(p % 4 == 3), skip_group_check=True)
            mm.then_inc(t_s, 1)

        def exp_act(act, i, n):
            act.wait_ge(t_pT, n + 1)
            act.wait_ge(t_sum, n + 1)
            for j in range(2):
                act.wait_ge(t_sub, 2 * n + j + 2)
                act.activation(pE[:, j * GW:(j + 1) * GW], ssub[:, j * GW:(j + 1) * GW], ACT.Exp).then_inc(t_exp, 1)

        def sq_act(act, i, n):
            act.wait_ge(t_q, n + 2)
            act.wait_ge(t_red, 2 * n + 1)
            act.activation(sqk[:, 0, :], two_banks(0), ACT.Square).then_inc(t_sqq, 1)
            act.wait_ge(t_k, n + 2)
            act.activation(sqk[:, 1, :], two_banks(2), ACT.Square).then_inc(t_sqk, 1)

        def root_act(act, i, n):
            act.wait_ge(t_sm, n + 2)
            act.wait_ge(t_nk, n + 1)
            act.activation(rqk[:, :, :], ssm[:, :, :], ACT.Ln).then_inc(t_ln, 1)
            act.wait_ge(t_ln, n + 2)
            act.activation(rqk[:, :, :], rqk[:, :, :], ACT.Exp, scale=-0.5).then_inc(t_root, 1)

        def pTc_act(act, i, n):
            act.wait_ge(t_pT, n + 2)
            act.wait_ge(t_o, n + 1)
            act.activation(pT[:, :, :].rearrange("p c t -> p (c t)"), two_banks(6), ACT.Copy).then_inc(t_pTc, 1)

        def placing(w, at, first, count, hd):
            cols = slice(hd * DH, (hd + 1) * DH)
            p0 = 2 * WIN * hd + WIN * at
            src = vst[WIN * first:WIN * (first + count), :].rearrange("p (c d) -> p c d", d=2 * DH)
            return Vbd[p0:p0 + WIN * count, w, :, cols], src[:, :, cols]

        def vc_act(act, i, n):
            act.wait_ge(t_v, n + 2)
            act.wait_ge(t_vc, n + 1)
            act.wait_ge(t_vcp, n + 1)
            act.wait_ge(t_vcd, n + 1)
            act.activation(vst[:, :], two_banks(0), ACT.Copy).then_inc(t_vs, 1)

        def place_act(act, i, n, part):
            if part == 0:
                act.wait_ge(t_o, n + 1)
                for hd in range(2):
                    q0 = 2 * WIN * hd
                    cols = slice(hd * DH, (hd + 1) * DH)
                    ins = act.activation(Vbd[q0:q0 + WIN, 0, :, cols], Vbd[q0 + WIN:q0 + 2 * WIN, NWIN - 1, :, cols], ACT.Copy)
                ins.then_inc(t_vlast, 1)
                act.wait_ge(t_vs, n + 2)
                for hd in range(2):
                    act.activation(*placing(0, 1, 0, 1, hd), ACT.Copy)
            else:
                act.wait_ge(t_vlast, n + 2)
                for hd in range(2):
                    ins = act.activation(*placing(3, 0, 2, 2, hd), ACT.Copy)
                ins.then_inc(t_vc, 1)

        def oTc_act(act, i, n):
            act.wait_ge(t_oT, n + 2)
            act.wait_ge(t_y, n + 1)
            act.activation(OTs[:, :, :].rearrange("p c t -> p (c t)"), two_banks(4), ACT.Copy).then_inc(t_oTc, 1)

        def qTc_act(act, i, n):
            act.wait_ge(t_qT, n + 2)
            act.wait_ge(t_s, n + 1)
            act.activation(qT[:, :, :].rearrange("p c t -> p (c t)"), two_banks(6), ACT.Copy).then_inc(t_qTc, 1)

        def kTc_act(act, i, n):
            act.wait_ge(t_kT, n + 2)
            act.wait_ge(t_halo, n + 2)
            act.activation(kbd[0:DH, :, 0, HALO:HALO + P],
                           PS[0:DH, 4:6, :].rearrange("p b (c t) -> p (b c) t", t=P), ACT.Copy)
            act.activation(kbd[DH:2 * DH, :, 1, HALO:HALO + P],
                           PS[DH:2 * DH, 4:6, :].rearrange("p b (c t) -> p (b c) t", t=P), ACT.Copy).then_inc(t_kTc, 1)

        def heads(ap, width):
            return ap.rearrange("p (h d) -> p h d", d=width)

        def rope_dve(dve, l):
            dve.wait_ge(s_wa, 16 * loads_a * (l + 1))
            dve.tensor_tensor(ropel[:, 0, :, :], rope[:, 0, :, :],
                              qks[:, :, :].rearrange("p k d -> p (k d)").unsqueeze(1).broadcast_to([P, TPB, 2 * DH]), ALU.mult)
            for half in range(2):
                a0, b0 = half * (DH // 2), (1 - half) * (DH // 2)
                for k in range(2):
                    ins = dve.tensor_tensor(ropel[:, 1, :, k * DH + a0:k * DH + a0 + DH // 2],
                                            rope[:, 1, :, k * DH + a0:k * DH + a0 + DH // 2],
                                            qks[:, k, b0:b0 + DH // 2].unsqueeze(1).broadcast_to([P, TPB, DH // 2]), ALU.mult)
            ins.then_inc(t_rope, 1)
            dve.wait_ge(t_rope, l + 2)

        def softmax_dve(dve, i, n):
            dve.wait_ge(t_s, n + 2)
            dve.tensor_reduce(smax[:, :], heads(two_banks(6), KEYS), AX.X, ALU.max).then_inc(t_max, 1)
            dve.wait_ge(t_max, n + 2)
            dve.wait_ge(t_exp, 2 * n + 1)
            h2 = HEADS // 2
            for j in range(2):
                dve.tensor_tensor(heads(ssub[:, j * GW:(j + 1) * GW], KEYS), heads(PS[:, 6 + j, :], KEYS),
                                  smax[:, j * h2:(j + 1) * h2].unsqueeze(2).broadcast_to([P, h2, KEYS]),
                                  ALU.subtract).then_inc(t_sub, 1)

        def red_dve(dve, i, n):
            dve.wait_ge(t_sm, n + 1)
            for k, squares in enumerate((t_sqq, t_sqk)):
                dve.wait_ge(squares, n + 2)
                dve.tensor_reduce(ss[:, k, :], heads(sqk[:, k, :], DH), AX.X, ALU.add).then_inc(t_red, 1)
            dve.wait_ge(t_red, 2 * n + 3)
            dve.wait_ge(t_ln, n + 1)
            dve.tensor_scalar(ssm[:, :, :], ss[:, :, :], 1e-24, None, ALU.max).then_inc(t_sm, 1)

        def scale_dve(dve, i, n, k):
            read, done = ((t_mq, t_nq), (t_mk, t_nk))[k]
            dve.wait_ge(t_root, n + 2)
            dve.wait_ge(read, n + 1)
            dve.tensor_tensor(heads(qkn[:, k, :], DH), heads(two_banks(2 * k), DH),
                              rqk[:, k, :].unsqueeze(2).broadcast_to([P, HEADS, DH]), ALU.mult).then_inc(done, 1)

        def rotate_dve(dve, i, n, k):
            T = i % TPB if isinstance(i, int) else dve.snap(i % TPB)
            half = DH // 2
            given, used, done = ((t_nq, t_qT, t_mq), (t_nk, t_kT, t_mk))[k]

            def table(c, d0, d1):
                return ropel[:, c, ds(T, 1), k * DH + d0:k * DH + d1].broadcast_to([P, HEADS, d1 - d0])

            dve.wait_ge(given, n + 2)
            dve.wait_ge(used, n + 1)
            v, w1, w2 = heads(qkn[:, k, :], DH), heads(m1[:, k, :], DH), heads(m2[:, k, :], DH)
            dve.tensor_tensor(w1, v, table(0, 0, DH), ALU.mult)
            dve.tensor_tensor(w2[:, :, 0:half], v[:, :, half:DH], table(1, 0, half), ALU.mult)
            dve.tensor_tensor(w2[:, :, half:DH], v[:, :, 0:half], table(1, half, DH), ALU.mult).then_inc(done, 1)

        def onorm_dve(dve, i, n):
            dve.wait_ge(t_sum, n + 2)
            dve.reciprocal(orec[:, :], psums[:, :]).then_inc(t_orec, 1)
            dve.wait_ge(t_o, n + 2)
            dve.wait_ge(t_orec, n + 2)
            dve.wait_ge(t_oT, n + 1)
            dve.tensor_tensor(heads(On[:, :], DH), heads(two_banks(4), DH),
                              orec[:, :].unsqueeze(2).broadcast_to([P, HEADS, DH]), ALU.mult).then_inc(t_on, 1)

        def place_dve(dve, i, n):
            dve.wait_ge(t_o, n + 1)
            dve.wait_ge(t_vs, n + 2)
            for hd in range(2):
                dve.tensor_copy(*placing(1, 0, 0, 2, hd))
                ins = dve.tensor_copy(*placing(2, 0, 1, 1, hd))
            ins.then_inc(t_vcd, 1)

        def sum_dve(dve, i, n):
            dve.wait_ge(t_exp, 2 * n + 3)
            dve.wait_ge(t_orec, n + 1)
            dve.tensor_reduce(psums[:, :], heads(pE[:, :], KEYS), AX.X, ALU.add).then_inc(t_sum, 1)

        def resid_dve(dve, i, n):
            dve.wait_ge(t_y, n + 2)
            h = H[:, ds(i * P, P)]
            dve.tensor_tensor(h, h, PS[:, 2, 0:P], ALU.add).then_inc(t_h, 1)

        def xt_pool(pool, i, n):
            off = column(pool, i, HALO)
            wait_apart(pool, t_k, n + 1)
            pool.tensor_copy(xt[:, :], XSA[:, ds(off, P)]).then_inc(t_xt, 1)
            wait_apart(pool, t_xt, n + 2)

        def xv_pool(pool, i, n):
            off = column(pool, i, HALO)
            wait_apart(pool, t_v, n + 1)
            pool.tensor_copy(xv[:, :], XSA[:, ds(off, P)]).then_inc(t_xv, 1)
            wait_apart(pool, t_xv, n + 2)

        def vc_pool(pool, i, n):
            pool.wait_ge(t_o, n + 1)
            wait_apart(pool, t_vs, n + 2)
            pool.tensor_copy(*placing(2, 1, 2, 1, 0))
            pool.tensor_copy(*placing(2, 1, 2, 1, 1)).then_inc(t_vcp, 1)
            wait_apart(pool, t_vcp, n + 2)

        def halo_pool(pool, i, n):
            wait_apart(pool, t_s, n + 1)
            pool.tensor_copy(kbd[:, :, :, 0:HALO], kbd[:, :, :, P:P + HALO]).then_inc(t_halo, 1)

        def rotate_pool(pool, i, n):
            for k, (given, done) in enumerate(((t_mq, t_rotq), (t_mk, t_rotk))):
                pool.wait_ge(given, n + 2)
                pool.tensor_tensor(rot[:, k, :], m1[:, k, :], m2[:, k, :], ALU.add).then_inc(done, 1)
            wait_apart(pool, t_rotk, n + 2)

        def shift_copies(pool, dst, off, src, done, n):
            w = src.shape[-1]
            pool.tensor_copy(dst[0:64, ds(off, w)], src[0:64, :])
            pool.tensor_copy(dst[64:128, ds(off + 1, w)], src[64:128, :]).then_inc(done, 1)
            wait_apart(pool, done, n + 2)

        def xs_pool(pool, i, n):
            off = column(pool, i, HALO)
            wait_apart(pool, t_h, n + 2)
            shift_copies(pool, XSF, off, H[:, ds(i * P, P)], t_xs, n)

        def att_pe(pe, i, n, A, B_, C_, D):
            if A:
                q_pe(pe, i, n, D)
                k_pe(pe, i, n, D)
            if C_:
                s_pe(pe, i - 2, n - 2)
            if D:
                pv_pe(pe, i - 3, n - 3)
            if C_:
                pT_pe(pe, i - 2, n - 2)
            if D:
                oT_pe(pe, i - 3, n - 3)
            if B_:
                qT_pe(pe, i - 1, n - 1)
            if C_:
                v_pe(pe, i - 2, n - 2, A)
            if B_:
                kT_pe(pe, i - 1, n - 1, D)
            if D:
                wo_pe(pe, i - 3, n - 3, A)

        def att_act(act, i, n, A, B_, C_, D):
            if A:
                sq_act(act, i, n)
            if D:
                place_act(act, i - 3, n - 3, 1)
            if A:
                root_act(act, i, n)
            if C_:
                exp_act(act, i - 2, n - 2)
                pTc_act(act, i - 2, n - 2)
            if D:
                oTc_act(act, i - 3, n - 3)
            if B_:
                qTc_act(act, i - 1, n - 1)
            if C_:
                vc_act(act, i - 2, n - 2)
            if B_:
                kTc_act(act, i - 1, n - 1)
            if C_:
                place_act(act, i - 2, n - 2, 0)

        def att_dve(dve, i, n, A, B_, C_, D):
            if A:
                red_dve(dve, i, n)
            if C_:
                softmax_dve(dve, i - 2, n - 2)
            if D:
                onorm_dve(dve, i - 3, n - 3)
            if A:
                scale_dve(dve, i, n, 0)
                scale_dve(dve, i, n, 1)
            if C_:
                sum_dve(dve, i - 2, n - 2)
            if A:
                rotate_dve(dve, i, n, 0)
            if D:
                resid_dve(dve, i - 3, n - 3)
            if A:
                rotate_dve(dve, i, n, 1)
            if C_:
                place_dve(dve, i - 2, n - 2)

        def att_pool(pool, i, n, A, B_, C_, D):
            if isinstance(i, int) and i == 0:
                xt_pool(pool, 0, n)
            if B_:
                rotate_pool(pool, i - 1, n - 1)
                halo_pool(pool, i - 1, n - 1)
            if C_:
                xv_pool(pool, i - 2, n - 2)
            if not isinstance(i, int) or i + 1 < NT:
                xt_pool(pool, i + 1, n + 1)
            if C_:
                vc_pool(pool, i - 2, n - 2)
            if D:
                xs_pool(pool, i - 3, n - 3)

        def tiles(eng, l, body):
            def peeled(i):
                body(eng, i, l * NT + i, *(s <= i < NT + s for s in range(4)))

            for i in range(3):
                peeled(i)
            with eng.Fori(3, NT - 1) as i:
                body(eng, i, l * NT + i, True, True, True, True)
            for i in range(NT - 1, NT + 3):
                peeled(i)

        def ff_mean_pe(pe, g, n):
            mean_pe(pe, XSF[:, ds(xs_group(XSF, g), GW)], LN_FFN + n, 0)

        def ff_up_pe(pe, g, n, blocks):
            pe.wait_ge(n_out, LN_FFN + n + 2)
            for c in blocks:
                c0, m = CH[c]
                pe.wait_ge(h_h if c == 0 else h_act, n + 1 if c == 0 else 3 * n + 1)
                pe.matmul(PS[0:m, 2 + c, :], W1[:, DIN + c0:DIN + c0 + m], fx[:, ds(n % 2, 1), :],
                          start=True, stop=True)
                pe.wait_ge(h_hg, 3 * n + 1)
                pe.matmul(PS[0:m, 5 + c, :], W1[:, c0:c0 + m], fx[:, ds(n % 2, 1), :],
                          start=True, stop=True).then_inc(h_u, 1)

        def ff_down_pe(pe, g, n):
            for c in range(3):
                c0, m = CH[c]
                pe.wait_ge(h_hg, 3 * n + c + 2)
                mm = pe.matmul(PS[:, 2, :], W2[0:m, c, :], hg[0:m, c, :], start=(c == 0), stop=(c == 2))
            mm.then_inc(h_y, 1)

        def ff_act(act, g, n, blocks):
            for c in blocks:
                c0, m = CH[c]
                act.wait_ge(h_u, 3 * n + c + 2)
                act.wait_ge(h_hg, 3 * n + 1)
                act.activation(gl[0:m, c, :], PS[0:m, 2 + c, :], ACT.Gelu, bias=b1col[0:m, 3 + c:4 + c]).then_inc(h_act, 1)

        def ff_mul_dve(dve, g, n, blocks):
            for c in blocks:
                c0, m = CH[c]
                dve.wait_ge(h_act, 3 * n + c + 2)
                dve.wait_ge(h_y, n + 1)
                dve.scalar_tensor_tensor(hg[0:m, c, :], PS[0:m, 5 + c, :], b1col[0:m, c:c + 1], gl[0:m, c, :],
                                         ALU.add, ALU.mult).then_inc(h_hg, 1)

        def ff_h_dve(dve, g, n):
            dve.wait_ge(h_y, n + 2)
            dve.scalar_tensor_tensor(group(H, g), PS[:, 2, :], b2col[:, 0:1], group(H, g), ALU.add, ALU.add).then_inc(h_h, 1)

        def ff_norm_dve(dve, g, n, part):
            u, su = LN_FFN + n, ST_FFN + n
            if part == 0:
                centre_dve(dve, XSF[:, ds(xs_group(XSF, g), GW)], u, su, 0)
            else:
                eps_dve(dve, su, 1, 1e-5)
                affine_dve(dve, fx[:, ds(n % 2, 1), :], u, su, lncol[:, 0:1], lncol[:, 1:2])

        def xs_off(eng, g):
            return xs_group(XSF, g) if isinstance(g, int) else eng.snap(xs_group(XSF, g))

        def ff_pool(pool, g, n):
            off = xs_off(pool, g)
            wait_apart(pool, h_h, n + 2)
            shift_copies(pool, XSA, off, group(H, g), h_xs, n)

        def groups(eng, l, first, body):
            first(eng, 0, l * NG)
            with eng.Fori(0, NG - 1) as g:
                body(eng, g, l * NG + g, True)
            body(eng, NG - 1, l * NG + NG - 1, False)

        def ff_body_pe(pe, g, n, more):
            if more:
                ff_mean_pe(pe, g + 1, n + 1)
            ff_up_pe(pe, g, n, (0,))
            if more:
                var_pe(pe, ST_FFN + n + 1, 1)
            ff_up_pe(pe, g, n, (1, 2))
            ff_down_pe(pe, g, n)

        def ff_first_pe(pe, g, n):
            ff_mean_pe(pe, g, n)
            var_pe(pe, ST_FFN + n, 1)

        def ff_sq_act(act, g, n):
            act.wait_ge(n_xc, LN_FFN + n + 2)
            square_act(act, xc[:, :], ST_FFN + n)

        def ff_first_act(act, g, n):
            ff_sq_act(act, g, n)
            rsqrt_act(act, ST_FFN + n, switch=True)
            act.preload_act_table_set(GELU)

        def ff_body_act(act, g, n, more):
            if more:
                ff_sq_act(act, g + 1, n + 1)
            ff_act(act, g, n, (0,))
            if more:
                rsqrt_act(act, ST_FFN + n + 1, switch=True)
            ff_act(act, g, n, (1, 2))

        def ff_first_dve(dve, g, n):
            ff_norm_dve(dve, g, n, 0)
            ff_norm_dve(dve, g, n, 1)

        def ff_body_dve(dve, g, n, more):
            if more:
                ff_norm_dve(dve, g + 1, n + 1, 0)
            ff_mul_dve(dve, g, n, (0,))
            if more:
                ff_norm_dve(dve, g + 1, n + 1, 1)
            ff_mul_dve(dve, g, n, (1, 2))
            ff_h_dve(dve, g, n)

        block = ctx.enter_context(nc.Block())

        @block.sync
        def _(sp):
            for s in primed:
                sp.sem_inc(s, 1)
            for dst, src in first_loads:
                sp.dma_start(dst, src).then_inc(s_first, 16)
            for dst, src in loads:
                sp.dma_start(dst, src).then_inc(s_load, 16)
            load_attention(sp, 0)
            load_ffn(sp, 0)
            sp.wait_ge(s_phase, 4 * (PH_WO1 + 1))
            for dst, src in late_loads:
                sp.dma_start(dst, src).then_inc(s_load2, 16)
            with sp.Fori(1, DEPTH) as l:
                sp.wait_ge(s_phase, 4 * (PH_LAYERS + 2 * l - 1))
                load_attention(sp, l)
                sp.wait_ge(s_phase, 4 * (PH_LAYERS + 2 * l))
                load_ffn(sp, l)
            with sp.Fori(0, NG) as g:
                sp.wait_ge(f_x, g + NG + 2)
                sp.dma_start(out[:, ds(g * GW, GW)], group(X, g)).then_inc(s_out, 16)
            sp.wait_ge(s_out, 16 * NG)

        @block.tensor
        def _(pe):
            pe.wait_ge(s_first, 16 * len(first_loads))
            pe.wait_ge(s_silu, 1)
            for k in range(2):
                for j in range(6):
                    o = (6 * k + j) * B
                    mm = pe.matmul(PS[:, 0, o:o + B], wmod[:, k, j * C:(j + 1) * C], scT[:, k, :], start=True, stop=True)
            mm.then_inc(s_modps, 1)
            end_phase(pe, PH_MOD)
            pe.wait_ge(s_load, 16 * len(loads))
            with pe.Fori(0, NG) as g:
                mean_pe(pe, group(X, g), LN_PREP0 + g, 0)
                var_pe(pe, ST_PREP0 + 2 * g, 1)
                var_pe(pe, ST_PREP0 + 2 * g + 1, 1)
            end_phase(pe, PH_PREP0)
            la_tiles(pe, la_pe, True)
            end_phase(pe, PH_ATT0)
            skewed(pe, mlp_pe)
            end_phase(pe, PH_MLP)
            skewed(pe, moe_pe)
            end_phase(pe, PH_MOE)
            with pe.Fori(0, NG) as g:
                mean_pe(pe, group(X, g), LN_PREP1 + g, 0)
                var_pe(pe, ST_PREP1 + g, 1)
                pe.wait_ge(n_out, LN_PREP1 + g + 2)
                pe.wait_ge(g_out, g + 1)
                pe.matmul(PS[:, 2, :], wl1[:, 4, :], group(XSF, g), start=True, stop=True).then_inc(g_ps, 1)
            end_phase(pe, PH_PREP1)
            la_tiles(pe, la_pe, False)
            end_phase(pe, PH_ATT1)
            with pe.Fori(0, NG) as g:
                pe.wait_ge(f_x, g + 1)
                pe.matmul(PS[:, 2, :], wl1[:, 3, :], group(H, g), start=True, stop=True).then_inc(f_wo, 1)
                pe.wait_ge(f_x, g + 2)
                mean_pe(pe, group(X, g), LN_WO1 + g, 0)
                var_pe(pe, ST_WO1 + g, 1)
            end_phase(pe, PH_WO1)
            end_phase(pe, PH_ZERO)
            with pe.Fori(0, DEPTH) as l:
                pe.wait_ge(s_wa, 16 * loads_a * (l + 1))
                pe.wait_ge(s_cast, 1)
                tiles(pe, l, att_pe)
                end_phase(pe, PH_LAYERS + 2 * l)
                pe.wait_ge(s_wf, 16 * loads_f * (l + 1))
                groups(pe, l, ff_first_pe, ff_body_pe)
                end_phase(pe, PH_LAYERS + 2 * l + 1)

        @block.scalar
        def _(act):
            act.wait_ge(s_first, 16 * len(first_loads))
            act.activation(scT[:, :, :], cT[:, :, :], ACT.Silu).then_inc(s_silu, 1)
            act.preload_act_table_set(LOG_EXP)
            end_phase(act, PH_MOD)
            act.wait_ge(s_load, 16 * len(loads))
            with act.Fori(0, NG) as g:
                act.wait_ge(n_xc, LN_PREP0 + g + 2)
                square_act(act, xc[:, :], ST_PREP0 + 2 * g)
                rsqrt_act(act, ST_PREP0 + 2 * g)
                act.wait_ge(n_out, LN_PREP0 + g + 2)
                square_act(act, group(H, g), ST_PREP0 + 2 * g + 1)
                rsqrt_act(act, ST_PREP0 + 2 * g + 1)
            end_phase(act, PH_PREP0)
            la_tiles(act, la_act, True)
            end_phase(act, PH_ATT0)
            skewed(act, mlp_all_act)
            end_phase(act, PH_MLP)
            skewed(act, moe_all_act)
            end_phase(act, PH_MOE)
            with act.Fori(0, NG) as g:
                act.wait_ge(n_xc, LN_PREP1 + g + 2)
                square_act(act, xc[:, :], ST_PREP1 + g)
                rsqrt_act(act, ST_PREP1 + g, switch=True)
                act.wait_ge(g_ps, g + 2)
                act.activation(group(H, g), PS[:, 2, :], ACT.Sigmoid, bias=bg1[:, 0:1]).then_inc(g_out, 1)
            act.preload_act_table_set(LOG_EXP)
            end_phase(act, PH_PREP1)
            la_tiles(act, la_act, False)
            end_phase(act, PH_ATT1)
            with act.Fori(0, NG) as g:
                act.wait_ge(n_xc, LN_WO1 + g + 2)
                square_act(act, xc[:, :], ST_WO1 + g)
                rsqrt_act(act, ST_WO1 + g)
            end_phase(act, PH_WO1)
            end_phase(act, PH_ZERO)
            with act.Fori(0, DEPTH) as l:
                act.preload_act_table_set(LOG_EXP)
                tiles(act, l, att_act)
                end_phase(act, PH_LAYERS + 2 * l)
                act.wait_ge(s_wf, 16 * loads_f * (l + 1))
                groups(act, l, ff_first_act, ff_body_act)
                end_phase(act, PH_LAYERS + 2 * l + 1)

        @block.gpsimd
        def _(pool):
            pool.memset(vaug[:, :, :], 0.0).then_inc(s_const, 1)
            pool.wait_ge(s_const, 1)
            pool.memset(vaug[:, :, HD:HD + 1], 1.0).then_inc(s_const, 1)
            end_phase(pool, PH_MOD)
            end_phase(pool, PH_PREP0)
            la_tiles(pool, la_pool, True)
            end_phase(pool, PH_ATT0)
            pool.memset(combT[:, :], 0.0)
            end_phase(pool, PH_MLP)
            end_phase(pool, PH_MOE)
            pool.memset(vaug[:, :, :], 0.0).then_inc(s_const, 1)
            pool.wait_ge(s_const, 4)
            pool.memset(vaug[:, :, HD:HD + 1], 1.0)
            end_phase(pool, PH_PREP1)
            pool.memset(XSA[:, :], 0.0)
            la_tiles(pool, la_pool, False)
            end_phase(pool, PH_ATT1)
            pool.memset(XSF[:, :], 0.0).then_inc(s_const, 1)
            pool.wait_ge(s_const, 6)
            with pool.Fori(0, NG) as g:
                off = xs_off(pool, g)
                wait_apart(pool, n_out, LN_WO1 + g + 2)
                shift_copies(pool, XSA, off, group(H, g), f_xs, g)
            end_phase(pool, PH_WO1)
            pool.memset(kbd[:, :, :, :], 0.0)
            pool.memset(Vbd[:, :, :, :], 0.0)
            end_phase(pool, PH_ZERO)
            with pool.Fori(0, DEPTH) as l:
                tiles(pool, l, att_pool)
                end_phase(pool, PH_LAYERS + 2 * l)
                with pool.Fori(0, NG) as g:
                    ff_pool(pool, g, l * NG + g)
                end_phase(pool, PH_LAYERS + 2 * l + 1)

        @block.vector
        def _(dve):
            dve.wait_ge(s_first, 16 * len(first_loads))
            dve.wait_ge(s_modps, 1)
            for k in range(2):
                ps = PS[:, 0, 6 * B * k:6 * B * (k + 1)].rearrange("p (j b) -> p j b", b=B)
                for j in range(6):
                    if j in (SCALE_A, SCALE_B):
                        dve.tensor_scalar(mod[:, k, j, :], ps[:, j, :], 1.0, None, ALU.add)
                    elif j in (SHIFT_A, SHIFT_B):
                        dve.tensor_copy(mod[:, k, j, :], ps[:, j, :])
                    else:
                        q = 2 * k + (j == GATE_B)
                        dve.tensor_copy(gtmp[:, q, :], ps[:, j, :])
                        dve.tensor_scalar(gsign[:, q, :], ps[:, j, :], 0.0, 2.0, ALU.is_ge, ALU.mult).then_inc(s_mod, 1)
            dve.wait_ge(s_mod, 4)
            dve.scalar_tensor_tensor(gabs[:, :, :], gtmp[:, :, :], -1.0, gtmp[:, :, :], ALU.mult, ALU.max).then_inc(s_mod, 1)
            dve.wait_ge(s_mod, 5)
            dve.tensor_scalar(gtmp[:, :, :], gabs[:, :, :], 0.25, None, ALU.max).then_inc(s_mod, 1)
            dve.wait_ge(s_mod, 6)
            for k in range(2):
                for j in (GATE_A, GATE_B):
                    q = 2 * k + (j == GATE_B)
                    dve.scalar_tensor_tensor(mod[:, k, j, :], gsign[:, q, :], -1.0, gtmp[:, q, :], ALU.add, ALU.mult)
            end_phase(dve, PH_MOD)
            dve.wait_ge(s_load, 16 * len(loads))
            with dve.Fori(0, NG) as g:
                u, su = LN_PREP0 + g, ST_PREP0 + 2 * g
                centre_dve(dve, group(X, g), u, su, 0)
                eps_dve(dve, su, 1, 1e-5)
                affine_dve(dve, group(H, g), u, su, modcol(0, SCALE_A, g), modcol(0, SHIFT_A, g))
                eps_dve(dve, su + 1, 1, 1e-6)
                dve.wait_ge(n_r, su + 3)
                dve.scalar_tensor_tensor(group(XSF, g), group(H, g), cols0[:, 1:2], rs[:, :], ALU.mult, ALU.mult).then_inc(n_used, 1)
            end_phase(dve, PH_PREP0)
            dve.memset(state[:, :, :, :], 0.0).then_inc(s_const, 1)
            dve.wait_ge(s_const, 3)
            la_tiles(dve, la_dve, True)
            end_phase(dve, PH_ATT0)
            skewed(dve, mlp_dve)
            end_phase(dve, PH_MLP)
            skewed(dve, moe_dve)
            end_phase(dve, PH_MOE)
            with dve.Fori(0, NG) as g:
                u, su = LN_PREP1 + g, ST_PREP1 + g
                centre_dve(dve, group(X, g), u, su, 0)
                eps_dve(dve, su, 1, 1e-5)
                affine_dve(dve, group(XSF, g), u, su, modcol(1, SCALE_A, g), modcol(1, SHIFT_A, g))
            end_phase(dve, PH_PREP1)
            dve.memset(state[:, :, :, :], 0.0).then_inc(s_const, 1)
            dve.wait_ge(s_const, 5)
            la_tiles(dve, la_dve, False)
            end_phase(dve, PH_ATT1)
            with dve.Fori(0, NG) as g:
                u, su = LN_WO1 + g, ST_WO1 + g
                dve.wait_ge(f_wo, g + 2)
                dve.scalar_tensor_tensor(group(X, g), PS[:, 2, :], modcol(1, GATE_A, g), group(X, g),
                                         ALU.mult, ALU.add).then_inc(f_x, 1)
                dve.wait_ge(f_x, g + 2)
                centre_dve(dve, group(X, g), u, su, 0)
                eps_dve(dve, su, 1, 1e-5)
                affine_dve(dve, group(H, g), u, su, modcol(1, SCALE_B, g), modcol(1, SHIFT_B, g))
            end_phase(dve, PH_WO1)
            end_phase(dve, PH_ZERO)
            dve.wait_ge(s_load2, 16 * len(late_loads))
            dve.tensor_copy(identh[:, :], ident[:, :])
            dve.tensor_copy(wmask[:, :, :], wmask32[:, :, 0:GW]).then_inc(s_cast, 1)
            dve.wait_ge(s_cast, 1)
            with dve.Fori(0, DEPTH) as l:
                rope_dve(dve, l)
                tiles(dve, l, att_dve)
                end_phase(dve, PH_LAYERS + 2 * l)
                dve.wait_ge(s_wf, 16 * loads_f * (l + 1))
                groups(dve, l, ff_first_dve, ff_body_dve)
                end_phase(dve, PH_LAYERS + 2 * l + 1)
            with dve.Fori(0, NG) as g:
                dve.scalar_tensor_tensor(group(X, g), group(H, g), modcol(1, GATE_B, g), group(X, g),
                                         ALU.mult, ALU.add).then_inc(f_x, 1)


def constants():
    import numpy as np
    f = np.float32
    k = {"ident": np.eye(P, dtype=f)}
    k["onesm"] = np.full((P, P), 1.0 / P, f)
    rows = np.arange(P)
    k["hmask"] = (rows[:, None] // HD == np.arange(HEADS)[None]).astype(f)
    k["hold"] = np.broadcast_to((np.arange(TPB) < TPB - 1)[None], (P, TPB)).astype(f)
    k["hm9"] = np.broadcast_to(np.tile(k["hmask"], (1, 2))[:, :, None], (P, 2 * HEADS, HD + 1)).astype(f)
    causal = (rows[None, :] >= rows[:, None])
    diff = (rows[None, :] - rows[:, None]) * (np.pi / 2 / L)
    k["cmask"] = np.stack([np.where(causal, np.cos(diff), 0.0), causal], 1).astype(f)
    angle = np.arange(L) * (np.pi / 2 / L)
    cs = np.stack([np.cos(angle), np.sin(angle)])
    k["crow"] = cs.astype(f)
    k["ccol"] = np.ascontiguousarray(cs.reshape(2, TPB, P).transpose(2, 0, 1)).astype(f)
    k["esel"] = np.zeros((P, EXPERTS, P), f)
    for e in range(EXPERTS):
        k["esel"][e, e, :] = 1
    e = np.arange(EXPERTS)
    k["low"] = np.broadcast_to((e[None, :] < e[:, None])[None], (P, EXPERTS, EXPERTS)).astype(f)
    half = np.arange(0, DH, 2)
    freq = np.arange(L)[:, None] / 10000.0 ** (half / DH)[None]
    freq = np.concatenate([freq, freq], 1)
    base = (half + 0.4 * DH) / (1.4 * DH)
    scale = base[None] ** ((np.arange(L) - L // 2) / (WIN // 2))[:, None]
    scale = np.concatenate([scale, scale], 1)
    sign = np.where(np.arange(DH) < DH // 2, -1.0, 1.0)[None]
    scale_q = scale * QK_SCALE
    t = np.stack([np.concatenate([np.cos(freq) * scale_q, np.cos(freq) / scale], 1),
                  np.concatenate([np.sin(freq) * scale_q * sign, np.sin(freq) / scale * sign], 1)])
    k["rope"] = np.ascontiguousarray(t.reshape(2, TPB, P, 2 * DH).transpose(2, 0, 1, 3)).astype(f)
    q, j = rows[:, None] % WIN, np.arange(KEYS)[None]
    seen = (j >= q) & (j <= q + WIN)
    first = seen & ~((rows[:, None] < WIN) & (j < WIN))
    m = np.stack([first, seen], 1)
    k["wmask"] = np.where(np.tile(m, (1, 1, GW // KEYS)), 0.0, NEG).astype(f)
    return k


def kernel(**inputs):
    import numpy as np
    import concourse.bacc as bacc
    from concourse import mybir as mb
    from concourse.bass_utils import run_bass_kernel_spmd as run

    x = {k: np.asarray(v) for k, v in inputs.items()}

    def lay(v):
        return np.ascontiguousarray(v)

    def col(*vs):
        return lay(np.stack(vs, -1))

    L0, F0, A1, F1 = "L0_attn_", "L0_ffn_", "L1_attn_", "L1_ffn_"
    arr = {
        "xT": lay(x[L0 + "x"].reshape(N, C).T),
        "cT": lay(np.stack([x["L0_c"].T, x["L1_c"].T], 1)),
        "wmod": lay(np.stack([x["L0_wmod"], x["L1_wmod"]], 1)),
        "qkv_w": x[L0 + "qkv_w"],
        "bqk0": col(x[L0 + "qkv_b"][0:C], x[L0 + "qkv_b"][C:2 * C]),
        "bkv0": lay(x[L0 + "qkv_b"][C:3 * C].reshape(1, 2 * C)),
        "out_w": x[L0 + "out_w"],
        "cols0": col(x[L0 + "out_b"], x[L0 + "norm1_w"], x[L0 + "norm2_w"], x[L0 + "mlp_b2"],
                     *x[L0 + "mlp_b1"].reshape(F_MLP, P)),
        "mlp_w1": x[L0 + "mlp_w1"],
        "mlp_w2": lay(x[L0 + "mlp_w2"].reshape(F_MLP, P, C).transpose(1, 0, 2)),
        "router_wT": lay(x[F0 + "router_w"].T),
        "router_bias": lay(x[F0 + "router_bias"].reshape(1, EXPERTS)),
        "sw1": x[F0 + "sw1"], "sw3": x[F0 + "sw3"],
        "sw2": lay(x[F0 + "sw2"].reshape(SHARED, P, C).transpose(1, 0, 2)),
        "ew1": lay(x[F0 + "ew1"].transpose(1, 0, 2)),
        "ew2": lay(x[F0 + "ew2"].transpose(1, 0, 2)),
        "wl1": lay(np.stack([x[A1 + w].T for w in ("Wq", "Wk", "Wv", "Wo", "Wg")], 1)),
        "bg1": lay(x[A1 + "bg"].reshape(C, 1)),
        "Wqkv": x[F1 + "Wqkv"],
        "Wo": lay(x[F1 + "Wo"].reshape(DEPTH, PAIRS, P, C).transpose(0, 2, 1, 3)),
        "qks": lay(np.stack([x[F1 + "q_scale"], x[F1 + "k_scale"]], 1)),
        "W1": x[F1 + "W1"],
        "lncol": col(x[F1 + "ln_g"], x[F1 + "ln_b"]),
        "b2col": lay(x[F1 + "b2"].reshape(DEPTH, C, 1)),
    }
    w2 = np.zeros((DEPTH, 3, P, C), np.float32)
    b1 = np.zeros((DEPTH, P, 6), np.float32)
    for c, (c0, m) in enumerate(CH):
        w2[:, c, 0:m] = x[F1 + "W2"][:, c0:c0 + m]
        b1[:, 0:m, c] = x[F1 + "b1"][:, c0:c0 + m]
        b1[:, 0:m, 3 + c] = x[F1 + "b1"][:, DIN + c0:DIN + c0 + m]
    arr["W2"] = lay(w2.transpose(0, 2, 1, 3))
    arr["b1col"] = b1
    arr.update(constants())

    nc = bacc.Bacc("TRN2", target_bir_lowering=False, num_devices=1)
    aps = {k: nc.dram_tensor(f"in_{k}", v.shape, mb.dt.from_np(v.dtype), kind="ExternalInput").ap() for k, v in arr.items()}
    out = nc.dram_tensor("out_xT", (C, N), F32, kind="ExternalOutput").ap()
    build(nc, aps, out)
    r = run(nc, [{f"in_{k}": v for k, v in arr.items()}], core_ids=[0])
    return np.ascontiguousarray(r.results[0]["out_xT"].T).reshape(B, L, C)
```
